# Optimizing a Trainium2 kernel written in Bass

```python
import numpy as np
import jax
import jax.numpy as jnp

def _softmax(x, axis=-1):
    return jax.nn.softmax(x, axis=axis)

def _gelu(x):
    return jax.nn.gelu(x, approximate=True)

def _silu(x):
    return jax.nn.silu(x)

def _sigmoid(x):
    return jax.nn.sigmoid(x)

def _layernorm(x, axis=-1, eps=1e-05):
    m = jnp.mean(x, axis=axis, keepdims=True)
    v = jnp.var(x, axis=axis, keepdims=True)
    return (x - m) / jnp.sqrt(v + eps)

def _scatter_add(tgt, idx, src, axis=0):
    return tgt.at[idx].add(src)

def _segment_sum(src, seg, n):
    return jax.ops.segment_sum(src, seg, n)
kernel_name = 'mk_perceiver_d1_seqx_r2_e72c59'

def setup_inputs(seed: int=0):
    np.random.seed(seed)
    _w = jnp.asarray

    def _rec_inputs():
        import jax
        import jax.numpy as jnp
        _rk = jax.random.key(seed)
        x = -0.0002928 + 1 * jax.random.normal(jax.random.fold_in(_rk, 1), (8, 64, 512), jnp.float32)
        _lenS = 64 - jax.random.randint(jax.random.fold_in(_rk, 7), (8,), 0, max(1, 64 // 4) + 1, jnp.int32)
        _lenS2 = 1601 - jax.random.randint(jax.random.fold_in(_rk, 8), (8,), 0, max(1, 1601 // 4) + 1, jnp.int32)
        _ctx_1024P = jax.random.normal(jax.random.fold_in(_rk, 11), (8, 16, 512), jnp.float32)
        _ctx_1024c = jax.random.dirichlet(jax.random.fold_in(_rk, 511), 0.3 * jnp.ones((16,), jnp.float32), (8, 1601))
        _ctx_1024t = jnp.einsum('bsk,bkd->bsd', _ctx_1024c, _ctx_1024P)
        _ctx_1024t = _ctx_1024t * jax.lax.rsqrt(jnp.mean(jnp.square(_ctx_1024t)) + 1e-12) * 0.953939
        ctx_1024 = -1.39393e-06 + 0.999914 * (_ctx_1024t + 0.3 * jax.random.normal(jax.random.fold_in(_rk, 611), (8, 1601, 512), jnp.float32))
        return (x, ctx_1024)
    x, ctx_1024 = _rec_inputs()

    def _L0_xattn_setup():
        import jax, jax.numpy as jnp
        import numpy as np
        D_MODEL = 512
        N_HEADS = 16
        HEAD = D_MODEL // N_HEADS
        D_FF = 2048
        LN_EPS = 1e-05

        def _layernorm(x, g, b):
            mu = jnp.mean(x, axis=-1, keepdims=True)
            var = jnp.mean(jnp.square(x - mu), axis=-1, keepdims=True)
            return (x - mu) * jax.lax.rsqrt(var + LN_EPS) * g + b

        def _mha(q_in, k_in, v_in, Wq, Wk, Wv, bv, causal):
            q = jnp.einsum('bsd,hde->bhse', q_in, Wq)
            k = jnp.einsum('btd,hde->bhte', k_in, Wk)
            v = jnp.einsum('btd,hde->bhte', v_in, Wv) + bv[None, :, None, :]
            scale = HEAD ** (-0.5)
            scores = jnp.einsum('bhse,bhte->bhst', q, k) * scale
            if causal:
                S, T = (scores.shape[-2], scores.shape[-1])
                mask = jnp.tril(jnp.ones((S, T), dtype=bool))
                scores = jnp.where(mask, scores, -jnp.inf)
            p = jax.nn.softmax(scores, axis=-1)
            o = jnp.einsum('bhst,bhte->bhse', p, v)
            B, H, S, E = o.shape
            return o.transpose(0, 2, 1, 3).reshape(B, S, H * E)
        key = jax.random.key(seed)
        ks = jax.random.split(key, 20)
        B, S, T = (2, 1024, 1024)
        sd = D_MODEL ** (-0.5)
        inp = {'input_tensor': jax.random.normal(ks[0], (B, S, D_MODEL), jnp.float32), 'encoder_output': jax.random.normal(ks[1], (B, T, D_MODEL), jnp.float32), 'Wq1': jax.random.normal(ks[2], (N_HEADS, D_MODEL, HEAD), jnp.float32) * sd, 'Wk1': jax.random.normal(ks[3], (N_HEADS, D_MODEL, HEAD), jnp.float32) * sd, 'Wv1': jax.random.normal(ks[4], (N_HEADS, D_MODEL, HEAD), jnp.float32) * sd, 'bv1': jnp.zeros((N_HEADS, HEAD), jnp.float32), 'Wq2': jax.random.normal(ks[5], (N_HEADS, D_MODEL, HEAD), jnp.float32) * sd, 'Wk2': jax.random.normal(ks[6], (N_HEADS, D_MODEL, HEAD), jnp.float32) * sd, 'Wv2': jax.random.normal(ks[7], (N_HEADS, D_MODEL, HEAD), jnp.float32) * sd, 'bv2': jnp.zeros((N_HEADS, HEAD), jnp.float32), 'g1': jnp.ones((D_MODEL,), jnp.float32), 'be1': jnp.zeros((D_MODEL,), jnp.float32), 'g2': jnp.ones((D_MODEL,), jnp.float32), 'be2': jnp.zeros((D_MODEL,), jnp.float32), 'g3': jnp.ones((D_MODEL,), jnp.float32), 'be3': jnp.zeros((D_MODEL,), jnp.float32), 'Wf1': jax.random.normal(ks[8], (D_MODEL, D_FF), jnp.float32) * sd, 'bf1': jnp.zeros((D_FF,), jnp.float32), 'Wf2': jax.random.normal(ks[9], (D_FF, D_MODEL), jnp.float32) * D_FF ** (-0.5), 'bf2': jnp.zeros((D_MODEL,), jnp.float32)}
        return inp
    _L0_xattn_all = _L0_xattn_setup()
    _L0_xattn_in = {k: v for k, v in _L0_xattn_all.items() if k in ('Wq1', 'Wk1', 'Wv1', 'bv1', 'Wq2', 'Wk2', 'Wv2', 'bv2', 'g1', 'be1', 'g2', 'be2', 'g3', 'be3', 'Wf1', 'bf1', 'Wf2', 'bf2')}
    del _L0_xattn_all

    def _L0_attn_setup():
        import jax, jax.numpy as jnp
        import numpy as np
        CHUNK = 32
        HEADS = 4
        EPS_RMS = 1e-05

        def silu(x):
            return jax.nn.silu(x)

        def l2norm(x, eps=1e-06):
            return x * jax.lax.rsqrt(jnp.sum(x * x, axis=-1, keepdims=True) + eps)

        def short_conv(x, w):
            K = w.shape[1]
            L = x.shape[1]
            xp = jnp.pad(x, ((0, 0), (K - 1, 0), (0, 0)))
            out = xp[:, 0:L, :] * w[:, 0]
            for k in range(1, K):
                out = out + xp[:, k:k + L, :] * w[:, k]
            return out

        def delta_rule_chunkwise(q, k, v, beta, chunk=CHUNK):
            b, h, l, dk = q.shape
            dv = v.shape[-1]
            n = l // chunk
            q = l2norm(q)
            k = l2norm(k)
            v = v * beta[..., None]
            k_beta = k * beta[..., None]
            resh = lambda x: x.reshape(b, h, n, chunk, -1)
            q, k, v, k_beta = map(resh, (q, k, v, k_beta))
            strict_lower = jnp.tril(jnp.ones((chunk, chunk), bool), -1)
            attn = jnp.where(strict_lower, -(k_beta @ jnp.swapaxes(k, -1, -2)), 0.0)
            for i in range(1, chunk):
                row = attn[..., i, :]
                new = attn[..., i, :i] + jnp.einsum('...j,...jk->...k', row, attn[..., :, :i])
                attn = attn.at[..., i, :i].set(new)
            attn = attn + jnp.eye(chunk, dtype=attn.dtype)
            u = attn @ v
            w = attn @ k_beta
            lower_incl = jnp.tril(jnp.ones((chunk, chunk), bool))
            qc, kc, uc, wc = [jnp.moveaxis(x, 2, 0) for x in (q, k, u, w)]
            S0 = jnp.zeros((b, h, dk, dv), q.dtype)

            def step(S, inp):
                q_i, k_i, u_i, w_i = inp
                attn_i = jnp.where(lower_incl, q_i @ jnp.swapaxes(k_i, -1, -2), 0.0)
                u_adj = u_i - w_i @ S
                o_i = q_i @ S + attn_i @ u_adj
                S = S + jnp.swapaxes(k_i, -1, -2) @ u_adj
                return (S, o_i)
            S, o = jax.lax.scan(step, S0, (qc, kc, uc, wc))
            o = jnp.moveaxis(o, 0, 2).reshape(b, h, l, dv)
            return (o, S)

        def ema_rule(v, gamma):
            v_t = jnp.moveaxis(v, 2, 0)
            g_t = jnp.moveaxis(gamma, 2, 0)
            s0 = jnp.zeros(v.shape[:2] + (v.shape[-1],), v.dtype)

            def step(s, inp):
                vt, gt = inp
                s = gt[..., None] * s + (1.0 - gt[..., None]) * vt
                return (s, s)
            s_fin, out = jax.lax.scan(step, s0, (v_t, g_t))
            return (jnp.moveaxis(out, 0, 2), s_fin)

        def rms_norm(x, w, eps=EPS_RMS):
            return x * jax.lax.rsqrt(jnp.mean(x * x, axis=-1, keepdims=True) + eps) * w
        key = jax.random.key(seed)
        ks = jax.random.split(key, 16)
        b, l, d = (4, 1024, 512)
        H, conv_K = (HEADS, 4)
        s = 0.02
        return {'hidden_states': jax.random.normal(ks[0], (b, l, d), jnp.float32), 'Wq': jax.random.normal(ks[1], (d, d), jnp.float32) * s, 'Wk': jax.random.normal(ks[2], (d, d), jnp.float32) * s, 'Wv': jax.random.normal(ks[3], (d, d), jnp.float32) * s, 'conv_q': jax.random.normal(ks[4], (d, conv_K), jnp.float32) * 0.3, 'conv_k': jax.random.normal(ks[5], (d, conv_K), jnp.float32) * 0.3, 'conv_v': jax.random.normal(ks[6], (d, conv_K), jnp.float32) * 0.3, 'Wb': jax.random.normal(ks[7], (d, H), jnp.float32) * s, 'Wdec': jax.random.normal(ks[8], (d, H), jnp.float32) * s, 'Wmix': jax.random.normal(ks[9], (d, H), jnp.float32) * s, 'conv_mix': jax.random.normal(ks[10], (H, conv_K), jnp.float32) * 0.3, 'mix_bias': jnp.full((H,), -2.0, jnp.float32), 'rms_w': jnp.ones((d // H,), jnp.float32), 'Wo': jax.random.normal(ks[11], (d, d), jnp.float32) * s}
    _L0_attn_all = _L0_attn_setup()
    _L0_attn_in = {k: v for k, v in _L0_attn_all.items() if k in ('Wq', 'Wk', 'Wv', 'conv_q', 'conv_k', 'conv_v', 'Wb', 'Wdec', 'Wmix', 'conv_mix', 'mix_bias', 'rms_w', 'Wo')}
    del _L0_attn_all

    def _L0_ffn_setup():
        import jax, jax.numpy as jnp
        import numpy as np
        D = 512
        H = 2048
        E = 8
        TOPK = 2
        CAP_F = 1.25
        key = jax.random.key(seed)
        ks = jax.random.split(key, 6)
        sc = 0.02
        return {'x': jax.random.normal(ks[0], (4, 1024, D), jnp.float32), 'Wg': jax.random.normal(ks[1], (D, E), jnp.float32) * sc, 'bg': jnp.zeros((E,), jnp.float32), 'W1': jax.random.normal(ks[2], (E, D, H), jnp.float32) * sc, 'W2': jax.random.normal(ks[3], (E, D, H), jnp.float32) * sc, 'W3': jax.random.normal(ks[4], (E, H, D), jnp.float32) * sc}
    _L0_ffn_all = _L0_ffn_setup()
    _L0_ffn_in = {k: v for k, v in _L0_ffn_all.items() if k in ('Wg', 'bg', 'W1', 'W2', 'W3')}
    del _L0_ffn_all
    return {'x': x, 'ctx_1024': ctx_1024, 'L0_xattn_Wq1': _L0_xattn_in['Wq1'], 'L0_xattn_Wk1': _L0_xattn_in['Wk1'], 'L0_xattn_Wv1': _L0_xattn_in['Wv1'], 'L0_xattn_bv1': _L0_xattn_in['bv1'], 'L0_xattn_Wq2': _L0_xattn_in['Wq2'], 'L0_xattn_Wk2': _L0_xattn_in['Wk2'], 'L0_xattn_Wv2': _L0_xattn_in['Wv2'], 'L0_xattn_bv2': _L0_xattn_in['bv2'], 'L0_xattn_g1': _L0_xattn_in['g1'], 'L0_xattn_be1': _L0_xattn_in['be1'], 'L0_xattn_g2': _L0_xattn_in['g2'], 'L0_xattn_be2': _L0_xattn_in['be2'], 'L0_xattn_g3': _L0_xattn_in['g3'], 'L0_xattn_be3': _L0_xattn_in['be3'], 'L0_xattn_Wf1': _L0_xattn_in['Wf1'], 'L0_xattn_bf1': _L0_xattn_in['bf1'], 'L0_xattn_Wf2': _L0_xattn_in['Wf2'], 'L0_xattn_bf2': _L0_xattn_in['bf2'], 'L0_attn_Wq': _L0_attn_in['Wq'], 'L0_attn_Wk': _L0_attn_in['Wk'], 'L0_attn_Wv': _L0_attn_in['Wv'], 'L0_attn_conv_q': _L0_attn_in['conv_q'], 'L0_attn_conv_k': _L0_attn_in['conv_k'], 'L0_attn_conv_v': _L0_attn_in['conv_v'], 'L0_attn_Wb': _L0_attn_in['Wb'], 'L0_attn_Wdec': _L0_attn_in['Wdec'], 'L0_attn_Wmix': _L0_attn_in['Wmix'], 'L0_attn_conv_mix': _L0_attn_in['conv_mix'], 'L0_attn_mix_bias': _L0_attn_in['mix_bias'], 'L0_attn_rms_w': _L0_attn_in['rms_w'], 'L0_attn_Wo': _L0_attn_in['Wo'], 'L0_ffn_Wg': _L0_ffn_in['Wg'], 'L0_ffn_bg': _L0_ffn_in['bg'], 'L0_ffn_W1': _L0_ffn_in['W1'], 'L0_ffn_W2': _L0_ffn_in['W2'], 'L0_ffn_W3': _L0_ffn_in['W3']}

def reference(x, ctx_1024, L0_xattn_Wq1, L0_xattn_Wk1, L0_xattn_Wv1, L0_xattn_bv1, L0_xattn_Wq2, L0_xattn_Wk2, L0_xattn_Wv2, L0_xattn_bv2, L0_xattn_g1, L0_xattn_be1, L0_xattn_g2, L0_xattn_be2, L0_xattn_g3, L0_xattn_be3, L0_xattn_Wf1, L0_xattn_bf1, L0_xattn_Wf2, L0_xattn_bf2, L0_attn_Wq, L0_attn_Wk, L0_attn_Wv, L0_attn_conv_q, L0_attn_conv_k, L0_attn_conv_v, L0_attn_Wb, L0_attn_Wdec, L0_attn_Wmix, L0_attn_conv_mix, L0_attn_mix_bias, L0_attn_rms_w, L0_attn_Wo, L0_ffn_Wg, L0_ffn_bg, L0_ffn_W1, L0_ffn_W2, L0_ffn_W3):
    import jax
    import jax.numpy as jnp

    def _L0_xattn_ref(input_tensor, encoder_output, Wq1, Wk1, Wv1, bv1, Wq2, Wk2, Wv2, bv2, g1, be1, g2, be2, g3, be3, Wf1, bf1, Wf2, bf2):
        import jax, jax.numpy as jnp
        import numpy as np
        D_MODEL = 512
        N_HEADS = 16
        HEAD = D_MODEL // N_HEADS
        D_FF = 2048
        LN_EPS = 1e-05

        def _layernorm(x, g, b):
            mu = jnp.mean(x, axis=-1, keepdims=True)
            var = jnp.mean(jnp.square(x - mu), axis=-1, keepdims=True)
            return (x - mu) * jax.lax.rsqrt(var + LN_EPS) * g + b

        def _mha(q_in, k_in, v_in, Wq, Wk, Wv, bv, causal):
            q = jnp.einsum('bsd,hde->bhse', q_in, Wq)
            k = jnp.einsum('btd,hde->bhte', k_in, Wk)
            v = jnp.einsum('btd,hde->bhte', v_in, Wv) + bv[None, :, None, :]
            scale = HEAD ** (-0.5)
            scores = jnp.einsum('bhse,bhte->bhst', q, k) * scale
            if causal:
                S, T = (scores.shape[-2], scores.shape[-1])
                mask = jnp.tril(jnp.ones((S, T), dtype=bool))
                scores = jnp.where(mask, scores, -jnp.inf)
            p = jax.nn.softmax(scores, axis=-1)
            o = jnp.einsum('bhst,bhte->bhse', p, v)
            B, H, S, E = o.shape
            return o.transpose(0, 2, 1, 3).reshape(B, S, H * E)
        x = input_tensor
        sa = _mha(x, x, x, Wq1, Wk1, Wv1, bv1, causal=True)
        x = _layernorm(sa + input_tensor, g1, be1)
        ca = _mha(x, encoder_output, encoder_output, Wq2, Wk2, Wv2, bv2, causal=False)
        x = _layernorm(x + ca, g2, be2)
        ffn = jax.nn.relu(x @ Wf1 + bf1) @ Wf2 + bf2
        x = _layernorm(x + ffn, g3, be3)
        return x

    def _L0_attn_ref(hidden_states, Wq, Wk, Wv, conv_q, conv_k, conv_v, Wb, Wdec, Wmix, conv_mix, mix_bias, rms_w, Wo):
        import jax, jax.numpy as jnp
        import numpy as np
        CHUNK = 32
        HEADS = 4
        EPS_RMS = 1e-05

        def silu(x):
            return jax.nn.silu(x)

        def l2norm(x, eps=1e-06):
            return x * jax.lax.rsqrt(jnp.sum(x * x, axis=-1, keepdims=True) + eps)

        def short_conv(x, w):
            K = w.shape[1]
            L = x.shape[1]
            xp = jnp.pad(x, ((0, 0), (K - 1, 0), (0, 0)))
            out = xp[:, 0:L, :] * w[:, 0]
            for k in range(1, K):
                out = out + xp[:, k:k + L, :] * w[:, k]
            return out

        def delta_rule_chunkwise(q, k, v, beta, chunk=CHUNK):
            b, h, l, dk = q.shape
            dv = v.shape[-1]
            n = l // chunk
            q = l2norm(q)
            k = l2norm(k)
            v = v * beta[..., None]
            k_beta = k * beta[..., None]
            resh = lambda x: x.reshape(b, h, n, chunk, -1)
            q, k, v, k_beta = map(resh, (q, k, v, k_beta))
            strict_lower = jnp.tril(jnp.ones((chunk, chunk), bool), -1)
            attn = jnp.where(strict_lower, -(k_beta @ jnp.swapaxes(k, -1, -2)), 0.0)
            for i in range(1, chunk):
                row = attn[..., i, :]
                new = attn[..., i, :i] + jnp.einsum('...j,...jk->...k', row, attn[..., :, :i])
                attn = attn.at[..., i, :i].set(new)
            attn = attn + jnp.eye(chunk, dtype=attn.dtype)
            u = attn @ v
            w = attn @ k_beta
            lower_incl = jnp.tril(jnp.ones((chunk, chunk), bool))
            qc, kc, uc, wc = [jnp.moveaxis(x, 2, 0) for x in (q, k, u, w)]
            S0 = jnp.zeros((b, h, dk, dv), q.dtype)

            def step(S, inp):
                q_i, k_i, u_i, w_i = inp
                attn_i = jnp.where(lower_incl, q_i @ jnp.swapaxes(k_i, -1, -2), 0.0)
                u_adj = u_i - w_i @ S
                o_i = q_i @ S + attn_i @ u_adj
                S = S + jnp.swapaxes(k_i, -1, -2) @ u_adj
                return (S, o_i)
            S, o = jax.lax.scan(step, S0, (qc, kc, uc, wc))
            o = jnp.moveaxis(o, 0, 2).reshape(b, h, l, dv)
            return (o, S)

        def ema_rule(v, gamma):
            v_t = jnp.moveaxis(v, 2, 0)
            g_t = jnp.moveaxis(gamma, 2, 0)
            s0 = jnp.zeros(v.shape[:2] + (v.shape[-1],), v.dtype)

            def step(s, inp):
                vt, gt = inp
                s = gt[..., None] * s + (1.0 - gt[..., None]) * vt
                return (s, s)
            s_fin, out = jax.lax.scan(step, s0, (v_t, g_t))
            return (jnp.moveaxis(out, 0, 2), s_fin)

        def rms_norm(x, w, eps=EPS_RMS):
            return x * jax.lax.rsqrt(jnp.mean(x * x, axis=-1, keepdims=True) + eps) * w
        b, l, d = hidden_states.shape
        H = HEADS
        dk = d // H
        dv = d // H
        q = silu(short_conv(hidden_states @ Wq, conv_q))
        k = silu(short_conv(hidden_states @ Wk, conv_k))
        v = silu(short_conv(hidden_states @ Wv, conv_v))
        mix_inp = silu(short_conv(hidden_states @ Wmix, conv_mix))
        q = silu(q)
        k = silu(k)
        to_heads = lambda x, dh: jnp.transpose(x.reshape(b, l, H, dh), (0, 2, 1, 3))
        q_d = to_heads(q, dk)
        k_d = to_heads(k, dk)
        v_d = to_heads(v, dv)
        beta = jax.nn.sigmoid(hidden_states @ Wb)
        beta_d = jnp.transpose(beta, (0, 2, 1))
        o_d, S = delta_rule_chunkwise(q_d, k_d, v_d, beta_d)
        o_d = jnp.transpose(o_d, (0, 2, 1, 3))
        gamma = jax.nn.sigmoid(hidden_states @ Wdec)
        gamma_d = jnp.transpose(gamma, (0, 2, 1))
        ema_out, ema_state = ema_rule(v_d, gamma_d)
        ema_out = jnp.transpose(ema_out, (0, 2, 1, 3))
        mix = jax.nn.sigmoid(mix_inp + mix_bias)
        o = (1.0 - mix[..., None]) * o_d + mix[..., None] * ema_out
        o = rms_norm(o, rms_w)
        out = o.reshape(b, l, H * dv) @ Wo
        return out

    def _L0_ffn_ref(x, Wg, bg, W1, W2, W3):
        import jax, jax.numpy as jnp
        import numpy as np
        D = 512
        H = 2048
        E = 8
        TOPK = 2
        CAP_F = 1.25
        b, s, d = x.shape
        xt = x.reshape(-1, d)
        T = xt.shape[0]
        capacity = int(T / E * CAP_F)
        gate_logits = xt @ Wg + bg
        top_v, top_i = jax.lax.top_k(gate_logits, TOPK)
        expert_label = jax.nn.one_hot(top_i, E, dtype=xt.dtype).sum(axis=1)
        seq = jnp.cumsum(expert_label, axis=0) * expert_label
        valid = (seq > 0) & (seq <= capacity)
        slot = (seq - 1.0).astype(jnp.int32)
        flat_idx = jnp.where(valid, jnp.arange(E, dtype=jnp.int32)[None, :] * capacity + slot, E * capacity)
        src = jnp.broadcast_to(xt[:, None, :], (T, E, d)).reshape(-1, d)
        buf = jnp.zeros((E * capacity + 1, d), xt.dtype).at[flat_idx.reshape(-1)].set(src)
        disp = buf[:-1].reshape(E, capacity, d)
        h = jax.nn.silu(jnp.einsum('ecd,edh->ech', disp, W1)) * jnp.einsum('ecd,edh->ech', disp, W2)
        out = jnp.einsum('ech,ehd->ecd', h, W3)
        out_flat = jnp.concatenate([out.reshape(E * capacity, d), jnp.zeros((1, d), xt.dtype)], axis=0)
        all_expert_output = out_flat[flat_idx]
        sel = jnp.take_along_axis(all_expert_output, top_i[:, :, None], axis=1)
        routing_w = jax.nn.softmax(top_v, axis=-1)
        y = (routing_w[:, :, None] * sel).sum(axis=1)
        return y.reshape(b, s, d)
    x = x + _L0_xattn_ref(_layernorm(x, axis=-1), ctx_1024, L0_xattn_Wq1, L0_xattn_Wk1, L0_xattn_Wv1, L0_xattn_bv1, L0_xattn_Wq2, L0_xattn_Wk2, L0_xattn_Wv2, L0_xattn_bv2, L0_xattn_g1, L0_xattn_be1, L0_xattn_g2, L0_xattn_be2, L0_xattn_g3, L0_xattn_be3, L0_xattn_Wf1, L0_xattn_bf1, L0_xattn_Wf2, L0_xattn_bf2)
    x = x + _L0_attn_ref(_layernorm(x, axis=-1), L0_attn_Wq, L0_attn_Wk, L0_attn_Wv, L0_attn_conv_q, L0_attn_conv_k, L0_attn_conv_v, L0_attn_Wb, L0_attn_Wdec, L0_attn_Wmix, L0_attn_conv_mix, L0_attn_mix_bias, L0_attn_rms_w, L0_attn_Wo)
    x = x + _L0_ffn_ref(_layernorm(x, axis=-1), L0_ffn_Wg, L0_ffn_bg, L0_ffn_W1, L0_ffn_W2, L0_ffn_W3)
    return x

_drawn_inputs = setup_inputs


def setup_inputs(seed=0):
    import zlib

    import numpy as np

    out = dict(_drawn_inputs(seed))
    spreads = {'L0_xattn_bv1': (0.0, 0.1),
     'L0_xattn_bv2': (0.0, 0.1),
     'L0_xattn_g1': (1.0, 0.2),
     'L0_xattn_be1': (0.0, 0.1),
     'L0_xattn_g2': (1.0, 0.2),
     'L0_xattn_be2': (0.0, 0.1),
     'L0_xattn_g3': (1.0, 0.2),
     'L0_xattn_be3': (0.0, 0.1),
     'L0_xattn_bf1': (0.0, 0.1),
     'L0_xattn_bf2': (0.0, 0.1),
     'L0_attn_mix_bias': (-2.0, 0.561),
     'L0_attn_rms_w': (1.0, 0.2),
     'L0_ffn_bg': (0.0, 2.0)}
    factors = {'L0_attn_Wdec': 2.703, 'L0_attn_Wmix': 5.05, 'L0_attn_conv_mix': 4.386, 'L0_ffn_Wg': 7.802}
    for name, (base, spread) in spreads.items():
        noise = np.random.default_rng([zlib.crc32(name.encode()), seed]).standard_normal(out[name].shape)
        drawn = base * np.exp(spread * noise) if base else spread * noise
        out[name] = jnp.asarray(drawn.astype(out[name].dtype))
    for name, factor in factors.items():
        out[name] = (out[name] * factor).astype(out[name].dtype)
    return out
```

```python
from contextlib import ExitStack

import numpy as np

import concourse.bass as bass
import concourse.mybir as mybir

F32 = mybir.dt.float32
F32R = mybir.dt.float32r
U32 = mybir.dt.uint32
ALU = mybir.AluOpType
ACT = mybir.ActivationFunctionType
AX = mybir.AxisListType

P = 128
B, S, D = 8, 64, 512
TOK = B * S
NT = TOK // P
NC = D // P
H, E = 16, 32
NP = H // 2
SCALE = float(E) ** -0.5
CTX = 1601
CW = CTX + 1
G = 256
NG = -(-CTX // G)
CT = -(-CTX // P)
LAST = CTX - (CT - 1) * P
EPS = 1e-5
MASKED = -3.0e38

HID = 2048
NH = HID // P
GH = 4
NEXP = 8
CAP = int(TOK / NEXP * 1.25)
TAPS = 4


def build(nc, a, out, debug=None):
    ctx = ExitStack()
    sems = {}

    def sem(name):
        if name not in sems:
            sems[name] = ctx.enter_context(nc.semaphore(name))
        return sems[name]

    base = 16512

    def at(name, offset, shape, dt=F32):
        return nc.alloc_sbuf_tensor_at(name, shape, dt, offset=base + offset)

    sc = ctx.enter_context(nc.psum_tensor("sc", [P, 4, 512], F32))
    ring = [ctx.enter_context(nc.psum_tensor(f"ring{i}", [P, 512], F32)) for i in range(3)]
    pv = ctx.enter_context(nc.psum_tensor("pv", [P, 512], F32))
    bank = [sc[:, 0, :], sc[:, 1, :], sc[:, 2, :], sc[:, 3, :], ring[0][:, :], ring[1][:, :], ring[2][:, :], pv[:, :]]

    ident = at("ident", 0, [P, P])
    ones = at("ones", 512, [P, P])
    stat = at("stat", 1024, [P, NT, 6])
    mv = at("mv", 1152, [P, NT, 2])
    rstd = at("rstd", 1216, [P, NT])
    mhalf = at("mhalf", 1248, [P, 64])
    nmax = at("nmax", 1536, [P, 2, NP])
    esum = at("esum", 1600, [P, 2, NP])
    rinv = at("rinv", 1664, [P, 2, NP])
    cat = at("cat", 2048, [P, D])
    xa = at("xa", 4096, [P, NT, D])
    R = 12288

    qT = at("qT", R, [P, NC, TOK])
    qb_h = at("qb_h", R + 8192, [P, NP, P], F32R)
    qb_l = at("qb_l", R + 12288, [P, NP, P], F32R)
    wk_h = at("wk_h", R + 16384, [P, NC, D], F32R)
    wk_l = at("wk_l", R + 24576, [P, NC, D], F32R)
    wv_h = at("wv_h", R + 32768, [P, NC, D], F32R)
    wv_l = at("wv_l", R + 40960, [P, NC, D], F32R)
    raw = at("raw", R + 49152, [P, 2, NC, G])
    x_h = at("x_h", R + 57344, [P, 2, NC, G], F32R)
    x_l = at("x_l", R + 65536, [P, 2, NC, G], F32R)
    K0 = R + 73728
    kT_h = at("kT_h", K0, [P, NC, CW], F32R)
    kT_l = at("kT_l", K0 + 25632, [P, NC, CW], F32R)
    V0 = K0 + 51264
    v_h = at("v_h", V0, [P, CT, D], F32R)
    v_l = at("v_l", V0 + 26624, [P, CT, D], F32R)
    pT_h = at("pT_h", V0 + 53248, [P, CT, P], F32R)
    pT_l = at("pT_l", V0 + 59904, [P, CT, P], F32R)
    prob = at("prob", V0 + 66560, [P, CW])
    bv2 = at("bv2", V0 + 72992, [P, D])

    xin = at("xin", K0, [P, NT, D])
    nT = at("nT", K0 + 8192, [P, NC, TOK])
    w_in = [at(f"w_in{i}", K0 + 16384 + 8192 * i, [P, NC, D]) for i in range(3)]
    kT1 = at("kT1", K0 + 40960, [P, NC, TOK])
    v1 = at("v1", K0 + 49152, [P, NT, D])
    s1 = at("s1", K0 + 57344, [P, 2, 512])
    p1 = at("p1", K0 + 61440, [P, 2, 512])
    pT1 = at("pT1", K0 + 65536, [P, 1024])
    mask = at("mask", K0 + 69632, [P, S])
    bv1 = at("bv1", K0 + 69888, [P, D])
    g1 = at("g1", K0 + 71936, [P, D])
    be1 = at("be1", K0 + 73984, [P, D])
    wq2 = at("wq2", K0 + 76032, [P, NC, D])
    wk2 = at("wk2", K0 + 84224, [P, NC, D])
    wv2 = at("wv2", K0 + 92416, [P, NC, D])
    sa = at("sa", K0 + 100608, [P, NT, D])
    qb1 = at("qb1", R + 8192, [P, B, NP, P])

    x_dram = a["x"].rearrange("b s d -> (b s) d").rearrange("(t p) d -> p t d", p=P)
    out_dram = out.rearrange("b s d -> (b s) d").rearrange("(t p) d -> p t d", p=P)

    def w_dram(name):
        return a[name].rearrange("(c p) n -> p c n", p=P)

    def row_dram(name):
        return a[name].partition_broadcast(P)

    block = ctx.enter_context(nc.Block())

    class Chain:

        def __init__(self, eng, name):
            self.eng, self.sem, self.n = eng, sem(name), 0

        def __call__(self, instruction):
            self.n += 1
            instruction.then_inc(self.sem, 1)
            self.eng.wait_ge(self.sem, self.n)

    def over_tiles(v, n=NT):
        return v.unsqueeze(1).to_broadcast([v.shape[0], n, v.shape[1]])

    def over_width(v, w):
        return v.unsqueeze(2).to_broadcast([v.shape[0], v.shape[1], w])

    def norm_stats(dve, link, src):
        for t in range(NT):
            link(dve.bn_stats(stat[:, t, :], src[:, t, :]))
        for t in range(NT):
            dve.bn_aggr(mv[:, t, :], stat[:, t, :]).then_inc(sem("variance_ready"), 1)

    def norm_rstd(pool, link, n):
        pool.wait_ge(sem("variance_ready"), NT * (n + 1))
        link(pool.tensor_scalar(rstd[:, :], mv[:, :, 1], EPS, None, ALU.add))
        pool.tensor_tensor(rstd[:, :], rstd[:, :], mhalf[:, 0:NT], ALU.pow).then_inc(sem("rstd_ready"), 1)

    def norm_apply(dve, n, dst, src, t, sem_name=None):
        if t == 0:
            dve.wait_ge(sem("rstd_ready"), n + 1)
        return dve.tensor_scalar(dst[:, t, :], src[:, t, :], mv[:, t, 0:1], rstd[:, t:t + 1], ALU.subtract, ALU.mult)

    def sp_self(sp):
        sp.dma_start(xin[:, :, :], x_dram).then_inc(sem("x_loaded"), 16)
        for i, name in enumerate(("wq1", "wk1", "wv1")):
            sp.dma_start(w_in[i][:, :, :], w_dram(name)).then_inc(sem(f"{name}_loaded"), 16)
        for dst, name in ((bv1, "bv1"), (g1, "g1"), (be1, "be1")):
            sp.dma_start(dst[:, :], row_dram(name)).then_inc(sem("self_rows_loaded"), 16)
        sp.dma_start(bv2[:, :], row_dram("bv2")).then_inc(sem("self_rows_loaded"), 16)
        for dst, name in ((wq2, "wq2"), (wk2, "wk2"), (wv2, "wv2")):
            sp.dma_start(dst[:, :, :], w_dram(name)).then_inc(sem(f"{name}_loaded"), 16)

    def pool_self(pool, link):
        link(pool.memset(ident[:, :], 0.0))
        pool.affine_select(out=ident[:, :], in_=ident[:, :], compare_op=ALU.not_equal, fill=1.0, base=0,
                           pattern=[[-1, P]], channel_multiplier=1).then_inc(sem("ident_ready"), 1)
        link(pool.memset(mhalf[:, :], -0.5))
        norm_rstd(pool, link, 0)
        link(pool.memset(mask[:, :], 0.0))
        for i, half in enumerate((slice(0, S), slice(S, P))):
            pool.affine_select(out=mask[half, :], in_=mask[half, :], compare_op=ALU.is_ge, fill=MASKED, base=0,
                               pattern=[[-1, S]], channel_multiplier=1).then_inc(sem("mask_ready"), 1)
            pool.wait_ge(sem("mask_ready"), i + 1)
        pool.memset(ones[:, :], 1.0).then_inc(sem("ones_ready"), 1)
        norm_rstd(pool, link, 1)

    def dve_self(dve, link):
        dve.memset(qb1[:, :, :, :], 0.0).then_inc(sem("qb1_zeroed"), 1)
        dve.wait_ge(sem("x_loaded"), 16)
        norm_stats(dve, link, xin)
        for t in range(NT):
            norm_apply(dve, 0, xa, xin, t).then_inc(sem("n0_ready"), 1)
        for c in (0, 1):
            dve.wait_ge(sem("turned"), 1)
            dve.tensor_copy(nT[:, c, :], bank[c]).then_inc(sem("turned_copied"), 1)
        dve.wait_ge(sem("qb1_zeroed"), 1)
        for c in range(NC):
            dve.wait_ge(sem("self_proj_done"), c + 1)
            for g in (0, 1):
                dve.tensor_scalar(qb1[32 * g:32 * g + 32, :, 2 * c + g // 2, (g % 2) * S:(g % 2) * S + S],
                                  bank[c][32 * g:32 * g + 32, :].rearrange("p (b s) -> p b s", b=B),
                                  SCALE, None, ALU.mult).then_inc(sem("qb1_filled_v"), 1)
        for c in (0, 1):
            dve.wait_ge(sem("self_proj_done"), NC + c + 1)
            dve.tensor_copy(kT1[:, c, :], bank[4 + c]).then_inc(sem("k1_copied"), 1)
        for t in (0, 1):
            dve.wait_ge(sem("self_proj_done"), 2 * NC + t + 1)
            dve.tensor_copy(v1[:, t, :], bank[t]).then_inc(sem("v1_copied"), 1)

        def scores(b):
            k = b % 2
            rows = s1[:, k, :].rearrange("p (h t) -> p h t", h=NP)
            dve.wait_ge(sem("s1_done"), b + 1)
            if b >= 2:
                dve.wait_ge(sem("p1_ready"), b - 1)
            link(dve.tensor_tensor(rows, bank[k].rearrange("p (h t) -> p h t", h=NP), over_tiles(mask[:, :], NP), ALU.add))
            link(dve.tensor_reduce(nmax[:, k, :], rows, AX.X, ALU.max, negate=True))
            dve.tensor_tensor(rows, rows, over_width(nmax[:, k, :], S), ALU.add).then_inc(sem("s1_ready"), 1)

        def rest(b):
            k, r = b % 2, slice((b % 2) * S, (b % 2) * S + S)
            dve.wait_ge(sem("p1_ready"), b + 1)
            link(dve.tensor_reduce(esum[:, k, :], p1[:, k, :].rearrange("p (h t) -> p h t", h=NP), AX.X, ALU.add))
            link(dve.reciprocal(rinv[:, k, :], esum[:, k, :]))
            dve.wait_ge(sem("pT1_done"), b + 1)
            dve.tensor_copy(pT1[r, 0:512], bank[2 + 2 * k][0:S, :]).then_inc(sem("pT1_copied_v"), 1)
            dve.wait_ge(sem("o1_done"), b + 1)
            for odd in (0, 1):
                q = slice(odd * S, odd * S + S)
                dve.tensor_tensor(sa[r, b // 2, :].rearrange("p (n h e) -> p n h e", n=NP, h=2)[:, :, odd, :],
                                  bank[6 + k][q, :].rearrange("p (n h e) -> p n h e", n=NP, h=2)[:, :, odd, :],
                                  over_width(rinv[q, k, :], E), ALU.mult).then_inc(sem("sa_written"), 1)

        dve.wait_ge(sem("mask_ready"), 2)
        scores(0)
        for b in range(B):
            if b + 1 < B:
                scores(b + 1)
            rest(b)
        dve.wait_ge(sem("sa_written"), 2 * B)
        dve.wait_ge(sem("self_rows_loaded"), 64)
        link(dve.tensor_tensor(sa[:, :, :], sa[:, :, :], over_tiles(bv1[:, :]), ALU.add))
        link(dve.tensor_tensor(sa[:, :, :], sa[:, :, :], xa[:, :, :], ALU.add))
        norm_stats(dve, link, sa)
        for t in range(NT):
            link(norm_apply(dve, 1, sa, sa, t))
        link(dve.tensor_tensor(sa[:, :, :], sa[:, :, :], over_tiles(g1[:, :]), ALU.mult))
        dve.tensor_tensor(xa[:, :, :], sa[:, :, :], over_tiles(be1[:, :]), ALU.add).then_inc(sem("xa_ready"), 1)
        for c in (0, 1):
            dve.wait_ge(sem("turned"), 2)
            dve.tensor_copy(nT[:, c, :], bank[c]).then_inc(sem("turned_copied"), 1)
        dve.wait_ge(sem("w2_high"), 1)
        dve.tensor_tensor(wk_l[:, :, :], wk2[:, :, :], wk_h[:, :, :].bitcast(F32), ALU.subtract).then_inc(sem("w2_low"), 1)
        dve.wait_ge(sem("w2_high"), 2)
        dve.tensor_tensor(wv_l[:, :, :], wv2[:, :, :], wv_h[:, :, :].bitcast(F32), ALU.subtract).then_inc(sem("w2_low"), 1)

    def act_self(act):
        for c in (2, 3):
            act.wait_ge(sem("turned"), 1)
            act.copy(nT[:, c, :], bank[c]).then_inc(sem("turned_copied"), 1)
        act.wait_ge(sem("qb1_zeroed"), 1)
        for c in range(NC):
            act.wait_ge(sem("self_proj_done"), c + 1)
            for g in (2, 3):
                act.mul(qb1[32 * g:32 * g + 32, :, 2 * c + g // 2, (g % 2) * S:(g % 2) * S + S],
                        bank[c][32 * g:32 * g + 32, :].rearrange("p (b s) -> p b s", b=B),
                        SCALE).then_inc(sem("qb1_filled_a"), 1)
        for c in (2, 3):
            act.wait_ge(sem("self_proj_done"), NC + c + 1)
            act.copy(kT1[:, c, :], bank[4 + c]).then_inc(sem("k1_copied"), 1)
        for t in (2, 3):
            act.wait_ge(sem("self_proj_done"), 2 * NC + t + 1)
            act.copy(v1[:, t, :], bank[t]).then_inc(sem("v1_copied"), 1)
        for b in range(B + 1):
            if b < B:
                k = b % 2
                act.wait_ge(sem("s1_ready"), b + 1)
                if b >= 2:
                    act.wait_ge(sem("pT1_done"), b - 1)
                    act.wait_ge(sem("sa_written"), 2 * (b - 1))
                act.activation(p1[:, k, :], s1[:, k, :], ACT.Exp).then_inc(sem("p1_ready"), 1)
            if b >= 1:
                r = slice(((b - 1) % 2) * S, ((b - 1) % 2) * S + S)
                act.wait_ge(sem("pT1_done"), b)
                act.copy(pT1[r, 512:1024], bank[3 + 2 * ((b - 1) % 2)][0:S, :]).then_inc(sem("pT1_copied_a"), 1)
        for c in (2, 3):
            act.wait_ge(sem("turned"), 2)
            act.copy(nT[:, c, :], bank[c]).then_inc(sem("turned_copied"), 1)
        act.wait_ge(sem("o1_done"), B)
        act.wait_ge(sem("wk2_loaded"), 16)
        act.copy(wk_h[:, :, :], wk2[:, :, :]).then_inc(sem("w2_high"), 1)
        act.wait_ge(sem("wv2_loaded"), 16)
        act.copy(wv_h[:, :, :], wv2[:, :, :]).then_inc(sem("w2_high"), 1)
        for c in range(NC):
            act.wait_ge(sem("self_proj_done"), 2 * NC + NT + c + 1)
            act.mul(qT[:, c, :], bank[4 + c], SCALE).then_inc(sem("qT_ready"), 1)

    def pe_self(pe):
        pe.wait_ge(sem("ident_ready"), 1)
        for t in range(NT):
            pe.wait_ge(sem("n0_ready"), t + 1)
            for c in range(NC):
                m = pe.transpose(bank[c][:, t * P:(t + 1) * P], xa[:, t, c * P:(c + 1) * P], ident[:, :])
        m.then_inc(sem("turned"), 1)
        pe.wait_ge(sem("turned_copied"), 4)
        for i, (name, b0) in enumerate((("wq1", 0), ("wk1", 4))):
            pe.wait_ge(sem(f"{name}_loaded"), 16)
            for j in range(NC):
                for c in range(NC):
                    m = pe.matmul(bank[b0 + j], w_in[i][:, c, j * P:(j + 1) * P], nT[:, c, :], start=c == 0, stop=c == NC - 1)
                m.then_inc(sem("self_proj_done"), 1)
        pe.wait_ge(sem("wv1_loaded"), 16)
        for t in range(NT):
            pe.wait_ge(sem("qb1_filled_v"), 2 * (t + 1))
            pe.wait_ge(sem("qb1_filled_a"), 2 * (t + 1))
            for c in range(NC):
                m = pe.matmul(bank[t], nT[:, c, t * P:(t + 1) * P], w_in[2][:, c, :], start=c == 0, stop=c == NC - 1)
            m.then_inc(sem("self_proj_done"), 1)

        def scores(b):
            if b >= 2:
                pe.wait_ge(sem("s1_ready"), b - 1)
            for p in range(NP):
                m = pe.matmul(bank[b % 2][:, p * S:(p + 1) * S], qb1[:, b, p, :], kT1[:, p // 2, b * S:(b + 1) * S],
                              start=True, stop=True)
            m.then_inc(sem("s1_done"), 1)

        pe.wait_ge(sem("k1_copied"), NC)
        pe.wait_ge(sem("v1_copied"), NT)
        scores(0)
        for b in range(B):
            k, r = b % 2, slice((b % 2) * S, (b % 2) * S + S)
            if b + 1 < B:
                scores(b + 1)
            pe.wait_ge(sem("p1_ready"), b + 1)
            if b >= 2:
                pe.wait_ge(sem("pT1_copied_v"), b - 1)
                pe.wait_ge(sem("pT1_copied_a"), b - 1)
            for p in range(NP):
                m = pe.transpose(bank[2 + 2 * k + p // 4][0:S, (p % 4) * P:(p % 4 + 1) * P], p1[:, k, p * S:(p + 1) * S],
                                 ident[:, :])
            m.then_inc(sem("pT1_done"), 1)
            pe.wait_ge(sem("pT1_copied_v"), b + 1)
            pe.wait_ge(sem("pT1_copied_a"), b + 1)
            if b >= 2:
                pe.wait_ge(sem("sa_written"), 2 * (b - 1))
            for p in range(NP):
                m = pe.matmul(bank[6 + k][:, p * S:(p + 1) * S], pT1[r, p * P:(p + 1) * P], v1[r, b // 2, p * S:(p + 1) * S],
                              start=True, stop=True)
            m.then_inc(sem("o1_done"), 1)
        pe.wait_ge(sem("xa_ready"), 1)
        for t in range(NT):
            for c in range(NC):
                m = pe.transpose(bank[c][:, t * P:(t + 1) * P], xa[:, t, c * P:(c + 1) * P], ident[:, :])
        m.then_inc(sem("turned"), 1)
        pe.wait_ge(sem("turned_copied"), 8)
        pe.wait_ge(sem("wq2_loaded"), 16)
        for j in range(NC):
            for c in range(NC):
                m = pe.matmul(bank[4 + j], wq2[:, c, j * P:(j + 1) * P], nT[:, c, :], start=c == 0, stop=c == NC - 1)
            m.then_inc(sem("self_proj_done"), 1)

    PROJ = []
    for g in range(NG - 2):
        PROJ += [("k", g, 0), ("k", g, 1), ("v", 2 * g), ("v", 2 * g + 1)]
    PROJ += [("k", g, j) for g in (NG - 2, NG - 1) for j in (0, 1)]
    PROJ += [("v", t) for t in range(2 * (NG - 2), CT)]
    QUART = -(-CT // 4)
    JOBS = PROJ + [("p", p, q) for p in range(NP) for q in range(QUART)]
    NJ = len(JOBS)
    FIRST_P = len(PROJ)
    EARLY = FIRST_P - 1

    def last_job(g):
        return max(k for k, j in enumerate(PROJ) if (j[1] if j[0] == "k" else j[1] // 2) == g)

    def group_width(g):
        return min(G, CW - g * G)

    def tile_rows(t):
        return min(P, CTX - t * P)

    def job_views(k):
        job, bk = JOBS[k], ring[k % 3]
        if job[0] == "k":
            w = group_width(job[1])
            s = slice(job[1] * G, job[1] * G + w)
            c = slice(2 * job[2], 2 * job[2] + 2)
            return bk[:, :].rearrange("p (c w) -> p c w", c=2)[:, :, 0:w], kT_h[:, c, s], kT_l[:, c, s]
        if job[0] == "v":
            r = tile_rows(job[1])
            return bk[0:r, :], v_h[0:r, job[1], :], v_l[0:r, job[1], :]
        t0 = 4 * job[2]
        n = min(4, CT - t0)
        r = tile_rows(t0 + n - 1)
        return (bk[0:r, 0:n * P].rearrange("p (t w) -> p t w", t=n), pT_h[0:r, t0:t0 + n, :], pT_l[0:r, t0:t0 + n, :])

    def loads_before(b0, i, g):
        return NG * i + (NG * b0 + g) // 2 + 1

    def sp_cross(sp, b0, i, first=False):
        b = b0 + 2 * i
        for g in range(NG):
            k, w = (b0 + g) % 2, min(G, CTX - g * G)
            if not (first and g < 2):
                sp.wait_ge(sem("ctx_low"), NG * b + g - 1)
            sp.dma_start(raw[:, k, :, 0:w],
                         a["ctxT"][b, :, g * G:g * G + w].rearrange("(c p) t -> p c t", p=P)).then_inc(sem(f"ctx_loaded{k}"), 16)

    def dve_queries(dve, b0, i):
        b = b0 + 2 * i
        dve.wait_ge(sem("qT_ready"), NC)
        for k in range(8):
            g = k % 4
            r = slice(32 * g, 32 * g + 32)
            src = qT[r, :, bass.ds(b * S, S)]
            hi = qb_h[r, :, :].rearrange("p (c h) w -> p c h w", h=2)[:, :, g // 2, (g % 2) * S:(g % 2) * S + S]
            lo = qb_l[r, :, :].rearrange("p (c h) w -> p c h w", h=2)[:, :, g // 2, (g % 2) * S:(g % 2) * S + S]
            if k < 4:
                dve.tensor_scalar(hi, src, 1.0, None, ALU.mult).then_inc(sem("queries_ready"), 1)
            else:
                dve.wait_ge(sem("queries_ready"), 8 * b + g + 1)
                dve.tensor_tensor(lo, src, hi.bitcast(F32), ALU.subtract).then_inc(sem("queries_ready"), 1)

    def pe_cross(pe, b0, i, first=False):
        b = b0 + 2 * i
        J = NJ * b

        def claim(k):
            if k >= 3:
                pe.wait_ge(sem("job_low"), J + k - 2)
            elif k == 0 and not first:
                pe.wait_ge(sem("job_low"), J)

        def project(k):
            job = PROJ[k]
            g = job[1] if job[0] == "k" else job[1] // 2
            s = (b0 + g) % 2
            claim(k)
            if job[0] == "k":
                w = group_width(g)
                pe.wait_ge(sem("ctx_low"), NG * b + g + 1)
                for j in (0, 1):
                    e = slice((2 * job[2] + j) * P, (2 * job[2] + j + 1) * P)
                    for c in range(NC):
                        for n, (wt, xt) in enumerate(((wk_h, x_h), (wk_h, x_l), (wk_l, x_h))):
                            m = pe.matmul(ring[k % 3][:, j * G:j * G + w], wt[:, c, e], xt[:, s, c, 0:w],
                                          start=c == 0 and n == 0, stop=c == NC - 1 and n == 2)
            else:
                r = min(P, CW - job[1] * P)
                t = slice((job[1] % 2) * P, (job[1] % 2) * P + r)
                for c in range(NC):
                    for n, (xt, wt) in enumerate(((x_h, wv_h), (x_h, wv_l), (x_l, wv_h))):
                        m = pe.matmul(ring[k % 3][0:r, :], xt[:, s, c, t], wt[:, c, :],
                                      start=c == 0 and n == 0, stop=c == NC - 1 and n == 2)
            m.then_inc(sem("job_done"), 1)

        def scores(p):
            if p == 0:
                pe.wait_ge(sem("queries_ready"), 8 * (b + 1))
            if not (first and p == 0):
                pe.wait_ge(sem("prob_ready"), NP * b + p)
            for n in range(4):
                w = min(512, CW - n * 512)
                for j, (qt, kt) in enumerate(((qb_h, kT_h), (qb_h, kT_l), (qb_l, kT_h))):
                    m = pe.matmul(sc[:, n, 0:w], qt[:, p, :], kt[:, p // 2, n * 512:n * 512 + w], start=j == 0, stop=j == 2)
            m.then_inc(sem("scores_done"), 1)

        def transposes(p):
            pe.wait_ge(sem("prob_ready"), NP * b + p + 1)
            for q in range(QUART):
                k = FIRST_P + QUART * p + q
                claim(k)
                for t in range(4 * q, min(4 * q + 4, CT)):
                    r = tile_rows(t)
                    m = pe.transpose(ring[k % 3][0:r, (t % 4) * P:(t % 4 + 1) * P], prob[:, t * P:t * P + r], ident[:, :])
                m.then_inc(sem("job_done"), 1)

        def outputs(p):
            pe.wait_ge(sem("job_low"), J + FIRST_P + QUART * (p + 1))
            if p == 0 and not first:
                pe.wait_ge(sem("cross_written"), 2 * b)
            e = slice(p * S, (p + 1) * S)
            for t in range(CT):
                r = tile_rows(t)
                for n, (pt, vt) in enumerate(((pT_h, v_h), (pT_h, v_l), (pT_l, v_h))):
                    m = pe.matmul(pv[:, e], pt[0:r, t, :], vt[0:r, t, e], start=t == 0 and n == 0, stop=t == CT - 1 and n == 2)
            m.then_inc(sem("outputs_done"), 1)

        if first:
            pe.wait_ge(sem("w2_low"), 2)
        for k in range(EARLY):
            project(k)
        pe.wait_ge(sem("job_low"), J + EARLY)
        scores(0)
        project(EARLY)
        for p in range(NP):
            transposes(p)
            if p + 1 < NP:
                scores(p + 1)
            outputs(p)

    def split_ready(eng, b0, i, g, first=False):
        b = b0 + 2 * i
        k = (b0 + g) % 2
        eng.wait_ge(sem(f"ctx_loaded{k}"), 16 * loads_before(b0, i, g))
        if not (first and g < 2):
            J = NJ * b + last_job(g - 2) + 1 if g >= 2 else NJ * (b - 1) + last_job(NG - 2 + g) + 1
            eng.wait_ge(sem("job_done"), J)

    def act_split(act, b0, i, g, first=False):
        k, w = (b0 + g) % 2, group_width(g)
        split_ready(act, b0, i, g, first)
        act.copy(x_h[:, k, :, 0:w], raw[:, k, :, 0:w]).then_inc(sem("ctx_high"), 1)

    def dve_split(dve, b0, i, g, first=False):
        b = b0 + 2 * i
        k, w = (b0 + g) % 2, group_width(g)
        dve.wait_ge(sem("ctx_high"), NG * b + g + 1)
        dve.tensor_tensor(x_l[:, k, :, 0:w], raw[:, k, :, 0:w], x_h[:, k, :, 0:w].bitcast(F32), ALU.subtract)\
           .then_inc(sem("ctx_low"), 1)

    def act_cross(act, b0, i, first=False, last=False):
        b = b0 + 2 * i
        J = NJ * b

        def high(k):
            src, hi, _ = job_views(k)
            act.wait_ge(sem("job_done"), J + k + 1)
            act.copy(hi, src).then_inc(sem("job_high"), 1)

        if first:
            act_split(act, b0, i, 0, True)
            act_split(act, b0, i, 1, True)
        for g in range(NG - 2):
            for k in range(4 * g, 4 * g + 4):
                high(k)
            act_split(act, b0, i, g + 2)
        for k in range(4 * (NG - 2), EARLY):
            high(k)
        for p in range(NP):
            act.wait_ge(sem("max_ready"), NP * b + p + 1)
            if p >= 1:
                act.wait_ge(sem("job_done"), J + FIRST_P + QUART * p)
            act.activation(prob[:, 0:CTX], sc[:, :, :].rearrange("p n w -> p (n w)")[:, 0:CTX], ACT.Exp,
                           bias=nmax[:, b0 % 2, p:p + 1], accum_out=esum[:, b0 % 2, p:p + 1]).then_inc(sem("prob_ready"), 1)
            if p == 0:
                high(EARLY)
            for k in range(FIRST_P + QUART * p, FIRST_P + QUART * (p + 1)):
                high(k)
            if p in (1, 2) and not last:
                act_split(act, b0 + 1, i, p - 1)

    def dve_cross(dve, b0, i, first=False, last=False):
        b = b0 + 2 * i
        J = NJ * b

        def low(k):
            src, hi, lo = job_views(k)
            dve.wait_ge(sem("job_high"), J + k + 1)
            dve.tensor_tensor(lo, src, hi.bitcast(F32), ALU.subtract).then_inc(sem("job_low"), 1)

        if first:
            dve.wait_ge(sem("queries_zeroed"), 1)
            dve_queries(dve, b0, i)
            dve_split(dve, b0, i, 0, True)
            dve_split(dve, b0, i, 1, True)
        for g in range(NG - 2):
            for k in range(4 * g, 4 * g + 4):
                low(k)
            dve_split(dve, b0, i, g + 2)
        for k in range(4 * (NG - 2), EARLY):
            low(k)
        for p in range(NP):
            dve.wait_ge(sem("scores_done"), NP * b + p + 1)
            dve.tensor_reduce(nmax[:, b0 % 2, p:p + 1], sc[:, :, :].rearrange("p n w -> p (n w)")[:, 0:CTX], AX.X, ALU.max,
                              negate=True).then_inc(sem("max_ready"), 1)
            if p == 0:
                low(EARLY)
            for k in range(FIRST_P + QUART * p, FIRST_P + QUART * (p + 1)):
                low(k)
            if p in (1, 2) and not last:
                dve_split(dve, b0 + 1, i, p - 1)
        if not last:
            dve_queries(dve, b0 + 1, i)
        dve.reciprocal(rinv[:, b0 % 2, :], esum[:, b0 % 2, :]).then_inc(sem("inverse_ready"), 1)
        dve.wait_ge(sem("inverse_ready"), b + 1)
        dve.wait_ge(sem("outputs_done"), NP * (b + 1))
        r = slice((b0 % 2) * S, (b0 % 2) * S + S)
        for odd in (0, 1):
            q = slice(odd * S, odd * S + S)
            dve.tensor_tensor(cat[r, :].rearrange("p (n h e) -> p n h e", n=NP, h=2)[:, :, odd, :],
                              pv[q, :].rearrange("p (n h e) -> p n h e", n=NP, h=2)[:, :, odd, :],
                              over_width(rinv[q, b0 % 2, :], E), ALU.mult).then_inc(sem("cross_written"), 1)
        dve.wait_ge(sem("cross_written"), 2 * (b + 1))
        t = i + b0 // 2
        dve.tensor_tensor(xa[r, t, :], xa[r, t, :], cat[r, :], ALU.add).then_inc(sem("cross_added"), 1)

    def batches(eng, step, **ends):
        step(eng, 0, 0, first=True)
        with eng.Fori(0, (B - 2) // 2) as i:
            step(eng, 1, i)
            step(eng, 2, i)
        step(eng, B - 1, 0, **ends)

    rows4 = at("rows4", R, [P, 4, D])
    bf2 = at("bf2", R + 8192, [P, D])
    bf1 = at("bf1", R + 10240, [P, NH])
    wf1 = at("wf1", R + 16384, [P, NC, HID])
    wf2 = at("wf2", R + 49152, [P, NH, D])
    hid = at("hid", R + 81920, [P, NH, TOK])
    xT = at("xT", R + 114688, [P, NC, TOK])
    tmp = at("tmp", R + 122880, [P, NT, D])
    xres = at("xres", R + 131072, [P, NT, D])

    def sp_ffn(sp):
        sp.wait_ge(sem("queries_ready"), 8 * B)
        for i, name in enumerate(("g2", "be2", "g3", "be3")):
            sp.dma_start(rows4[:, i, :], row_dram(name)).then_inc(sem("ffn_rows_loaded"), 16)
        sp.wait_ge(sem("job_done"), NJ * (B - 1) + FIRST_P)
        sp.dma_start(wf1[:, :, :], w_dram("wf1")).then_inc(sem("wf1_loaded"), 16)
        sp.wait_ge(sem("scores_done"), NP * B)
        sp.dma_start(bf2[:, :], row_dram("bf2")).then_inc(sem("ffn_rows_loaded"), 16)
        sp.dma_start(bf1[:, :], a["bf1"]).then_inc(sem("ffn_rows_loaded"), 16)
        sp.dma_start(wf2[:, :, :], w_dram("wf2")).then_inc(sem("wf2_loaded"), 16)
        sp.wait_ge(sem("outputs_done"), NP * B)
        sp.dma_start(xres[:, :, :], x_dram).then_inc(sem("xres_loaded"), 16)

    def pe_turn(pe, src, ready):
        pe.wait_ge(sem(ready), 1)
        for t in range(NT):
            for c in range(NC):
                m = pe.transpose(bank[c][:, t * P:(t + 1) * P], src[:, t, c * P:(c + 1) * P], ident[:, :])
        m.then_inc(sem("turned"), 1)

    def copy_turned(eng, copy, n, chunks, dst):
        eng.wait_ge(sem("turned"), n + 1)
        for c in chunks:
            copy(dst[:, c, :], bank[c]).then_inc(sem("turned_copied"), 1)

    def pool_ffn(pool, link):
        norm_rstd(pool, link, 2)
        norm_rstd(pool, link, 3)

    def dve_ffn(dve, link):
        dve.wait_ge(sem("cross_added"), B)
        dve.wait_ge(sem("ffn_rows_loaded"), 96)
        link(dve.tensor_tensor(xa[:, :, :], xa[:, :, :], over_tiles(bv2[:, :]), ALU.add))
        norm_stats(dve, link, xa)
        for t in range(NT):
            link(norm_apply(dve, 2, xa, xa, t))
        link(dve.tensor_tensor(xa[:, :, :], xa[:, :, :], over_tiles(rows4[:, 0, :]), ALU.mult))
        dve.tensor_tensor(xa[:, :, :], xa[:, :, :], over_tiles(rows4[:, 1, :]), ALU.add).then_inc(sem("xb_ready"), 1)
        copy_turned(dve, dve.tensor_copy, 2, (0, 1), xT)
        dve_xor(dve, link)
        for m in range(1, NH, 2):
            dve.wait_ge(sem("hid_done"), m + 1)
            dve.tensor_scalar(hid[:, m, :], bank[4 + m % 4], bf1[:, m:m + 1], 0.0, ALU.add, ALU.max)\
               .then_inc(sem("hid_ready_v"), 1)
        dve.wait_ge(sem("xb_ready"), 1)
        link(dve.tensor_tensor(xa[:, :, :], xa[:, :, :], over_tiles(bf2[:, :]), ALU.add))
        for t in range(NT):
            dve.wait_ge(sem("ffn_done"), t + 1)
            link(dve.tensor_tensor(tmp[:, t, :], bank[t], xa[:, t, :], ALU.add))
        norm_stats(dve, link, tmp)
        for t in range(NT):
            link(norm_apply(dve, 3, tmp, tmp, t))
        link(dve.tensor_tensor(tmp[:, :, :], tmp[:, :, :], over_tiles(rows4[:, 2, :]), ALU.mult))
        link(dve.tensor_tensor(tmp[:, :, :], tmp[:, :, :], over_tiles(rows4[:, 3, :]), ALU.add))
        dve.wait_ge(sem("xres_loaded"), 16)
        link(dve.tensor_tensor(xa[:, :, :], tmp[:, :, :], xres[:, :, :], ALU.add))

    def act_ffn(act):
        copy_turned(act, act.copy, 2, (2, 3), xT)
        act.wait_ge(sem("ffn_rows_loaded"), 96)
        for m in range(0, NH, 2):
            act.wait_ge(sem("hid_done"), m + 1)
            act.activation(hid[:, m, :], bank[4 + m % 4], ACT.Relu, bias=bf1[:, m:m + 1]).then_inc(sem("hid_ready_a"), 1)

    def pe_ffn(pe):
        pe_turn(pe, xa, "xb_ready")
        pe.wait_ge(sem("turned_copied"), 12)
        pe.wait_ge(sem("wf1_loaded"), 16)
        for m in range(NH):
            if m >= 4:
                pe.wait_ge(sem("hid_ready_v" if m % 2 else "hid_ready_a"), (m - 4) // 2 + 1)
            for c in range(NC):
                k = pe.matmul(bank[4 + m % 4], wf1[:, c, m * P:(m + 1) * P], xT[:, c, :], start=c == 0, stop=c == NC - 1)
            k.then_inc(sem("hid_done"), 1)
        pe.wait_ge(sem("wf2_loaded"), 16)
        pe.wait_ge(sem("hid_ready_v"), NH // 2)
        pe.wait_ge(sem("hid_ready_a"), NH // 2)
        for t in range(NT):
            for m in range(NH):
                k = pe.matmul(bank[t], hid[:, m, t * P:(t + 1) * P], wf2[:, m, :], start=m == 0, stop=m == NH - 1)
            k.then_inc(sem("ffn_done"), 1)

    NM = NT * GH
    LEVELS = (1, 2, 4, 8, 16, 32)
    kf = at("kf", R + 81920, [P, GH, TOK])
    qf = at("qf", R + 90112, [P, GH, TOK])
    vf = at("vf", R + 98304, [P, GH, TOK])
    ema = at("ema", R + 106496, [P, GH, TOK])
    vtok = at("vtok", R + 122880, [P, NM, P])
    qk = at("qk", R + 131072, [P, NM, P])
    nT_s = at("nT_s", R + 139264, [P, NM, P])
    nT_all = at("nT_all", R + 147456, [P, NM, P])
    xm = at("xm", R, [P, NM, P])
    xmT = at("xmT", R + 8192, [P, NM, P])
    dwo = at("dwo", R + 159744, [P, NC, D])
    dw = [at(f"dw{i}", R + 167936 + 8192 * i, [P, NC, D]) for i in range(3)]
    ybuf = at("ybuf", R + 167936, [P, NM, P])
    tbuf = at("tbuf", R + 176128, [P, NM, P])
    rbuf = at("rbuf", R + 184320, [P, NM, P])
    S0 = R + 192512
    conv = at("conv", S0, [P, 3, NC, TAPS])
    wgates = at("wgates", S0 + 192, [P, NC, 12])
    cmix = at("cmix", S0 + 384, [GH, TAPS])
    mbias = at("mbias", S0 + 416, [GH, 1])
    hbias = at("hbias", S0 + 448, [GH, 1])
    sel = at("sel", S0 + 512, [GH, GH, P])
    rmsw = at("rmsw", S0 + 2560, [P, P])
    gtok = at("gtok", S0 + 3072, [P, 2, NT, GH])
    norms = at("norms", S0 + 3200, [P, 2, NM])
    scal = at("scal", S0 + 3328, [P, 4, NM])
    Z = at("Z", S0 + 3584, [P, 2, P])
    zint = at("zint", S0 + 4608, [P, 2, P], mybir.dt.int32)
    masks = at("masks", R + 155648, [P, len(LEVELS), P])
    mask1 = at("mask1", R + 158720, [P, P])
    incl = at("incl", R + 159232, [P, P])
    gamma = at("gamma", S0 + 5632, [GH, TOK])
    beta = at("beta", 2048, [GH, TOK])
    mixr = at("mixr", R + 122880, [GH, TOK])
    trow = at("trow", R + 124928, [GH, TOK])
    th = at("th", R + 131072, [P, 3 * NC, TOK])
    NPROJ = 3 * NC
    feats = (kf, qf, vf)

    def sp_delta(sp):
        for i, name in enumerate(("dwk", "dwq", "dwv")):
            sp.dma_start(dw[i][:, :, :], w_dram(name)).then_inc(sem("dw_loaded"), 16)
        for i, name in enumerate(("conv_k", "conv_q", "conv_v")):
            sp.dma_start(conv[:, i, :, :], a[name]).then_inc(sem("delta_small_loaded"), 16)
        sp.dma_start(wgates[:, :, :], w_dram("wgates")).then_inc(sem("delta_small_loaded"), 16)
        sp.dma_start(cmix[:, :], a["conv_mix"]).then_inc(sem("delta_small_loaded"), 16)
        sp.dma_start(mbias[:, :], a["mix_bias"]).then_inc(sem("delta_small_loaded"), 16)
        sp.dma_start(rmsw[:, :], row_dram("rms_w")).then_inc(sem("delta_small_loaded"), 16)
        sp.dma_start(wg[:, :, :], w_dram("wg")).then_inc(sem("delta_small_loaded"), 16)
        sp.dma_start(bg[:, :], row_dram("bg")).then_inc(sem("delta_small_loaded"), 16)
        sp.dma_start(dwo[:, :, :], w_dram("dwo")).then_inc(sem("dwo_loaded"), 16)

    def pool_masks(pool, link):
        pool.wait_ge(sem("outputs_done"), NP * B)
        link(pool.iota(zint[:, 0, :], pattern=[[0, P]], base=0, channel_multiplier=1))
        pool.iota(zint[:, 1, :], pattern=[[1, P]], base=0, channel_multiplier=0).then_inc(sem("indices_ready"), 1)
        pool.wait_ge(sem("xor_ready"), 1)
        link(pool.affine_select(out=Z[:, 0, :], in_=Z[:, 0, :], compare_op=ALU.is_gt, fill=0.0, base=0,
                                pattern=[[-1, P]], channel_multiplier=1))
        link(pool.affine_select(out=Z[:, 1, :], in_=Z[:, 1, :], compare_op=ALU.is_gt, fill=0.0, base=0,
                                pattern=[[1, P]], channel_multiplier=-1))

        def between(dst, z, lo, hi):
            link(pool.tensor_scalar(dst, z, float(lo), None, ALU.is_ge))
            link(pool.tensor_scalar(incl[:, :], z, float(hi), None, ALU.is_ge))
            link(pool.tensor_tensor(dst, dst, incl[:, :], ALU.subtract))

        for i, s in enumerate(LEVELS):
            between(masks[:, i, :], Z[:, 1, :], s, 2 * s)
        between(mask1[:, :], Z[:, 0, :], 1, 2)
        link(pool.tensor_scalar(incl[:, :], Z[:, 1, :], float(S), None, ALU.is_ge))
        link(pool.tensor_scalar(Z[:, 1, :], Z[:, 1, :], 1.0, None, ALU.is_ge))
        link(pool.tensor_tensor(incl[:, :], Z[:, 1, :], incl[:, :], ALU.subtract))
        link(pool.tensor_tensor(incl[:, :], incl[:, :], ident[:, :], ALU.add))
        link(pool.memset(sel[:, :, :], 0.0))
        pool.affine_select(out=sel[:, :, :], in_=sel[:, :, :], compare_op=ALU.not_equal, fill=1.0, base=0,
                           pattern=[[-1, GH], [0, P]], channel_multiplier=1).then_inc(sem("masks_ready"), 1)

    def dve_xor(dve, link):
        dve.wait_ge(sem("indices_ready"), 1)
        link(dve.tensor_tensor(zint[:, 0, :], zint[:, 0, :], zint[:, 1, :], ALU.bitwise_xor))
        link(dve.tensor_copy(Z[:, 0, :], zint[:, 0, :]))
        dve.tensor_copy(Z[:, 1, :], zint[:, 0, :]).then_inc(sem("xor_ready"), 1)

    def level_matrix(m):
        return slice((m % 4) * P, (m % 4 + 1) * P)

    def four(v, t):
        return v[:, 4 * t:4 * t + 4, :].rearrange("p m w -> p (m w)")

    def four3(v, t):
        return v[:, 4 * t:4 * t + 4, :]

    def bank3(i):
        return bank[i].rearrange("p (m w) -> p m w", m=4)

    def pool_delta(pool, link):
        norm_rstd(pool, link, 4)
        for i, f in enumerate((kf, qf)):
            pool.wait_ge(sem("feature_ready"), NC * (i + 1))
            pool.tensor_tensor(th[:, 4 * i:4 * i + 4, :], f[:, :, :], f[:, :, :], ALU.mult).then_inc(sem("squares_ready"), 1)
        pool.wait_ge(sem("norms_summed"), 1)
        link(pool.tensor_tensor(norms[:, :, :].rearrange("p a m -> p (a m)"), norms[:, :, :].rearrange("p a m -> p (a m)"),
                                mhalf[:, 0:2 * NM], ALU.pow))
        pool.tensor_tensor(scal[:, 0, :], norms[:, 0, :], norms[:, 0, :], ALU.mult).then_inc(sem("norms_ready"), 1)
        for l in range(1, len(LEVELS)):
            if l == 1:
                pool.wait_ge(sem("nT_ready"), NT)
                pool.wait_ge(sem("transposed_n"), NT)
                pool.wait_ge(sem("xm_started"), 1)
            else:
                pool.wait_ge(sem("y_done"), NT * (l - 1))
            for t in range(NT):
                pool.tensor_tensor(four3(nT_s, t), four3(nT_all, t), over_tiles(masks[:, l, :], 4), ALU.mult)\
                    .then_inc(sem("level_ready"), 1)
        pool.wait_ge(sem("mean_square"), 1)
        pool.tensor_tensor(norms[:, 0, :], norms[:, 0, :], mhalf[:, 0:NM], ALU.pow).then_inc(sem("rms_ready"), 1)

    def dve_delta(dve, link):
        norm_stats(dve, link, xa)
        for t in range(NT):
            norm_apply(dve, 4, tmp, xa, t).then_inc(sem("n1_ready"), 1)
        copy_turned(dve, dve.tensor_copy, 3, (0, 1), xT)
        dve.wait_ge(sem("delta_small_loaded"), 16 * 9)
        dve.tensor_scalar(hbias[:, :], mbias[:, :], 0.5, None, ALU.mult).then_inc(sem("hbias_ready"), 1)
        for i, g in enumerate((beta, gamma)):
            dve.wait_ge(sem("gate_tanh"), i + 1)
            dve.tensor_scalar(g[:, :], g[:, :], 0.5, 0.5, ALU.mult, ALU.add).then_inc(sem("gates_ready"), 1)
        logit = bank[6][0:GH, :].rearrange("p (b s) -> p b s", b=B)
        mix3 = mixr[:, :].rearrange("p (b s) -> p b s", b=B)
        dve.wait_ge(sem("gates_done"), 3)
        link(dve.tensor_scalar(mix3, logit, cmix[:, TAPS - 1:TAPS], None, ALU.mult))
        for k in range(1, TAPS):
            ins = dve.scalar_tensor_tensor(mix3[:, :, k:S], logit[:, :, 0:S - k], cmix[:, TAPS - 1 - k:TAPS - k],
                                           mix3[:, :, k:S], ALU.mult, ALU.add)
            if k < TAPS - 1:
                link(ins)
        ins.then_inc(sem("mix_conv"), 1)
        dve.wait_ge(sem("mix_tanh"), 1)
        dve.scalar_tensor_tensor(mixr[:, :], trow[:, :], 1.0, mixr[:, :], ALU.add, ALU.mult).then_inc(sem("mix_silu"), 1)
        dve.wait_ge(sem("mix_tanh"), 2)
        dve.tensor_scalar(mixr[:, :], trow[:, :], 0.5, 0.5, ALU.mult, ALU.add).then_inc(sem("gates_ready"), 1)

        def dst(n):
            return feats[n // NC][:, n % NC, :]

        for n in range(NPROJ + 2):
            if n < NPROJ:
                x3 = bank[n % 4].rearrange("p (b s) -> p b s", b=B)
                y3 = dst(n).rearrange("p (b s) -> p b s", b=B)
                dve.wait_ge(sem("first_tap"), n + 1)
                for k in range(1, TAPS):
                    ins = dve.scalar_tensor_tensor(y3[:, :, k:S], x3[:, :, 0:S - k],
                                                   conv[:, n // NC, n % NC, TAPS - 1 - k:TAPS - k], y3[:, :, k:S],
                                                   ALU.mult, ALU.add)
                    if k < TAPS - 1:
                        link(ins)
                ins.then_inc(sem("conv_done"), 1)
            if 1 <= n <= NPROJ:
                m = n - 1
                dve.wait_ge(sem("tanh_first"), m + 1)
                ins = dve.scalar_tensor_tensor(dst(m), th[:, m, :], 1.0, dst(m), ALU.add, ALU.mult)
                ins.then_inc(sem("silu_first" if m < 2 * NC else "values_ready"), 1)
            if 2 <= n < 2 * NC + 2:
                m = n - 2
                dve.wait_ge(sem("tanh_second"), m + 1)
                dve.scalar_tensor_tensor(dst(m), th[:, m, :], 1.0, dst(m), ALU.add, ALU.mult)\
                   .then_inc(sem("feature_ready"), 1)
        for h in range(GH):
            dve.wait_ge(sem("gamma_spread"), h + 1)
            if h == 0:
                dve.wait_ge(sem("values_ready"), NC)
            dve.scalar_tensor_tensor(four(ybuf, h), bank[h], 1.0, vf[:, h, :], ALU.subtract, ALU.mult)\
               .then_inc(sem("gamma_used_v"), 1)
            dve.wait_ge(sem("gamma_used_a"), h + 1)
            link(dve.memset(tbuf[:, 4 * h:4 * h + 4, :].rearrange("p m w -> p (m w)")[:, 0:TOK:S], 0.0))
            dve.wait_ge(sem("gamma_used_v"), h + 1)
            dve.tensor_tensor_scan(ema[:, h, :], four(tbuf, h), four(ybuf, h), 0.0, ALU.mult, ALU.subtract)\
               .then_inc(sem("ema_ready"), 1)
        dve.wait_ge(sem("gates_turned"), 1)
        dve.tensor_copy(gtok[:, :, :, :].rearrange("p a t h -> p (a t h)"), bank[7][:, 0:2 * NM]).then_inc(sem("gtok_ready"), 1)
        dve.wait_ge(sem("norms_done"), 1)
        dve.tensor_scalar(norms[:, :, :].rearrange("p a m -> p (a m)"), bank[6][:, 0:2 * NM], 16e-6, None, ALU.add)\
           .then_inc(sem("norms_summed"), 1)
        dve.wait_ge(sem("gtok_ready"), 1)
        dve.wait_ge(sem("norms_ready"), 1)
        bt = gtok[:, 0, :, :].rearrange("p t h -> p (t h)")
        mt = gtok[:, 1, :, :].rearrange("p t h -> p (t h)")
        dve.tensor_tensor(scal[:, 0, :], scal[:, 0, :], bt, ALU.mult).then_inc(sem("factors_ready"), 1)
        dve.scalar_tensor_tensor(scal[:, 1, :], bt, 0.5, norms[:, 0, :], ALU.mult, ALU.mult).then_inc(sem("factors_ready"), 1)
        link(dve.tensor_scalar(scal[:, 2, :], mt, -1.0, 1.0, ALU.mult, ALU.add))
        link(dve.tensor_tensor(scal[:, 2, :], scal[:, 2, :], norms[:, 1, :], ALU.mult))
        link(dve.tensor_scalar(scal[:, 3, :], mt, 0.5, None, ALU.mult))
        dve.wait_ge(sem("factors_ready"), 2)

        def factor(i, t):
            return over_width(scal[:, i, 4 * t:4 * t + 4], P)

        for t in range(NT):
            dve.wait_ge(sem("v_turned"), t + 1)
            dve.tensor_tensor(four3(vtok, t), bank3(4 + t), factor(1, t), ALU.mult).then_inc(sem("vtok_ready"), 1)
        for t in range(NT):
            dve.wait_ge(sem("gram_done"), t + 1)
            dve.tensor_tensor(four3(nT_s, t), bank3(t), factor(0, t), ALU.mult).then_inc(sem("n_ready"), 1)
        dve.wait_ge(sem("n_ready"), NT)
        dve.wait_ge(sem("masks_ready"), 1)
        link(dve.tensor_tensor(tbuf[:, :, :], nT_s[:, :, :], over_tiles(mask1[:, :], NM), ALU.mult))
        link(dve.tensor_tensor(xm[:, :, :], over_tiles(ident[:, :], NM), tbuf[:, :, :], ALU.subtract))
        dve.wait_ge(sem("nT_ready"), NT)
        link(dve.tensor_tensor(tbuf[:, :, :], nT_all[:, :, :], over_tiles(masks[:, 0, :], NM), ALU.mult))
        dve.tensor_tensor(xmT[:, :, :], over_tiles(ident[:, :], NM), tbuf[:, :, :], ALU.subtract).then_inc(sem("xm_started"), 1)
        for t in range(NT):
            dve.wait_ge(sem("qk_done"), t + 1)
            dve.tensor_tensor(four3(qk, t), bank3(t), over_tiles(incl[:, :], 4), ALU.mult).then_inc(sem("qk_ready"), 1)
        dve.wait_ge(sem("xm_started"), 1)
        for l in range(1, len(LEVELS) - 1):
            for t in range(NT):
                n = NT * (l - 1) + t
                if l < len(LEVELS) - 2:
                    dve.wait_ge(sem("w_done"), n + 1)
                    dve.tensor_tensor(four(xm, t), four(xm, t), bank[4 + t % 2], ALU.subtract).then_inc(sem("xm_ready"), 1)
                dve.wait_ge(sem("wT_done"), n + 1)
                dve.tensor_tensor(four(xmT, t), four(xmT, t), bank[6 + t % 2], ALU.subtract).then_inc(sem("xmT_ready"), 1)
            dve.wait_ge(sem("xm_ready"), NT * min(l, len(LEVELS) - 3))
            dve.wait_ge(sem("xmT_ready"), NT * l)
        for t in range(NT):
            dve.wait_ge(sem("r1_done"), t + 1)
            dve.tensor_copy(four(rbuf, t), bank[t]).then_inc(sem("r1_ready"), 1)
        dve.wait_ge(sem("r1_ready"), NT)
        for t in range(NT):
            dve.wait_ge(sem("r2_done"), t + 1)
            dve.tensor_tensor(four(rbuf, t), four(rbuf, t), bank[t], ALU.subtract).then_inc(sem("u_ready"), 1)
        for t in range(NT):
            dve.wait_ge(sem("o_done"), t + 1)
            link(dve.tensor_tensor(four3(ybuf, t), bank3(4 + t), factor(2, t), ALU.mult))
            dve.wait_ge(sem("ema_turned"), t + 1)
            link(dve.tensor_tensor(four3(tbuf, t), bank3(t), factor(3, t), ALU.mult))
            link(dve.tensor_tensor(four(ybuf, t), four(ybuf, t), four(tbuf, t), ALU.add))
        link(dve.tensor_tensor(tbuf[:, :, :], ybuf[:, :, :], ybuf[:, :, :], ALU.mult))
        link(dve.tensor_reduce(norms[:, 0, :], tbuf[:, :, :], AX.X, ALU.add))
        dve.tensor_scalar(norms[:, 0, :], norms[:, 0, :], 1.0 / P, EPS, ALU.mult, ALU.add).then_inc(sem("mean_square"), 1)
        dve.wait_ge(sem("rms_ready"), 1)
        link(dve.tensor_tensor(ybuf[:, :, :], ybuf[:, :, :], over_width(norms[:, 0, :], P), ALU.mult))
        dve.tensor_tensor(ybuf[:, :, :], ybuf[:, :, :], over_tiles(rmsw[:, :], NM), ALU.mult).then_inc(sem("mixed_ready"), 1)
        for c in (0, 1):
            dve.wait_ge(sem("turned"), 5)
            dve.tensor_copy(kf[:, c, :], bank[c]).then_inc(sem("turned_copied"), 1)
        for t in range(NT):
            dve.wait_ge(sem("wo_done"), t + 1)
            link(dve.tensor_tensor(xa[:, t, :], xa[:, t, :], bank[4 + t], ALU.add))

    def act_delta(act):
        copy_turned(act, act.copy, 3, (2, 3), xT)
        for i, g in enumerate((beta, gamma)):
            act.wait_ge(sem("gates_done"), i + 1)
            act.activation(g[:, :], bank[4 + i][0:GH, :], ACT.Tanh, scale=0.5).then_inc(sem("gate_tanh"), 1)
        act.wait_ge(sem("mix_conv"), 1)
        act.activation(trow[:, :], mixr[:, :], ACT.Tanh, scale=0.5).then_inc(sem("mix_tanh"), 1)
        act.wait_ge(sem("mix_silu"), 1)
        act.wait_ge(sem("hbias_ready"), 1)
        act.activation(trow[:, :], mixr[:, :], ACT.Tanh, scale=0.25, bias=hbias[:, :]).then_inc(sem("mix_tanh"), 1)

        def src(n):
            return feats[n // NC][:, n % NC, :]

        act.wait_ge(sem("delta_small_loaded"), 16 * 9)
        for n in range(NPROJ + 2):
            if n < NPROJ:
                act.wait_ge(sem("proj_done"), n + 1)
                act.activation(src(n), bank[n % 4], ACT.Copy, scale=conv[:, n // NC, n % NC, TAPS - 1:TAPS])\
                   .then_inc(sem("first_tap"), 1)
            if 1 <= n <= NPROJ:
                act.wait_ge(sem("conv_done"), n)
                act.activation(th[:, n - 1, :], src(n - 1), ACT.Tanh, scale=0.5).then_inc(sem("tanh_first"), 1)
            if 2 <= n < 2 * NC + 2:
                act.wait_ge(sem("silu_first"), n - 1)
                act.activation(th[:, n - 2, :], src(n - 2), ACT.Tanh, scale=0.25).then_inc(sem("tanh_second"), 1)
        for h in range(GH):
            act.wait_ge(sem("gamma_spread"), h + 1)
            act.wait_ge(sem("gamma_used_v"), h + 1)
            act.copy(four(tbuf, h), bank[h]).then_inc(sem("gamma_used_a"), 1)
        for t in range(NT):
            act.wait_ge(sem("transposed_n"), t + 1)
            act.copy(four(nT_all, t), bank[4 + t]).then_inc(sem("nT_ready"), 1)
        for l in range(1, len(LEVELS) - 1):
            for t in range(NT):
                act.wait_ge(sem("y_done"), NT * (l - 1) + t + 1)
                act.copy(four(ybuf, t), bank[t]).then_inc(sem("y_ready"), 1)
        for t in range(NT):
            act.wait_ge(sem("c_done"), t + 1)
            act.copy(four(ybuf, t), bank[4 + t]).then_inc(sem("c_ready"), 1)
        for c in (2, 3):
            act.wait_ge(sem("turned"), 5)
            act.copy(kf[:, c, :], bank[c]).then_inc(sem("turned_copied"), 1)

    def pe_delta(pe):
        pe.wait_ge(sem("n1_ready"), NT)
        pe_turn(pe, tmp, "n1_ready")
        pe.wait_ge(sem("turned_copied"), 16)
        pe.wait_ge(sem("delta_small_loaded"), 16 * 9)
        for i in range(3):
            for c in range(NC):
                k = pe.matmul(bank[4 + i][0:GH, :], wgates[:, c, GH * i:GH * (i + 1)], xT[:, c, :], start=c == 0, stop=c == NC - 1)
            k.then_inc(sem("gates_done"), 1)
        pe.wait_ge(sem("dw_loaded"), 48)
        for n in range(NPROJ):
            if n >= 4:
                pe.wait_ge(sem("conv_done"), n - 3)
            for c in range(NC):
                k = pe.matmul(bank[n % 4], dw[n // NC][:, c, (n % NC) * P:(n % NC + 1) * P], xT[:, c, :],
                              start=c == 0, stop=c == NC - 1)
            k.then_inc(sem("proj_done"), 1)
        pe.wait_ge(sem("gates_ready"), 3)
        pe.wait_ge(sem("masks_ready"), 1)
        pe.wait_ge(sem("conv_done"), NPROJ)
        for h in range(GH):
            pe.matmul(bank[h], sel[:, h, :], gamma[:, :], start=True, stop=True).then_inc(sem("gamma_spread"), 1)
        for i, g in enumerate((beta, mixr)):
            for t in range(NT):
                k = pe.transpose(bank[7][:, (i * NT + t) * GH:(i * NT + t + 1) * GH], g[:, t * P:(t + 1) * P],
                                 ident[0:GH, 0:GH])
        k.then_inc(sem("gates_turned"), 1)
        pe.wait_ge(sem("squares_ready"), 2)
        for i in range(2):
            for m in range(NM):
                k = pe.matmul(bank[6][:, i * NM + m:i * NM + m + 1],
                              th[:, 4 * i + m % GH, (m // GH) * P:(m // GH + 1) * P], ones[:, 0:1], start=True, stop=True)
        k.then_inc(sem("norms_done"), 1)

        def tile(f, m):
            return f[:, m % GH, (m // GH) * P:(m // GH + 1) * P]

        def each(b0, t, lhs, rhs, done):
            for m in range(4 * t, 4 * t + 4):
                k = pe.matmul(bank[b0][:, level_matrix(m)], lhs(m), rhs(m), start=True, stop=True)
            k.then_inc(sem(done), 1)

        def turn(b0, t, src, done):
            for m in range(4 * t, 4 * t + 4):
                k = pe.transpose(bank[b0][:, level_matrix(m)], src(m), ident[:, :])
            k.then_inc(sem(done), 1)

        pe.wait_ge(sem("feature_ready"), 2 * NC)
        pe.wait_ge(sem("values_ready"), NC)
        pe.wait_ge(sem("gtok_ready"), 1)
        pe.wait_ge(sem("norms_summed"), 1)
        for t in range(NT):
            turn(4 + t, t, lambda m: tile(vf, m), "v_turned")
        for t in range(NT):
            pe.wait_ge(sem("gamma_used_a"), NT)
            each(t, t, lambda m: tile(kf, m), lambda m: tile(kf, m), "gram_done")
        for t in range(NT):
            pe.wait_ge(sem("vtok_ready"), t + 1)
            pe.wait_ge(sem("n_ready"), t + 1)
            turn(4 + t, t, lambda m: nT_s[:, m, :], "transposed_n")
        for t in range(NT):
            each(t, t, lambda m: tile(kf, m), lambda m: tile(qf, m), "qk_done")
        pe.wait_ge(sem("xm_started"), 1)
        for t in range(NT):
            pe.wait_ge(sem("nT_ready"), t + 1)
        for l in range(1, len(LEVELS) - 1):
            for t in range(NT):
                if l == 1:
                    pe.wait_ge(sem("qk_ready"), t + 1)
                pe.wait_ge(sem("level_ready"), NT * (l - 1) + t + 1)
                if l > 1:
                    pe.wait_ge(sem("xm_ready"), NT * (l - 2) + t + 1)
                each(t, t, lambda m: nT_s[:, m, :], lambda m: xm[:, m, :], "y_done")
            for t in range(NT):
                pe.wait_ge(sem("y_ready"), NT * (l - 1) + t + 1)
                n = NT * (l - 1) + t
                if n >= 2:
                    pe.wait_ge(sem("xmT_ready"), n - 1)
                if l < len(LEVELS) - 2:
                    each(4 + t % 2, t, lambda m: xmT[:, m, :], lambda m: ybuf[:, m, :], "w_done")
                each(6 + t % 2, t, lambda m: ybuf[:, m, :], lambda m: xmT[:, m, :], "wT_done")
        for t in range(NT):
            pe.wait_ge(sem("xmT_ready"), NT * (len(LEVELS) - 3) + t + 1)
            each(t, t, lambda m: xmT[:, m, :], lambda m: vtok[:, m, :], "r1_done")
        for t in range(NT):
            pe.wait_ge(sem("r1_ready"), t + 1)
            pe.wait_ge(sem("level_ready"), NT * (len(LEVELS) - 2) + t + 1)
            if t == 0:
                pe.wait_ge(sem("xmT_ready"), NT * (len(LEVELS) - 2))
            each(4 + t, t, lambda m: nT_s[:, m, :], lambda m: rbuf[:, m, :], "c_done")
        for t in range(NT):
            pe.wait_ge(sem("c_ready"), t + 1)
            each(t, t, lambda m: xmT[:, m, :], lambda m: ybuf[:, m, :], "r2_done")
        for t in range(NT):
            pe.wait_ge(sem("u_ready"), t + 1)
            each(4 + t, t, lambda m: qk[:, m, :], lambda m: rbuf[:, m, :], "o_done")
        for t in range(NT):
            if t == 0:
                pe.wait_ge(sem("ema_ready"), GH)
            turn(t, t, lambda m: tile(ema, m), "ema_turned")
        pe.wait_ge(sem("mixed_ready"), 1)
        for t in range(NT):
            for c in range(NC):
                k = pe.transpose(bank[c][:, t * P:(t + 1) * P], ybuf[:, 4 * t + c, :], ident[:, :])
        k.then_inc(sem("turned"), 1)
        pe.wait_ge(sem("turned_copied"), 20)
        pe.wait_ge(sem("dwo_loaded"), 16)
        for t in range(NT):
            for c in range(NC):
                k = pe.matmul(bank[4 + t], kf[:, c, t * P:(t + 1) * P], dwo[:, c, :], start=c == 0, stop=c == NC - 1)
            k.then_inc(sem("wo_done"), 1)

    NS = 8
    NPIECE = 6
    HH = HID // 2
    NG2 = NH // 2
    PERIOD = 4
    place = [16384, 32768, 49152, 65536, 114688, 131072, 98304, 81920]
    w12 = [at(f"w12_{k}", R + place[k], [P, NC, HH]) for k in range(NS)]
    w3 = [at(f"w3_{k}", R + place[k], [P, NH // 2, D]) for k in range(NS)]
    n2T = at("n2T", R, [P, NC, TOK])
    wslots = at("wslots", R, [P, NT * NEXP, CAP])
    eout = at("eout", R + 10240, [P, D])
    yT = at("yT", R, [P, NC, TOK])
    n2 = at("n2", R + 147456, [P, NT, D])
    eth = at("eth", R + 147456, [P, 3, 2 * CAP])
    slots = at("slots", R + 155648, [P, NT * NEXP, CAP])
    scat = at("scat", R + 165888, [P, NEXP, TOK])
    disp = at("disp", R + 182272, [P, NC, NEXP * CAP])
    hT = at("hT", R + 192512, [P, NH, CAP])
    M0 = R + 197632
    upper = at("upper", M0, [P, P])
    iotac = at("iotac", M0 + 512, [P, CAP])
    iotae = at("iotae", M0 + 832, [P, NEXP])
    logit = at("logit", M0 + 864, [P, NT, NEXP])
    top = at("top", M0 + 992, [P, NT, 8])
    topi = at("topi", M0 + 1120, [P, NT, 8], U32)
    topf = at("topf", M0 + 1248, [P, NT, 8])
    first = at("first", M0 + 1376, [P, NT, NEXP])
    second = at("second", M0 + 1504, [P, NT, NEXP])
    chosen = at("chosen", M0 + 1632, [P, NT, NEXP])
    weight = at("weight", M0 + 1760, [P, NT, NEXP])
    pos = at("pos", M0 + 1888, [P, NT, NEXP])
    rw = at("rw", M0 + 2016, [P, 2, NT])
    wg = at("wg", 1728, [P, NC, NEXP])
    bg = at("bg", 1856, [P, NEXP])

    def sp_experts(sp):
        freed = {4: ("r1_done", NT), 5: ("o_done", NT), 6: ("ema_turned", NT), 7: ("wo_done", NT)}
        for n in range(NPIECE * NEXP):
            e, j, k = n // NPIECE, n % NPIECE, n % NS
            if n == 0:
                sp.wait_ge(sem("ffn_done"), NT)
            elif n in freed:
                sp.wait_ge(sem(freed[n][0]), freed[n][1])
            elif n >= NS:
                sp.wait_ge(sem("pieces_used"), n - NS + 1)
            if j < 4:
                src = a["ew1" if j % 2 == 0 else "ew2"][e, :, (j // 2) * HH:(j // 2 + 1) * HH]
                sp.dma_start(w12[k][:, :, :], src.rearrange("(c p) n -> p c n", p=P)).then_inc(sem(f"piece_loaded{k}"), 16)
            else:
                src = a["ew3"][e, (j - 4) * HH:(j - 3) * HH, :]
                sp.dma_start(w3[k][:, :, :], src.rearrange("(c p) n -> p c n", p=P)).then_inc(sem(f"piece_loaded{k}"), 16)

    def pool_experts(pool, link):
        pool.wait_ge(sem("turned"), 5)
        link(pool.memset(upper[:, :], 1.0))
        link(pool.affine_select(out=upper[:, :], in_=upper[:, :], compare_op=ALU.is_ge, fill=0.0, base=0,
                                pattern=[[1, P]], channel_multiplier=-1))
        link(pool.iota(topi[:, :, :].rearrange("p t k -> p (t k)")[:, 0:NEXP], pattern=[[1, NEXP]], base=0, channel_multiplier=0))
        link(pool.tensor_copy(iotae[:, :], topi[:, :, :].rearrange("p t k -> p (t k)")[:, 0:NEXP]))
        link(pool.iota(hT[:, 0, :].bitcast(U32), pattern=[[1, CAP]], base=0, channel_multiplier=0))
        pool.tensor_copy(iotac[:, :], hT[:, 0, :].bitcast(U32)).then_inc(sem("iotas_ready"), 1)
        norm_rstd(pool, link, 5)
        pool.memset(scat[:, :, :], 0.0).then_inc(sem("scat_zeroed"), 1)
        pool.wait_ge(sem("scat_turned"), NEXP)
        pool.memset(eout[:, :], 0.0).then_inc(sem("zeros_ready"), 1)

    def dve_experts(dve, link):
        norm_stats(dve, link, xa)
        for t in range(NT):
            norm_apply(dve, 5, n2, xa, t).then_inc(sem("n2_ready"), 1)
        copy_turned(dve, dve.tensor_copy, 5, (0, 1), n2T)
        dve.wait_ge(sem("delta_small_loaded"), 16 * 9)
        dve.wait_ge(sem("router_product"), 1)
        link(dve.tensor_tensor(logit[:, :, :], bank[4][:, 0:NT * NEXP].rearrange("p (t e) -> p t e", t=NT),
                               over_tiles(bg[:, :]), ALU.add))
        dve.wait_ge(sem("iotas_ready"), 1)
        for t in range(NT):
            link(dve.max(top[:, t, :], logit[:, t, :]))
            link(dve.max_index(topi[:, t, :], top[:, t, :], logit[:, t, :]))
        dve.tensor_tensor(rw[:, 1, :], top[:, :, 1], top[:, :, 0], ALU.subtract).then_inc(sem("margin_ready"), 1)
        link(dve.tensor_copy(topf[:, :, :], topi[:, :, :]))
        link(dve.tensor_tensor(first[:, :, :], over_tiles(iotae[:, :]), over_width(topf[:, :, 0], NEXP), ALU.is_equal))
        link(dve.tensor_tensor(second[:, :, :], over_tiles(iotae[:, :]), over_width(topf[:, :, 1], NEXP), ALU.is_equal))
        dve.tensor_tensor(chosen[:, :, :], first[:, :, :], second[:, :, :], ALU.add).then_inc(sem("chosen_ready"), 1)
        dve.wait_ge(sem("margin_exp"), 1)
        link(dve.tensor_scalar(rw[:, 0, :], rw[:, 1, :], 1.0, None, ALU.add))
        link(dve.reciprocal(rw[:, 0, :], rw[:, 0, :]))
        link(dve.tensor_tensor(rw[:, 1, :], rw[:, 1, :], rw[:, 0, :], ALU.mult))
        link(dve.tensor_tensor(first[:, :, :], first[:, :, :], over_width(rw[:, 0, :], NEXP), ALU.mult))
        link(dve.tensor_tensor(second[:, :, :], second[:, :, :], over_width(rw[:, 1, :], NEXP), ALU.mult))
        link(dve.tensor_tensor(weight[:, :, :], first[:, :, :], second[:, :, :], ALU.add))
        link(dve.tensor_scalar(weight[:, :, :], weight[:, :, :], 0.5, None, ALU.mult))
        dve.wait_ge(sem("router_product"), 2)
        link(dve.tensor_tensor(pos[:, :, :].rearrange("p t e -> p (t e)"), bank[5][:, 0:NT * NEXP],
                               chosen[:, :, :].rearrange("p t e -> p (t e)"), ALU.mult))
        link(dve.tensor_scalar(pos[:, :, :], pos[:, :, :], -1.0, None, ALU.add))
        dve.tensor_tensor(slots[:, :, :], over_tiles(iotac[:, :], NT * NEXP),
                          over_width(pos[:, :, :].rearrange("p t e -> p (t e)"), CAP), ALU.is_equal).then_inc(sem("slots_ready"), 1)
        dve.wait_ge(sem("slots_ready"), 1)
        dve.tensor_tensor(wslots[:, :, :], slots[:, :, :], over_width(weight[:, :, :].rearrange("p t e -> p (t e)"), CAP),
                          ALU.mult).then_inc(sem("wslots_ready"), 1)
        half = NEXP * CAP // 2
        for c in range(NC):
            dve.wait_ge(sem("gathered"), c + 1)
            dve.tensor_copy(disp[:, c, 0:half], bank[c][:, 0:half]).then_inc(sem("disp_ready_v"), 1)
        dve.wait_ge(sem("scat_zeroed"), 1)
        for e in range(0, NEXP, 2):
            dve.wait_ge(sem("scat_turned"), e + 1)
            dve.tensor_copy(scat[0:CAP, e, :], bank[e][0:CAP, :]).then_inc(sem("scat_ready_v"), 1)
        dve.wait_ge(sem("zeros_ready"), 1)
        dve.memset(stat[:, :, :], 0.0).then_inc(sem("hidden_ready"), NG2)

    def pe_experts(pe):
        pe.wait_ge(sem("n2_ready"), NT)
        pe_turn(pe, n2, "n2_ready")
        pe.wait_ge(sem("turned_copied"), 24)
        for t in range(NT):
            for c in range(NC):
                k = pe.matmul(bank[4][:, t * NEXP:(t + 1) * NEXP], n2T[:, c, t * P:(t + 1) * P], wg[:, c, :],
                              start=c == 0, stop=c == NC - 1)
        k.then_inc(sem("router_product"), 1)
        pe.wait_ge(sem("chosen_ready"), 1)
        for t in range(NT):
            for s in range(t + 1):
                k = pe.matmul(bank[5][:, t * NEXP:(t + 1) * NEXP], upper[:, :] if s == t else ones[:, :], chosen[:, s, :],
                              start=s == 0, stop=s == t)
        k.then_inc(sem("router_product"), 1)
        pe.wait_ge(sem("slots_ready"), 1)
        half = NEXP // 2
        for c in range(NC):
            for h in range(2):
                for t in range(NT):
                    k = pe.matmul(bank[c + 4 * h][:, 0:half * CAP], n2[:, t, c * P:(c + 1) * P],
                                  slots[:, t * NEXP + h * half:t * NEXP + (h + 1) * half, :].rearrange("p e s -> p (e s)"),
                                  start=t == 0, stop=t == NT - 1)
            k.then_inc(sem("gathered"), 1)
        pe.wait_ge(sem("wslots_ready"), 1)
        for e in range(NEXP):
            pe.wait_ge(sem("disp_ready_v" if e < 4 else "disp_ready_a"), e % 4 + 1)
            for t in range(NT):
                k = pe.transpose(bank[e][0:CAP, t * P:(t + 1) * P], wslots[:, t * NEXP + e, :], ident[:, :])
            k.then_inc(sem("scat_turned"), 1)
        pe.wait_ge(sem("scat_ready_v"), NEXP // 2)
        pe.wait_ge(sem("scat_ready_a"), NEXP // 2)
        pe.wait_ge(sem("disp_ready_v"), NC)
        pe.wait_ge(sem("disp_ready_a"), NC)
        for c in range(NC):
            for t in range(NT):
                pe.matmul(bank[c][:, t * P:(t + 1) * P], xa[:, t, c * P:(c + 1) * P], ident[:, :], start=t == 0, stop=False,
                          skip_group_check=True)

        def hidden(e0, i, g):
            e = e0 + PERIOD * i
            pe.wait_ge(sem("hidden_ready"), NG2 * e + g + (7 if g < 2 else 6))
            half = g // (NG2 // 2)
            places = [(NPIECE * e0 + 2 * half + w) % NS for w in (0, 1)]
            if g % (NG2 // 2) == 0:
                for w in (0, 1):
                    pe.wait_ge(sem(f"piece_loaded{places[w]}"), 16 * (3 * i + (NPIECE * e0 + 2 * half + w) // NS + 1))
            for w in (0, 1):
                for m in (0, 1):
                    f = ((2 * g + m) * P) % HH
                    for c in range(NC):
                        k = pe.matmul(bank[4 + g % 3][:, (2 * w + m) * CAP:(2 * w + m + 1) * CAP], w12[places[w]][:, c, f:f + P],
                                      disp[:, c, bass.ds(e * CAP, CAP)], start=c == 0, stop=c == NC - 1)
            k.then_inc(sem("hidden_done"), 1)

        def down(e0, i):
            e = e0 + PERIOD * i
            pe.wait_ge(sem("hidden_ready"), NG2 * (e + 2))
            pe.wait_ge(sem("eout_ready"), e + 1)
            for f in range(NH):
                n = NPIECE * e0 + 4 + f // (NH // 2)
                if f % (NH // 2) == 0:
                    pe.wait_ge(sem(f"piece_loaded{n % NS}"), 16 * (3 * i + n // NS + 1))
                k = pe.matmul(bank[7][0:CAP, :], hT[:, f, :], w3[n % NS][:, f % (NH // 2), :], start=f == 0, stop=f == NH - 1)
                if f == NH // 2 - 1:
                    k.then_inc(sem("pieces_used"), 5)
                if f == NH - 1:
                    k.then_inc(sem("down_done"), 1)

        def scatter(e0, i):
            e = e0 + PERIOD * i
            pe.wait_ge(sem("eout_ready"), e + 2)
            for c in range(NC):
                k = pe.matmul(bank[c], eout[:, c * P:(c + 1) * P], scat[:, bass.ds(e, 1), :].rearrange("p e t -> p (e t)"),
                              start=False, stop=False, skip_group_check=True)
            k.then_inc(sem("pieces_used"), 1)

        with pe.Fori(0, NEXP // PERIOD) as i:
            for e0 in range(PERIOD):
                for g in range(NG2):
                    hidden(e0, i, g)
                down(e0, i)
                scatter(e0, i)
        pe.wait_ge(sem("yT_ready"), 4)
        for t in range(NT):
            for c in range(NC):
                k = pe.transpose(bank[4 + t % 4][:, c * P:(c + 1) * P], yT[:, c, t * P:(t + 1) * P], ident[:, :])
            k.then_inc(sem("y_turned"), 1)

    def act_experts(act):
        copy_turned(act, act.copy, 5, (2, 3), n2T)
        act.wait_ge(sem("margin_ready"), 1)
        act.activation(rw[:, 1, :], rw[:, 1, :], ACT.Exp).then_inc(sem("margin_exp"), 1)
        half = NEXP * CAP // 2
        for c in range(NC):
            act.wait_ge(sem("gathered"), c + 1)
            act.copy(disp[:, c, half:2 * half], bank[4 + c][:, 0:half]).then_inc(sem("disp_ready_a"), 1)
        act.wait_ge(sem("scat_zeroed"), 1)
        for e in range(1, NEXP, 2):
            act.wait_ge(sem("scat_turned"), e + 1)
            act.copy(scat[0:CAP, e, :], bank[e][0:CAP, :]).then_inc(sem("scat_ready_a"), 1)
        act.wait_ge(sem("zeros_ready"), 1)
        act.copy(rstd[:, :], rstd[:, :]).then_inc(sem("eout_ready"), 1)
        with act.Fori(0, NEXP // PERIOD) as i:
            for e0 in range(PERIOD):
                e = e0 + PERIOD * i
                for g in range(NG2):
                    act.wait_ge(sem("hidden_done"), NG2 * e + g + 1)
                    act.activation(eth[:, g % 3, :], bank[4 + g % 3][:, 0:2 * CAP], ACT.Tanh, scale=0.5)\
                       .then_inc(sem("hidden_tanh"), 1)
                act.wait_ge(sem("down_done"), e + 1)
                act.copy(eout[0:CAP, :], bank[7][0:CAP, :]).then_inc(sem("eout_ready"), 1)
        act.wait_ge(sem("pieces_used"), NPIECE * NEXP)
        for c in (2, 3):
            act.copy(yT[:, c, :], bank[c]).then_inc(sem("yT_ready"), 1)

    def dve_experts_loop(dve):
        with dve.Fori(0, NEXP // PERIOD) as i:
            for e0 in range(PERIOD):
                e = e0 + PERIOD * i
                for g in range(NG2):
                    n = NG2 * e + g
                    dve.wait_ge(sem("hidden_tanh"), n + 1)
                    dve.scalar_tensor_tensor(eth[:, g % 3, :], eth[:, g % 3, :], 1.0, bank[4 + g % 3][:, 0:2 * CAP],
                                             ALU.add, ALU.mult).then_inc(sem("gate_ready"), 1)
                    dve.wait_ge(sem("gate_ready"), n + 1)
                    dve.tensor_tensor(hT[:, 2 * g:2 * g + 2, :].rearrange("p f s -> p (f s)"), eth[:, g % 3, :],
                                      bank[4 + g % 3][:, 2 * CAP:4 * CAP], ALU.mult).then_inc(sem("hidden_ready"), 1)
        dve.wait_ge(sem("pieces_used"), NPIECE * NEXP)
        for c in (0, 1):
            dve.tensor_copy(yT[:, c, :], bank[c]).then_inc(sem("yT_ready"), 1)
        for t in range(NT):
            dve.wait_ge(sem("y_turned"), t + 1)
            dve.tensor_copy(xa[:, t, :], bank[4 + t % 4]).then_inc(sem("result_ready"), 1)

    @block.sync
    def _(sp):
        sp_self(sp)
        batches(sp, sp_cross)
        sp_ffn(sp)
        sp_delta(sp)
        sp_experts(sp)
        for t in range(NT):
            sp.wait_ge(sem("result_ready"), t + 1)
            sp.dma_start(out_dram[:, t, :], xa[:, t, :]).then_inc(sem("out_written"), 16)
        sp.wait_ge(sem("out_written"), 16 * NT)

    @block.gpsimd
    def _(pool):
        link = Chain(pool, "pool_chain")
        pool_self(pool, link)
        pool.wait_ge(sem("o1_done"), B)
        pool.memset(qb_h[:, :, :].bitcast(U32), 0)
        pool.memset(qb_l[:, :, :].bitcast(U32), 0).then_inc(sem("queries_zeroed"), 1)
        norm_rstd(pool, link, 2)
        pool_masks(pool, link)
        norm_rstd(pool, link, 3)
        pool_delta(pool, link)
        pool_experts(pool, link)

    @block.vector
    def _(dve):
        link = Chain(dve, "dve_chain")
        dve_self(dve, link)
        batches(dve, dve_cross, last=True)
        dve_ffn(dve, link)
        dve_delta(dve, link)
        dve_experts(dve, link)
        dve_experts_loop(dve)

    @block.scalar
    def _(act):
        act_self(act)
        batches(act, act_cross, last=True)
        act_ffn(act)
        act_delta(act)
        act_experts(act)

    @block.tensor
    def _(pe):
        pe_self(pe)
        batches(pe, pe_cross)
        pe_ffn(pe)
        pe_delta(pe)
        pe_experts(pe)


def kernel(**inputs):
    from concourse.bacc import Bacc
    from concourse.bass_utils import run_bass_kernel_spmd

    def get(name):
        return np.asarray(inputs[name])

    arrays = {"x": get("x"), "ctxT": get("ctx_1024").transpose(0, 2, 1)}
    for name in ("Wq1", "Wk1", "Wv1", "Wq2", "Wk2", "Wv2"):
        arrays[name.lower()] = get("L0_xattn_" + name).transpose(1, 0, 2).reshape(D, D)
    for name in ("bv1", "bv2", "g1", "be1", "g2", "be2", "g3", "be3", "bf2"):
        arrays[name] = get("L0_xattn_" + name).reshape(-1)
    for name in ("Wf1", "Wf2"):
        arrays[name.lower()] = get("L0_xattn_" + name)
    arrays["bf1"] = get("L0_xattn_bf1").reshape(NH, P).T
    for name in ("Wq", "Wk", "Wv", "Wo"):
        arrays["d" + name.lower()] = get("L0_attn_" + name)
    for name in ("conv_q", "conv_k", "conv_v"):
        arrays[name] = get("L0_attn_" + name).reshape(NC, P, TAPS).transpose(1, 0, 2)
    arrays["wgates"] = np.concatenate([get("L0_attn_" + n) for n in ("Wb", "Wdec", "Wmix")], axis=1)
    arrays["conv_mix"] = get("L0_attn_conv_mix")
    arrays["mix_bias"] = get("L0_attn_mix_bias").reshape(GH, 1)
    arrays["rms_w"] = get("L0_attn_rms_w")
    arrays["wg"] = get("L0_ffn_Wg")
    arrays["bg"] = get("L0_ffn_bg")
    for name in ("W1", "W2", "W3"):
        arrays["e" + name.lower()] = get("L0_ffn_" + name)
    arrays = {f"in_{k}": np.ascontiguousarray(v) for k, v in arrays.items()}

    nc = Bacc("TRN2", target_bir_lowering=False, num_devices=1)
    a = {k[3:]: nc.dram_tensor(k, v.shape, F32, kind="ExternalInput").ap() for k, v in arrays.items()}
    out = nc.dram_tensor("out", (B, S, D), F32, kind="ExternalOutput").ap()
    build(nc, a, out)
    result = run_bass_kernel_spmd(nc, [arrays], core_ids=[0])
    return result.results[0]["out"]
```

```python
from contextlib import ExitStack

import numpy as np

import concourse.bass as bass
import concourse.mybir as mybir

F32 = mybir.dt.float32
F32R = mybir.dt.float32r
U32 = mybir.dt.uint32
ALU = mybir.AluOpType
ACT = mybir.ActivationFunctionType
AX = mybir.AxisListType

P = 128
B, S, D = 8, 64, 512
TOK = B * S
NT = TOK // P
NC = D // P
H, E = 16, 32
NP = H // 2
SCALE = float(E) ** -0.5
CTX = 1601
CW = CTX + 1
G = 256
NG = -(-CTX // G)
CT = -(-CTX // P)
LAST = CTX - (CT - 1) * P
EPS = 1e-5
MASKED = -3.0e38

HID = 2048
NH = HID // P
GH = 4
NEXP = 8
CAP = int(TOK / NEXP * 1.25)
TAPS = 4


def build(nc, a, out):
    ctx = ExitStack()
    sems = {}

    def sem(name):
        if name not in sems:
            sems[name] = ctx.enter_context(nc.semaphore(name))
        return sems[name]

    base = 16512

    def at(name, offset, shape, dt=F32):
        return nc.alloc_sbuf_tensor_at(name, shape, dt, offset=base + offset)

    sc = ctx.enter_context(nc.psum_tensor("sc", [P, 4, 512], F32))
    ring = [ctx.enter_context(nc.psum_tensor(f"ring{i}", [P, 512], F32)) for i in range(3)]
    pv = ctx.enter_context(nc.psum_tensor("pv", [P, 512], F32))
    bank = [sc[:, 0, :], sc[:, 1, :], sc[:, 2, :], sc[:, 3, :], ring[0][:, :], ring[1][:, :], ring[2][:, :], pv[:, :]]

    ident = at("ident", 0, [P, P])
    ones = at("ones", 512, [P, P])
    stat = at("stat", 1024, [P, NT, 6])
    mv = at("mv", 1152, [P, NT, 2])
    rstd = at("rstd", 1216, [P, NT])
    mhalf = at("mhalf", 1248, [P, 64])
    nmax = at("nmax", 1536, [P, 2, NP])
    esum = at("esum", 1600, [P, 2, NP])
    rinv = at("rinv", 1664, [P, 2, NP])
    hmax = at("hmax", 1888, [P, 2])
    esum_b = at("esum_b", 1920, [P, 2, NP])
    cat = at("cat", 2048, [P, D])
    xa = at("xa", 4096, [P, NT, D])
    R = 12288

    qT = at("qT", R, [P, NC, TOK])
    qb_h = at("qb_h", R + 8192, [P, NP, P], F32R)
    qb_l = at("qb_l", R + 12288, [P, NP, P], F32R)
    wk_h = at("wk_h", R + 16384, [P, NC, D], F32R)
    wk_l = at("wk_l", R + 24576, [P, NC, D], F32R)
    wv_h = at("wv_h", R + 32768, [P, NC, D], F32R)
    wv_l = at("wv_l", R + 40960, [P, NC, D], F32R)
    raw = at("raw", R + 49152, [P, 2, NC, G])
    x_h = at("x_h", R + 57344, [P, 2, NC, G], F32R)
    x_l = at("x_l", R + 65536, [P, 2, NC, G], F32R)
    K0 = R + 73728
    kT = at("kT", K0, [P, NP, CW], F32R)
    V0 = K0 + 51264
    v = at("v", V0, [P, 2, CT, D], F32R)
    pT_h = at("pT_h", V0 + 53248, [P, CT, P], F32R)
    pT_l = at("pT_l", V0 + 59904, [P, CT, P], F32R)
    prob = at("prob", V0 + 66560, [P, CW])
    bv2 = at("bv2", V0 + 72992, [P, D])
    half_out = at("half_out", V0 + 75040, [P, NP // 2, E])

    xin = at("xin", K0, [P, NT, D])
    nT = at("nT", K0 + 8192, [P, NC, TOK])
    w_in = [at(f"w_in{i}", K0 + 16384 + 8192 * i, [P, NC, D]) for i in range(3)]
    kT1 = at("kT1", K0 + 40960, [P, NC, TOK])
    v1 = at("v1", K0 + 49152, [P, NT, D])
    s1 = at("s1", K0 + 57344, [P, 2, 512])
    p1 = at("p1", K0 + 61440, [P, 2, 512])
    pT1 = at("pT1", K0 + 65536, [P, 1024])
    mask = at("mask", K0 + 69632, [P, S])
    bv1 = at("bv1", K0 + 69888, [P, D])
    g1 = at("g1", K0 + 71936, [P, D])
    be1 = at("be1", K0 + 73984, [P, D])
    wq2 = at("wq2", K0 + 76032, [P, NC, D])
    wk2 = at("wk2", K0 + 84224, [P, NC, D])
    wv2 = at("wv2", K0 + 92416, [P, NC, D])
    sa = at("sa", K0 + 100608, [P, NT, D])
    qb1 = at("qb1", R + 8192, [P, B, NP, P])

    x_dram = a["x"].rearrange("b s d -> (b s) d").rearrange("(t p) d -> p t d", p=P)
    out_dram = out.rearrange("b s d -> (b s) d").rearrange("(t p) d -> p t d", p=P)

    def w_dram(name):
        return a[name].rearrange("(c p) n -> p c n", p=P)

    def row_dram(name):
        return a[name].partition_broadcast(P)

    block = ctx.enter_context(nc.Block())

    class Chain:

        def __init__(self, eng, name):
            self.eng, self.sem, self.n = eng, sem(name), 0

        def __call__(self, instruction):
            self.n += 1
            instruction.then_inc(self.sem, 1)
            self.eng.wait_ge(self.sem, self.n)

    def over_tiles(v, n=NT):
        return v.unsqueeze(1).to_broadcast([v.shape[0], n, v.shape[1]])

    def over_width(v, w):
        return v.unsqueeze(2).to_broadcast([v.shape[0], v.shape[1], w])

    def norm_count(n, t):
        return NT * n + t + 1

    def norm_stats(dve, link, src, t):
        link(dve.bn_stats(stat[:, t, :], src[:, t, :]))
        dve.bn_aggr(mv[:, t, :], stat[:, t, :]).then_inc(sem("variance_ready"), 1)

    def norm_rstd(pool, link, n, t):
        pool.wait_ge(sem("variance_ready"), norm_count(n, t))
        link(pool.tensor_scalar(rstd[:, t:t + 1], mv[:, t, 1:2], EPS, None, ALU.add))
        pool.tensor_tensor(rstd[:, t:t + 1], rstd[:, t:t + 1], mhalf[:, 0:1], ALU.pow).then_inc(sem("rstd_ready"), 1)

    def norm_apply(dve, n, dst, src, t):
        dve.wait_ge(sem("rstd_ready"), norm_count(n, t))
        return dve.tensor_scalar(dst[:, t, :], src[:, t, :], mv[:, t, 0:1], rstd[:, t:t + 1], ALU.subtract, ALU.mult)

    def norm_center(dve, src, t, gain):
        return dve.scalar_tensor_tensor(src[:, t, :], src[:, t, :], mv[:, t, 0:1], gain, ALU.subtract, ALU.mult)

    def norm_shift(dve, n, dst, src, t, shift):
        dve.wait_ge(sem("rstd_ready"), norm_count(n, t))
        return dve.scalar_tensor_tensor(dst[:, t, :], src[:, t, :], rstd[:, t:t + 1], shift, ALU.mult, ALU.add)

    def norm_affine(dve, link, n, dst, src, t, gain, shift):
        dve.wait_ge(sem("variance_ready"), norm_count(n, t))
        link(norm_center(dve, src, t, gain))
        return norm_shift(dve, n, dst, src, t, shift)

    def sp_self(sp):
        sp.dma_start(xin[:, :, :], x_dram).then_inc(sem("x_loaded"), 16)
        for i, name in enumerate(("wq1", "wk1", "wv1")):
            sp.dma_start(w_in[i][:, :, :], w_dram(name)).then_inc(sem(f"{name}_loaded"), 16)
        for dst, name in ((bv1, "bv1"), (g1, "g1"), (be1, "be1")):
            sp.dma_start(dst[:, :], row_dram(name)).then_inc(sem("self_rows_loaded"), 16)
        sp.dma_start(bv2[:, :], row_dram("bv2")).then_inc(sem("self_rows_loaded"), 16)
        for dst, name in ((wq2, "wq2"), (wk2, "wk2"), (wv2, "wv2")):
            sp.dma_start(dst[:, :, :], w_dram(name)).then_inc(sem("w2_loaded"), 16)

    def pool_self(pool, link):
        link(pool.memset(ident[:, :], 0.0))
        pool.affine_select(out=ident[:, :], in_=ident[:, :], compare_op=ALU.not_equal, fill=1.0, base=0,
                           pattern=[[-1, P]], channel_multiplier=1).then_inc(sem("ident_ready"), 1)
        link(pool.memset(mhalf[:, :], -0.5))
        for t in range(NT):
            norm_rstd(pool, link, 0, t)
        link(pool.memset(mask[:, :], 0.0))
        for i, half in enumerate((slice(0, S), slice(S, P))):
            pool.affine_select(out=mask[half, :], in_=mask[half, :], compare_op=ALU.is_ge, fill=MASKED, base=0,
                               pattern=[[-1, S]], channel_multiplier=1).then_inc(sem("mask_ready"), 1)
            pool.wait_ge(sem("mask_ready"), i + 1)
        pool.memset(ones[:, :], 1.0).then_inc(sem("ones_ready"), 1)
        for t in range(NT):
            norm_rstd(pool, link, 1, t)

    def dve_self(dve, link):
        dve.memset(qb1[:, 0:B // 2, :, :], 0.0).then_inc(sem("qb1_zeroed"), 1)
        dve.wait_ge(sem("x_loaded"), 16)
        for t in range(NT):
            norm_stats(dve, link, xin, t)
        for t in range(NT):
            norm_apply(dve, 0, xa, xin, t).then_inc(sem("n0_ready"), 1)
        for c in (0, 1):
            dve.wait_ge(sem("turned"), 1)
            dve.tensor_copy(nT[:, c, :], bank[c]).then_inc(sem("turned_copied"), 1)
        dve.memset(qb1[:, B // 2:B, :, :], 0.0).then_inc(sem("qb1_zeroed"), 1)
        dve.wait_ge(sem("qb1_zeroed"), 2)
        for c in range(NC):
            dve.wait_ge(sem("self_proj_done"), c + 1)
            for g in (0, 1):
                dve.tensor_scalar(qb1[32 * g:32 * g + 32, :, 2 * c + g // 2, (g % 2) * S:(g % 2) * S + S],
                                  bank[c][32 * g:32 * g + 32, :].rearrange("p (b s) -> p b s", b=B),
                                  SCALE, None, ALU.mult).then_inc(sem("qb1_filled_v"), 1)
        for c in (0, 1):
            dve.wait_ge(sem("self_proj_done"), NC + c + 1)
            dve.tensor_copy(kT1[:, c, :], bank[4 + c]).then_inc(sem("self_kv_copied"), 1)
        for t in (0, 1):
            dve.wait_ge(sem("self_proj_done"), 2 * NC + t + 1)
            dve.tensor_copy(v1[:, t, :], bank[t]).then_inc(sem("self_kv_copied"), 1)

        def score_rows(b):
            return s1[:, b % 2, :].rearrange("p (h t) -> p h t", h=NP)

        def maxima(b):
            k, rows = b % 2, score_rows(b)
            dve.wait_ge(sem("s1_done"), b + 1)
            if b >= 2:
                dve.wait_ge(sem("p1_ready"), b - 1)
            link(dve.tensor_tensor(rows, bank[k].rearrange("p (h t) -> p h t", h=NP), over_tiles(mask[:, :], NP), ALU.add))
            link(dve.tensor_reduce(nmax[:, k, :], rows, AX.X, ALU.max, negate=True))

        def take_maxima(b):
            dve.tensor_tensor(score_rows(b), score_rows(b), over_width(nmax[:, b % 2, :], S), ALU.add)\
               .then_inc(sem("s1_ready"), 1)

        def copy_turned_probs(b):
            r = slice((b % 2) * S, (b % 2) * S + S)
            dve.wait_ge(sem("pT1_done"), b + 1)
            dve.tensor_copy(pT1[r, 0:512], bank[2 + 2 * (b % 2)][0:S, :]).then_inc(sem("pT1_copied_v"), 1)

        def rest(b):
            k, r = b % 2, slice((b % 2) * S, (b % 2) * S + S)
            dve.wait_ge(sem("p1_ready"), b + 1)
            link(dve.tensor_reduce(esum[:, k, :], p1[:, k, :].rearrange("p (h t) -> p h t", h=NP), AX.X, ALU.add))
            link(dve.reciprocal(rinv[:, k, :], esum[:, k, :]))
            dve.wait_ge(sem("o1_done"), b + 1)
            for odd in (0, 1):
                q = slice(odd * S, odd * S + S)
                dve.tensor_tensor(sa[r, b // 2, :].rearrange("p (n h e) -> p n h e", n=NP, h=2)[:, :, odd, :],
                                  bank[6 + k][q, :].rearrange("p (n h e) -> p n h e", n=NP, h=2)[:, :, odd, :],
                                  over_width(rinv[q, k, :], E), ALU.mult).then_inc(sem("sa_written"), 1)

        dve.wait_ge(sem("mask_ready"), 2)
        maxima(0)
        take_maxima(0)
        for b in range(B):
            if b + 1 < B:
                maxima(b + 1)
            copy_turned_probs(b)
            if b + 1 < B:
                take_maxima(b + 1)
            rest(b)
            if b % 2:
                t = b // 2
                dve.wait_ge(sem("sa_written"), 2 * (b + 1))
                if t == 0:
                    dve.wait_ge(sem("self_rows_loaded"), 64)
                    dve.wait_ge(sem("n0_ready"), NT)
                link(dve.tensor_tensor(sa[:, t, :], sa[:, t, :], bv1[:, :], ALU.add))
                link(dve.tensor_tensor(sa[:, t, :], sa[:, t, :], xa[:, t, :], ALU.add))
                norm_stats(dve, link, sa, t)
                norm_affine(dve, link, 1, xa, sa, t, g1[:, :], be1[:, :]).then_inc(sem("xa_ready"), 1)
        for c in (0, 1):
            dve.wait_ge(sem("turned"), 2)
            dve.tensor_copy(nT[:, c, :], bank[c]).then_inc(sem("turned_copied"), 1)
        dve.wait_ge(sem("w2_high"), 1)
        dve.tensor_tensor(wk_l[:, :, :], wk2[:, :, :], wk_h[:, :, :].bitcast(F32), ALU.subtract).then_inc(sem("w2_low"), 1)
        dve.wait_ge(sem("w2_high"), 2)
        dve.tensor_tensor(wv_l[:, :, :], wv2[:, :, :], wv_h[:, :, :].bitcast(F32), ALU.subtract).then_inc(sem("w2_low"), 1)

    def act_self(act):
        for c in (2, 3):
            act.wait_ge(sem("turned"), 1)
            act.copy(nT[:, c, :], bank[c]).then_inc(sem("turned_copied"), 1)
        act.wait_ge(sem("qb1_zeroed"), 2)
        for c in range(NC):
            act.wait_ge(sem("self_proj_done"), c + 1)
            for g in (2, 3):
                act.mul(qb1[32 * g:32 * g + 32, :, 2 * c + g // 2, (g % 2) * S:(g % 2) * S + S],
                        bank[c][32 * g:32 * g + 32, :].rearrange("p (b s) -> p b s", b=B),
                        SCALE).then_inc(sem("qb1_filled_a"), 1)
        for c in (2, 3):
            act.wait_ge(sem("self_proj_done"), NC + c + 1)
            act.copy(kT1[:, c, :], bank[4 + c]).then_inc(sem("self_kv_copied"), 1)
        for t in (2, 3):
            act.wait_ge(sem("self_proj_done"), 2 * NC + t + 1)
            act.copy(v1[:, t, :], bank[t]).then_inc(sem("self_kv_copied"), 1)
        for b in range(B + 1):
            if b >= 1:
                r = slice(((b - 1) % 2) * S, ((b - 1) % 2) * S + S)
                act.wait_ge(sem("pT1_done"), b)
                act.copy(pT1[r, 512:1024], bank[3 + 2 * ((b - 1) % 2)][0:S, :]).then_inc(sem("pT1_copied_a"), 1)
            if b < B:
                k = b % 2
                act.wait_ge(sem("s1_ready"), b + 1)
                if b >= 2:
                    act.wait_ge(sem("pT1_done"), b - 1)
                    act.wait_ge(sem("sa_written"), 2 * (b - 1))
                act.activation(p1[:, k, :], s1[:, k, :], ACT.Exp).then_inc(sem("p1_ready"), 1)
        for c in (2, 3):
            act.wait_ge(sem("turned"), 2)
            act.copy(nT[:, c, :], bank[c]).then_inc(sem("turned_copied"), 1)
        act.wait_ge(sem("o1_done"), B)
        act.wait_ge(sem("w2_loaded"), 48)
        act.copy(wk_h[:, :, :], wk2[:, :, :]).then_inc(sem("w2_high"), 1)
        act.wait_ge(sem("w2_loaded"), 48)
        act.copy(wv_h[:, :, :], wv2[:, :, :]).then_inc(sem("w2_high"), 1)
        for c in range(NC):
            act.wait_ge(sem("self_proj_done"), 2 * NC + NT + c + 1)
            act.mul(qT[:, c, :], bank[4 + c], SCALE).then_inc(sem("qT_ready"), 1)

    def pe_self(pe):
        pe.wait_ge(sem("ident_ready"), 1)
        for t in range(NT):
            pe.wait_ge(sem("n0_ready"), t + 1)
            for c in range(NC):
                m = pe.transpose(bank[c][:, t * P:(t + 1) * P], xa[:, t, c * P:(c + 1) * P], ident[:, :])
        m.then_inc(sem("turned"), 1)
        pe.wait_ge(sem("turned_copied"), 4)
        for i, (name, b0) in enumerate((("wq1", 0), ("wk1", 4))):
            pe.wait_ge(sem(f"{name}_loaded"), 16)
            for j in range(NC):
                for c in range(NC):
                    m = pe.matmul(bank[b0 + j], w_in[i][:, c, j * P:(j + 1) * P], nT[:, c, :], start=c == 0, stop=c == NC - 1)
                m.then_inc(sem("self_proj_done"), 1)
        pe.wait_ge(sem("wv1_loaded"), 16)
        for t in range(NT):
            pe.wait_ge(sem("qb1_filled_v"), 2 * (t + 1))
            pe.wait_ge(sem("qb1_filled_a"), 2 * (t + 1))
            for c in range(NC):
                m = pe.matmul(bank[t], nT[:, c, t * P:(t + 1) * P], w_in[2][:, c, :], start=c == 0, stop=c == NC - 1)
            m.then_inc(sem("self_proj_done"), 1)

        def scores(b):
            if b >= 2:
                pe.wait_ge(sem("s1_ready"), b - 1)
            for p in range(NP):
                m = pe.matmul(bank[b % 2][:, p * S:(p + 1) * S], qb1[:, b, p, :], kT1[:, p // 2, b * S:(b + 1) * S],
                              start=True, stop=True)
            m.then_inc(sem("s1_done"), 1)

        pe.wait_ge(sem("self_kv_copied"), NC + NT)
        scores(0)
        for b in range(B):
            k, r = b % 2, slice((b % 2) * S, (b % 2) * S + S)
            if b + 1 < B:
                scores(b + 1)
            pe.wait_ge(sem("p1_ready"), b + 1)
            if b >= 2:
                pe.wait_ge(sem("pT1_copied_v"), b - 1)
                pe.wait_ge(sem("pT1_copied_a"), b - 1)
            for p in range(NP):
                m = pe.transpose(bank[2 + 2 * k + p // 4][0:S, (p % 4) * P:(p % 4 + 1) * P], p1[:, k, p * S:(p + 1) * S],
                                 ident[:, :])
            m.then_inc(sem("pT1_done"), 1)
            pe.wait_ge(sem("pT1_copied_v"), b + 1)
            pe.wait_ge(sem("pT1_copied_a"), b + 1)
            if b >= 2:
                pe.wait_ge(sem("sa_written"), 2 * (b - 1))
            for p in range(NP):
                m = pe.matmul(bank[6 + k][:, p * S:(p + 1) * S], pT1[r, p * P:(p + 1) * P], v1[r, b // 2, p * S:(p + 1) * S],
                              start=True, stop=True)
            m.then_inc(sem("o1_done"), 1)
        for t in range(NT):
            pe.wait_ge(sem("xa_ready"), t + 1)
            for c in range(NC):
                m = pe.transpose(bank[c][:, t * P:(t + 1) * P], xa[:, t, c * P:(c + 1) * P], ident[:, :])
        m.then_inc(sem("turned"), 1)
        pe.wait_ge(sem("turned_copied"), 8)
        pe.wait_ge(sem("w2_loaded"), 48)
        for j in range(NC):
            for c in range(NC):
                m = pe.matmul(bank[4 + j], wq2[:, c, j * P:(j + 1) * P], nT[:, c, :], start=c == 0, stop=c == NC - 1)
            m.then_inc(sem("self_proj_done"), 1)

    PROJ = []
    for g in range(NG - 2):
        PROJ += [("k", g, 0), ("k", g, 1), ("v", 2 * g), ("v", 2 * g + 1)]
    PROJ += [("k", g, j) for g in (NG - 2, NG - 1) for j in (0, 1)]
    PROJ += [("v", t) for t in range(2 * (NG - 2), CT)]
    QUART = -(-CT // 4)
    JOBS = PROJ + [("p", p, q) for p in range(NP) for q in range(QUART)]
    NJ = len(JOBS)
    FIRST_P = len(PROJ)
    LAST_K = max(k for k, j in enumerate(PROJ) if j[0] == "k")
    EARLY = FIRST_P - 2
    HALVES = ((0, 1024), (1024, CTX))

    def last_job(g):
        return max(k for k, j in enumerate(PROJ) if (j[1] if j[0] == "k" else j[1] // 2) == g)

    def group_width(g):
        return min(G, CW - g * G)

    def tile_rows(t):
        return min(P, CTX - t * P)

    def job_views(k):
        job, bk = JOBS[k], ring[k % 3]
        if job[0] == "k":
            w = group_width(job[1])
            s = slice(job[1] * G, job[1] * G + w)
            views = []
            for odd in (0, 1):
                pairs = kT[:, 4 * job[2]:4 * job[2] + 4, s].rearrange("p (c h) w -> p c h w", h=2)[:, :, odd, :]
                own, other = slice(odd * 64, odd * 64 + 64), slice(64 - odd * 64, 128 - odd * 64)
                views.append((bk[:, :].rearrange("p (c w) -> p c w", c=2)[own, :, 0:w], pairs[own], pairs[other]))
            return views
        if job[0] == "v":
            r = tile_rows(job[1])
            return [(bk[0:r, :], v[0:r, 0, job[1], :], v[0:r, 1, job[1], :])]
        t0 = 4 * job[2]
        n = min(4, CT - t0)
        r = tile_rows(t0 + n - 1)
        return [(bk[0:r, 0:n * P].rearrange("p (t w) -> p t w", t=n), pT_h[0:r, t0:t0 + n, :], pT_l[0:r, t0:t0 + n, :])]

    def loads_before(b0, i, g):
        return NG * i + (NG * b0 + g) // 2 + 1

    def sp_cross(sp, b0, i, first=False):
        b = b0 + 2 * i
        for g in range(NG):
            k, w = (b0 + g) % 2, min(G, CTX - g * G)
            if not (first and g < 2):
                sp.wait_ge(sem("ctx_low"), NG * b + g - 1)
            sp.dma_start(raw[:, k, :, 0:w],
                         a["ctxT"][b, :, g * G:g * G + w].rearrange("(c p) t -> p c t", p=P)).then_inc(sem(f"ctx_loaded{k}"), 16)

    def dve_queries(dve, b0, i):
        b = b0 + 2 * i
        dve.wait_ge(sem("qT_ready"), NC)
        for k in range(12):
            g = k % 4
            own = slice(32 * g, 32 * g + 32)
            other = slice(32 * ((g + 2) % 4), 32 * ((g + 2) % 4) + 32)
            src = qT[own, :, bass.ds(b * S, S)]

            def place(v, r):
                return v[r, :, :].rearrange("p (c h) w -> p c h w", h=2)[:, :, g // 2, (g % 2) * S:(g % 2) * S + S]

            if k < 8:
                dve.tensor_scalar(place(qb_h, own if k < 4 else other), src, 1.0, None, ALU.mult)\
                   .then_inc(sem("queries_ready"), 1)
            else:
                dve.wait_ge(sem("queries_ready"), 12 * b + g + 1)
                dve.tensor_tensor(place(qb_l, own), src, place(qb_h, own).bitcast(F32), ALU.subtract)\
                   .then_inc(sem("queries_ready"), 1)

    def pe_cross(pe, b0, i, first=False):
        b = b0 + 2 * i
        J = NJ * b

        def claim(k):
            if k >= 3:
                pe.wait_ge(sem("job_low"), J + k - 2)
            elif k == 0 and not first:
                pe.wait_ge(sem("job_low"), J)

        def project(k):
            job = PROJ[k]
            g = job[1] if job[0] == "k" else job[1] // 2
            s = (b0 + g) % 2
            claim(k)
            if job[0] == "k":
                w = group_width(g)
                pe.wait_ge(sem("ctx_low"), NG * b + g + 1)
                for j in (0, 1):
                    e = slice((2 * job[2] + j) * P, (2 * job[2] + j + 1) * P)
                    for c in range(NC):
                        for n, (wt, xt) in enumerate(((wk_h, x_h), (wk_h, x_l), (wk_l, x_h))):
                            m = pe.matmul(ring[k % 3][:, j * G:j * G + w], wt[:, c, e], xt[:, s, c, 0:w],
                                          start=c == 0 and n == 0, stop=c == NC - 1 and n == 2)
            else:
                r = min(P, CW - job[1] * P)
                t = slice((job[1] % 2) * P, (job[1] % 2) * P + r)
                for c in range(NC):
                    for n, (xt, wt) in enumerate(((x_h, wv_h), (x_h, wv_l), (x_l, wv_h))):
                        m = pe.matmul(ring[k % 3][0:r, :], xt[:, s, c, t], wt[:, c, :],
                                      start=c == 0 and n == 0, stop=c == NC - 1 and n == 2)
            m.then_inc(sem("job_done"), 1)

        def scores(p, half):
            if p == 0 and half == 0:
                pe.wait_ge(sem("queries_ready"), 12 * (b + 1))
                pe.wait_ge(sem("job_low"), J + LAST_K + 1)
            if not (first and p == 0):
                pe.wait_ge(sem("prob_ready"), 2 * (NP * b + p) - 1 + half)
            for n in (2 * half, 2 * half + 1):
                w = min(512, CW - n * 512)
                for j, qt in enumerate((qb_h, qb_l)):
                    m = pe.matmul(sc[:, n, 0:w], qt[:, p, :], kT[:, p, n * 512:n * 512 + w], start=j == 0, stop=j == 1)
            m.then_inc(sem("scores_done"), 1)

        def transposes(p, quarters):
            for q in quarters:
                pe.wait_ge(sem("prob_ready"), 2 * (NP * b + p) + 1 + q // 2)
                k = FIRST_P + QUART * p + q
                claim(k)
                for t in range(4 * q, min(4 * q + 4, CT)):
                    r = tile_rows(t)
                    m = pe.transpose(ring[k % 3][0:r, (t % 4) * P:(t % 4 + 1) * P], prob[:, t * P:t * P + r], ident[:, :])
                m.then_inc(sem("job_done"), 1)

        def outputs(p):
            if p == NP // 2:
                pe.wait_ge(sem("cross_summed"), 4 * b + 2)
            elif p == 0 and not first:
                pe.wait_ge(sem("cross_summed"), 4 * b)
            e = slice(p * S, (p + 1) * S)
            o = (p % (NP // 2)) * P
            for t in range(CT):
                r = tile_rows(t)
                if t % 4 == 0:
                    pe.wait_ge(sem("job_low"), J + FIRST_P + QUART * p + t // 4 + 1)
                for n in ((0, 1) if t == 0 else (1, 0)):
                    if n == 0:
                        m = pe.matmul(pv[:, o:o + P], pT_h[0:r, t, :], v[0:r, :, t, e], start=t == 0, stop=t == CT - 1)
                    else:
                        m = pe.matmul(pv[:, o:o + S], pT_l[0:r, t, :], v[0:r, 0, t, e], start=False, stop=False)
            m.then_inc(sem("outputs_done"), 1)

        if first:
            pe.wait_ge(sem("w2_low"), 2)
        for k in range(EARLY):
            project(k)
        scores(0, 0)
        scores(0, 1)
        for k in range(EARLY, FIRST_P):
            project(k)
        for p in range(NP):
            transposes(p, (0, 1))
            if p + 1 < NP:
                scores(p + 1, 0)
            transposes(p, (2, 3))
            if p + 1 < NP:
                scores(p + 1, 1)
            outputs(p)

    def split_ready(eng, b0, i, g, first=False):
        b = b0 + 2 * i
        k = (b0 + g) % 2
        eng.wait_ge(sem(f"ctx_loaded{k}"), 16 * loads_before(b0, i, g))
        if not (first and g < 2):
            J = NJ * b + last_job(g - 2) + 1 if g >= 2 else NJ * (b - 1) + last_job(NG - 2 + g) + 1
            eng.wait_ge(sem("job_done"), J)

    def act_split(act, b0, i, g, first=False):
        k, w = (b0 + g) % 2, group_width(g)
        split_ready(act, b0, i, g, first)
        act.copy(x_h[:, k, :, 0:w], raw[:, k, :, 0:w]).then_inc(sem("ctx_high"), 1)

    def dve_split(dve, b0, i, g, first=False):
        b = b0 + 2 * i
        k, w = (b0 + g) % 2, group_width(g)
        dve.wait_ge(sem("ctx_high"), NG * b + g + 1)
        dve.tensor_tensor(x_l[:, k, :, 0:w], raw[:, k, :, 0:w], x_h[:, k, :, 0:w].bitcast(F32), ALU.subtract)\
           .then_inc(sem("ctx_low"), 1)

    def act_cross(act, b0, i, first=False, last=False):
        b = b0 + 2 * i
        J = NJ * b

        def high(k):
            act.wait_ge(sem("job_done"), J + k + 1)
            for src, hi, _ in job_views(k):
                ins = act.copy(hi, src)
            ins.then_inc(sem("job_high"), 1)

        if first:
            act_split(act, b0, i, 0, True)
            act_split(act, b0, i, 1, True)
        for g in range(NG - 2):
            for k in range(4 * g, 4 * g + 4):
                high(k)
            act_split(act, b0, i, g + 2)
        for k in range(4 * (NG - 2), EARLY):
            high(k)
        for p in range(NP):
            act.wait_ge(sem("max_ready"), NP * b + p + 1)
            if p >= 1:
                act.wait_ge(sem("job_done"), J + FIRST_P + QUART * p)
            for (lo, hi), total in zip(HALVES, (esum, esum_b)):
                act.activation(prob[:, lo:hi], sc[:, :, :].rearrange("p n w -> p (n w)")[:, lo:hi], ACT.Exp,
                               bias=nmax[:, b0 % 2, p:p + 1], accum_out=total[:, b0 % 2, p:p + 1])\
                   .then_inc(sem("prob_ready"), 1)
            if p == 0:
                for k in range(EARLY, FIRST_P):
                    high(k)
            for k in range(FIRST_P + QUART * p, FIRST_P + QUART * (p + 1)):
                high(k)
            if p in (1, 2) and not last:
                act_split(act, b0 + 1, i, p - 1)

    def dve_cross(dve, b0, i, first=False, last=False, link=None):
        b = b0 + 2 * i
        J = NJ * b

        def low(k):
            dve.wait_ge(sem("job_high"), J + k + 1)
            for src, hi, lo in job_views(k):
                ins = dve.tensor_tensor(lo, src, hi.bitcast(F32), ALU.subtract)
            ins.then_inc(sem("job_low"), 1)

        if first:
            dve.wait_ge(sem("queries_zeroed"), 1)
            dve_queries(dve, b0, i)
            dve_split(dve, b0, i, 0, True)
            dve_split(dve, b0, i, 1, True)
        for g in range(NG - 2):
            for k in range(4 * g, 4 * g + 4):
                low(k)
            dve_split(dve, b0, i, g + 2)
            if last and g >= 2:
                dve_x_b(dve, link, g - 2)
        for k in range(4 * (NG - 2), EARLY):
            low(k)

        def maximum(p, half):
            lo, hi = HALVES[half]
            dve.wait_ge(sem("scores_done"), 2 * (NP * b + p) + half + 1)
            dve.tensor_reduce(hmax[:, half:half + 1], sc[:, :, :].rearrange("p n w -> p (n w)")[:, lo:hi], AX.X,
                              ALU.max).then_inc(sem("half_max"), 1)
            if half == 1:
                dve.wait_ge(sem("half_max"), 2 * (NP * b + p + 1))
                dve.tensor_reduce(nmax[:, b0 % 2, p:p + 1], hmax[:, :], AX.X, ALU.max, negate=True)\
                   .then_inc(sem("max_ready"), 1)

        r = slice((b0 % 2) * S, (b0 % 2) * S + S)

        def write_outputs(half):
            n = slice(half * (NP // 2), (half + 1) * (NP // 2))
            total, inverse = esum[:, b0 % 2, n], rinv[:, b0 % 2, n]
            dve.tensor_tensor(total, total, esum_b[:, b0 % 2, n], ALU.add).then_inc(sem("inverse_ready"), 1)
            dve.wait_ge(sem("inverse_ready"), 4 * b + 2 * half + 1)
            dve.reciprocal(inverse, total).then_inc(sem("inverse_ready"), 1)
            dve.wait_ge(sem("outputs_done"), NP * b + (NP // 2) * (half + 1))
            parts = pv[:, :].rearrange("p (n x h e) -> p n x h e", n=NP // 2, x=2, h=2)
            for odd in (0, 1):
                q = slice(odd * S, odd * S + S)
                dve.tensor_copy(half_out[q, :, :], parts[q, :, 0, odd, :]).then_inc(sem("cross_copied"), 1)
            for odd in (0, 1):
                q = slice(odd * S, odd * S + S)
                dve.wait_ge(sem("cross_copied"), 4 * b + 2 * half + odd + 1)
                dve.tensor_tensor(half_out[q, :, :], parts[q, :, 1, odd, :], half_out[q, :, :], ALU.add)\
                   .then_inc(sem("cross_summed"), 1)
            dve.wait_ge(sem("inverse_ready"), 4 * b + 2 * half + 2)
            for odd in (0, 1):
                q = slice(odd * S, odd * S + S)
                dve.wait_ge(sem("cross_summed"), 4 * b + 2 * half + odd + 1)
                dve.tensor_tensor(cat[r, :].rearrange("p (n h e) -> p n h e", n=NP, h=2)[:, n, odd, :], half_out[q, :, :],
                                  over_width(rinv[q, b0 % 2, n], E), ALU.mult).then_inc(sem("cross_written"), 1)

        maximum(0, 0)
        maximum(0, 1)
        for k in range(EARLY, FIRST_P):
            low(k)
        for p in range(NP):
            for q in (0, 1):
                low(FIRST_P + QUART * p + q)
            if p == NP // 2:
                write_outputs(0)
            dve.wait_ge(sem("max_ready"), NP * b + p + 1)
            if p + 1 < NP:
                maximum(p + 1, 0)
            for q in (2, 3):
                low(FIRST_P + QUART * p + q)
            if p + 1 < NP:
                maximum(p + 1, 1)
            if p in (1, 2) and not last:
                dve_split(dve, b0 + 1, i, p - 1)
        if not last:
            dve_queries(dve, b0 + 1, i)
        write_outputs(1)
        dve.wait_ge(sem("cross_written"), 4 * (b + 1))
        t = i + b0 // 2
        dve.tensor_tensor(xa[r, t, :], xa[r, t, :], cat[r, :], ALU.add).then_inc(sem("cross_added"), 1)

    def batches(eng, step, **ends):
        step(eng, 0, 0, first=True)
        with eng.Fori(0, (B - 2) // 2) as i:
            step(eng, 1, i)
            step(eng, 2, i)
        step(eng, B - 1, 0, **ends)

    rows4 = at("rows4", R, [P, 4, D])
    bf2 = at("bf2", R + 8192, [P, D])
    bf1 = at("bf1", R + 10240, [P, NH])
    wf1 = at("wf1", R + 16384, [P, NC, HID])
    wf2 = at("wf2", R + 49152, [P, NH, D])
    xb_h = at("xb_h", R + 114688, [P, NC, TOK], F32R)
    xb_l = at("xb_l", R + 139264, [P, NC, TOK], F32R)
    F0 = R + 81920
    hid = at("hid", F0, [P, 2, TOK])
    hid_h = at("hid_h", F0 + 4096, [P, 2, TOK], F32R)
    hid_l = at("hid_l", F0 + 8192, [P, 2, TOK], F32R)
    w1_h = at("w1_h", F0 + 12288, [P, 2, NC, P], F32R)
    w1_l = at("w1_l", F0 + 16384, [P, 2, NC, P], F32R)
    w2_h = at("w2_h", F0 + 20480, [P, 2, D], F32R)
    w2_l = at("w2_l", F0 + 24576, [P, 2, D], F32R)
    xT = at("xT", R + 114688, [P, NC, TOK])
    tmp = at("tmp", R + 122880, [P, NT, D])
    xres = at("xres", R + 131072, [P, NT, D])

    def sp_ffn(sp):
        sp.wait_ge(sem("queries_ready"), 12 * B)
        for i, name in enumerate(("g2", "be2", "g3", "be3")):
            sp.dma_start(rows4[:, i, :], row_dram(name)).then_inc(sem("ffn_rows_loaded"), 16)
        sp.wait_ge(sem("job_done"), NJ * (B - 1) + FIRST_P)
        sp.dma_start(wf1[:, :, :], w_dram("wf1")).then_inc(sem("wf1_loaded"), 16)
        sp.wait_ge(sem("scores_done"), 2 * NP * B)
        sp.dma_start(bf2[:, :], row_dram("bf2")).then_inc(sem("ffn_rows_loaded"), 16)
        sp.dma_start(bf1[:, :], a["bf1"]).then_inc(sem("ffn_rows_loaded"), 16)
        sp.dma_start(wf2[:, :, :], w_dram("wf2")).then_inc(sem("wf2_loaded"), 16)
        sp.wait_ge(sem("outputs_done"), NP * B)
        sp.dma_start(xres[:, :, :], x_dram).then_inc(sem("xres_loaded"), 16)

    def pe_turn(pe, src, ready):
        for t in range(NT):
            pe.wait_ge(sem(ready), t + 1)
            for c in range(NC):
                m = pe.transpose(bank[c][:, t * P:(t + 1) * P], src[:, t, c * P:(c + 1) * P], ident[:, :])
        m.then_inc(sem("turned"), 1)

    def copy_turned(eng, copy, n, chunks, dst):
        eng.wait_ge(sem("turned"), n + 1)
        for c in chunks:
            copy(dst[:, c, :], bank[c]).then_inc(sem("turned_copied"), 1)

    SPLITS = [("first", 0), ("first", 1)]
    for m in range(NH):
        SPLITS += [("second", m), ("hidden", m)] + ([("first", m + 2)] if m + 2 < NH else [])

    def split_views(what, m):
        k = m % 2
        if what == "first":
            return wf1[:, :, m * P:(m + 1) * P], w1_h[:, k, :, :], w1_l[:, k, :, :]
        if what == "second":
            return wf2[:, m, :], w2_h[:, k, :], w2_l[:, k, :]
        return hid[:, k, :], hid_h[:, k, :], hid_l[:, k, :]

    def dve_x_b(dve, link, t):
        dve.wait_ge(sem("cross_added"), 2 * (t + 1))
        if t == 0:
            dve.wait_ge(sem("ffn_rows_loaded"), 64)
        link(dve.tensor_tensor(xa[:, t, :], xa[:, t, :], bv2[:, :], ALU.add))
        norm_stats(dve, link, xa, t)
        norm_affine(dve, link, 2, xa, xa, t, rows4[:, 0, :], rows4[:, 1, :]).then_inc(sem("xb_ready"), 1)

    def dve_ffn(dve, link):
        def split(k):
            full, hi, lo = split_views(*SPLITS[k])
            dve.wait_ge(sem("ffn_high"), k + 1 if k < 2 else NC + k + 1)
            dve.tensor_tensor(lo, full, hi.bitcast(F32), ALU.subtract).then_inc(sem("ffn_low"), 1)

        split(0)
        split(1)
        dve_x_b(dve, link, NT - 1)
        for c in range(NC):
            dve.wait_ge(sem("ffn_high"), 2 + c + 1)
            dve.tensor_tensor(xb_l[:, c, :], bank[c], xb_h[:, c, :].bitcast(F32), ALU.subtract)\
               .then_inc(sem("turned_copied"), 1)
        dve_xor(dve, link)
        dve.wait_ge(sem("ffn_rows_loaded"), 96)
        dve.wait_ge(sem("xb_ready"), NT)
        dve.wait_ge(sem("xres_loaded"), 16)
        link(dve.tensor_tensor(xa[:, :, :], xa[:, :, :], over_tiles(bf2[:, :]), ALU.add))
        for k in range(2, len(SPLITS)):
            split(k)
        for t in range(NT):
            dve.wait_ge(sem("ffn_done"), t + 1)
            link(dve.tensor_tensor(tmp[:, t, :], bank[4 + t], xa[:, t, :], ALU.add))
            norm_stats(dve, link, tmp, t)
            dve.wait_ge(sem("variance_ready"), norm_count(3, t))
            link(norm_center(dve, tmp, t, rows4[:, 2, :]))
        for t in range(NT + 1):
            if t < NT:
                link(norm_shift(dve, 3, tmp, tmp, t, rows4[:, 3, :]))
                link(dve.tensor_tensor(xa[:, t, :], tmp[:, t, :], xres[:, t, :], ALU.add))
                norm_stats(dve, link, xa, t)
            if t >= 1:
                norm_apply(dve, 4, tmp, xa, t - 1).then_inc(sem("n1_ready"), 1)

    def act_ffn(act):
        act.wait_ge(sem("wf1_loaded"), 16)
        act.wait_ge(sem("scores_done"), 2 * NP * B)
        for what, m in SPLITS:
            full, hi, lo = split_views(what, m)
            if what == "second" and m == 0:
                act.wait_ge(sem("turned"), 3)
                for c in range(NC):
                    act.copy(xb_h[:, c, :], bank[c]).then_inc(sem("ffn_high"), 1)
                act.wait_ge(sem("ffn_rows_loaded"), 96)
                act.wait_ge(sem("wf2_loaded"), 16)
            if what == "hidden":
                act.wait_ge(sem("hid_done"), m + 1)
                if m >= 2:
                    act.wait_ge(sem("ffn_low"), SPLITS.index(("hidden", m - 2)) + 1)
                    act.wait_ge(sem("down_products"), m - 1)
                act.activation(full, bank[m % 4], ACT.Relu, bias=bf1[:, m:m + 1])
                act.activation(hi, bank[m % 4], ACT.Relu, bias=bf1[:, m:m + 1]).then_inc(sem("ffn_high"), 1)
            else:
                if m >= 2:
                    act.wait_ge(sem("hid_done" if what == "first" else "down_products"), m - 1)
                act.copy(hi, full).then_inc(sem("ffn_high"), 1)

    def pe_ffn(pe):
        pe_turn(pe, xa, "xb_ready")
        pe.wait_ge(sem("turned_copied"), 12)

        def hidden(m):
            pe.wait_ge(sem("ffn_low"), SPLITS.index(("first", m)) + 1)
            for c in range(NC):
                for n, (wt, xt) in enumerate(((w1_h, xb_h), (w1_h, xb_l), (w1_l, xb_h))):
                    k = pe.matmul(bank[m % 4], wt[:, m % 2, c, :], xt[:, c, :], start=c == 0 and n == 0,
                                  stop=c == NC - 1 and n == 2)
            k.then_inc(sem("hid_done"), 1)

        def down(m):
            pe.wait_ge(sem("ffn_low"), SPLITS.index(("second", m)) + 1)
            pe.wait_ge(sem("ffn_low"), SPLITS.index(("hidden", m)) + 1)
            for t in range(NT):
                for n, (ht, wt) in enumerate(((hid_h, w2_h), (hid_h, w2_l), (hid_l, w2_h))):
                    k = pe.matmul(bank[4 + t], ht[:, m % 2, t * P:(t + 1) * P], wt[:, m % 2, :], start=m == 0 and n == 0,
                                  stop=m == NH - 1 and n == 2)
                if m == NH - 1:
                    k.then_inc(sem("ffn_done"), 1)
            if m < NH - 1:
                k.then_inc(sem("down_products"), 1)

        hidden(0)
        for m in range(NH):
            if m + 1 < NH:
                hidden(m + 1)
            down(m)

    NM = NT * GH
    LEVELS = (1, 2, 4, 8, 16, 32)
    kf = at("kf", R + 81920, [P, GH, TOK])
    qf = at("qf", R + 90112, [P, GH, TOK])
    vf = at("vf", R + 98304, [P, GH, TOK])
    ema = at("ema", R + 106496, [P, GH, TOK])
    vtok = at("vtok", R + 122880, [P, NM, P])
    qk = at("qk", R + 131072, [P, NM, P])
    nT_s = at("nT_s", R + 139264, [P, NM, P])
    nT_all = at("nT_all", R + 147456, [P, NM, P])
    xm = at("xm", R, [P, NM, P])
    xmT = at("xmT", R + 8192, [P, NM, P])
    dwo = at("dwo", R + 159744, [P, NC, D])
    dw = [at(f"dw{i}", R + 167936 + 8192 * i, [P, NC, D]) for i in range(3)]
    ybuf = at("ybuf", R + 167936, [P, NM, P])
    tbuf = at("tbuf", R + 176128, [P, NM, P])
    rbuf = at("rbuf", R + 184320, [P, NM, P])
    S0 = R + 192512
    conv = at("conv", S0, [P, 3, NC, TAPS])
    wgates = at("wgates", S0 + 192, [P, NC, 12])
    cmix = at("cmix", S0 + 384, [GH, TAPS])
    mbias = at("mbias", S0 + 416, [GH, 1])
    hbias = at("hbias", S0 + 448, [GH, 1])
    sel = at("sel", S0 + 512, [GH, GH, P])
    rmsw = at("rmsw", S0 + 2560, [P, 1])
    gtok = at("gtok", S0 + 3072, [P, 2, NT, GH])
    norms = at("norms", S0 + 3200, [P, 2, NM])
    scal = at("scal", S0 + 3328, [P, 4, NM])
    Z = at("Z", S0 + 3584, [P, 2, P])
    zint = at("zint", S0 + 4608, [P, 2, P], mybir.dt.int32)
    masks = at("masks", R + 155648, [P, len(LEVELS), P])
    mask1 = at("mask1", R + 158720, [P, P])
    incl = at("incl", R + 159232, [P, P])
    gamma = at("gamma", S0 + 5632, [GH, TOK])
    beta = at("beta", 2048, [GH, TOK])
    mixr = at("mixr", R + 122880, [GH, TOK])
    trow = at("trow", R + 124928, [GH, TOK])
    th = at("th", R + 131072, [P, 3 * NC, TOK])
    NPROJ = 3 * NC
    feats = (kf, qf, vf)
    squares = (th[:, 0:4, :], xT[:, :, :])

    def sp_delta(sp):
        for i, name in enumerate(("dwk", "dwq", "dwv")):
            sp.dma_start(dw[i][:, :, :], w_dram(name)).then_inc(sem("dw_loaded"), 16)
        for i, name in enumerate(("conv_k", "conv_q", "conv_v")):
            sp.dma_start(conv[:, i, :, :], a[name]).then_inc(sem("delta_small_loaded"), 16)
        sp.dma_start(wgates[:, :, :], w_dram("wgates")).then_inc(sem("delta_small_loaded"), 16)
        sp.dma_start(cmix[:, :], a["conv_mix"]).then_inc(sem("delta_small_loaded"), 16)
        sp.dma_start(mbias[:, :], a["mix_bias"]).then_inc(sem("delta_small_loaded"), 16)
        sp.dma_start(rmsw[:, :], a["rms_w"]).then_inc(sem("delta_small_loaded"), 16)
        sp.dma_start(wg[:, :, :], w_dram("wg")).then_inc(sem("delta_small_loaded"), 16)
        sp.dma_start(bg[:, :], row_dram("bg")).then_inc(sem("delta_small_loaded"), 16)
        sp.dma_start(dwo[:, :, :], w_dram("dwo")).then_inc(sem("dw_loaded"), 16)

    def pool_masks(pool, link):
        pool.wait_ge(sem("outputs_done"), NP * B)
        link(pool.iota(zint[:, 0, :], pattern=[[0, P]], base=0, channel_multiplier=1))
        pool.iota(zint[:, 1, :], pattern=[[1, P]], base=0, channel_multiplier=0).then_inc(sem("indices_ready"), 1)
        pool.wait_ge(sem("xor_ready"), 1)
        link(pool.affine_select(out=Z[:, 0, :], in_=Z[:, 0, :], compare_op=ALU.is_gt, fill=0.0, base=0,
                                pattern=[[-1, P]], channel_multiplier=1))
        link(pool.affine_select(out=Z[:, 1, :], in_=Z[:, 1, :], compare_op=ALU.is_gt, fill=0.0, base=0,
                                pattern=[[1, P]], channel_multiplier=-1))

        def between(dst, z, lo, hi):
            link(pool.tensor_scalar(dst, z, float(lo), None, ALU.is_ge))
            link(pool.tensor_scalar(incl[:, :], z, float(hi), None, ALU.is_ge))
            link(pool.tensor_tensor(dst, dst, incl[:, :], ALU.subtract))

        for i, s in enumerate(LEVELS):
            between(masks[:, i, :], Z[:, 1, :], s, 2 * s)
        between(mask1[:, :], Z[:, 0, :], 1, 2)
        link(pool.tensor_scalar(incl[:, :], Z[:, 1, :], float(S), None, ALU.is_ge))
        link(pool.tensor_scalar(Z[:, 1, :], Z[:, 1, :], 1.0, None, ALU.is_ge))
        link(pool.tensor_tensor(incl[:, :], Z[:, 1, :], incl[:, :], ALU.subtract))
        link(pool.tensor_tensor(incl[:, :], incl[:, :], ident[:, :], ALU.add))
        link(pool.memset(sel[:, :, :], 0.0))
        pool.affine_select(out=sel[:, :, :], in_=sel[:, :, :], compare_op=ALU.not_equal, fill=1.0, base=0,
                           pattern=[[-1, GH], [0, P]], channel_multiplier=1).then_inc(sem("masks_ready"), 1)

    def dve_xor(dve, link):
        dve.wait_ge(sem("indices_ready"), 1)
        link(dve.tensor_tensor(zint[:, 0, :], zint[:, 0, :], zint[:, 1, :], ALU.bitwise_xor))
        link(dve.tensor_copy(Z[:, 0, :], zint[:, 0, :]))
        dve.tensor_copy(Z[:, 1, :], zint[:, 0, :]).then_inc(sem("xor_ready"), 1)

    def level_matrix(m):
        return slice((m % 4) * P, (m % 4 + 1) * P)

    def four(v, t):
        return v[:, 4 * t:4 * t + 4, :].rearrange("p m w -> p (m w)")

    def four3(v, t):
        return v[:, 4 * t:4 * t + 4, :]

    def bank3(i):
        return bank[i].rearrange("p (m w) -> p m w", m=4)

    def pool_delta(pool, link):
        for n in (3, 4):
            for t in range(NT):
                norm_rstd(pool, link, n, t)
        for i, f in enumerate((kf, qf)):
            pool.wait_ge(sem("feature_ready"), NC * (i + 1))
            if i == 1:
                pool.wait_ge(sem("proj_done"), NPROJ)
            pool.tensor_tensor(squares[i], f[:, :, :], f[:, :, :], ALU.mult).then_inc(sem("squares_ready"), 1)
        pool.wait_ge(sem("norms_summed"), 1)
        link(pool.tensor_tensor(norms[:, 0, :], norms[:, 0, :], mhalf[:, 0:NM], ALU.pow))
        pool.tensor_tensor(scal[:, 0, :], norms[:, 0, :], norms[:, 0, :], ALU.mult).then_inc(sem("norms_ready"), 1)
        for l in range(1, len(LEVELS)):
            if l == 1:
                pool.wait_ge(sem("nT_ready"), NT)
                pool.wait_ge(sem("transposed_n"), NT)
                pool.wait_ge(sem("xm_started"), 1)
            else:
                pool.wait_ge(sem("y_done"), NT * (l - 1))
            for t in range(NT):
                pool.tensor_tensor(four3(nT_s, t), four3(nT_all, t), over_tiles(masks[:, l, :], 4), ALU.mult)\
                    .then_inc(sem("level_ready"), 1)
            if l == 1:
                pool.wait_ge(sem("norms_summed"), 2)
                pool.tensor_tensor(norms[:, 1, :], norms[:, 1, :], mhalf[:, 0:NM], ALU.pow).then_inc(sem("norms_ready"), 1)
        for t in range(NT):
            pool.wait_ge(sem("mean_square"), t + 1)
            pool.tensor_tensor(norms[:, 0, 4 * t:4 * t + 4], norms[:, 0, 4 * t:4 * t + 4], mhalf[:, 0:4], ALU.pow)\
                .then_inc(sem("rms_ready"), 1)

    def dve_delta(dve, link):
        copy_turned(dve, dve.tensor_copy, 3, (0, 1), xT)
        dve.wait_ge(sem("delta_small_loaded"), 16 * 9)
        dve.tensor_scalar(hbias[:, :], mbias[:, :], 0.5, None, ALU.mult).then_inc(sem("hbias_ready"), 1)
        for i, g in enumerate((beta, gamma)):
            dve.wait_ge(sem("gate_tanh"), i + 1)
            dve.tensor_scalar(g[:, :], g[:, :], 0.5, 0.5, ALU.mult, ALU.add).then_inc(sem("gates_ready"), 1)
        logit = bank[6][0:GH, :].rearrange("p (b s) -> p b s", b=B)
        mix3 = mixr[:, :].rearrange("p (b s) -> p b s", b=B)
        dve.wait_ge(sem("gates_done"), 3)
        link(dve.tensor_scalar(mix3, logit, cmix[:, TAPS - 1:TAPS], None, ALU.mult))
        for k in range(1, TAPS):
            ins = dve.scalar_tensor_tensor(mix3[:, :, k:S], logit[:, :, 0:S - k], cmix[:, TAPS - 1 - k:TAPS - k],
                                           mix3[:, :, k:S], ALU.mult, ALU.add)
            if k < TAPS - 1:
                link(ins)
        ins.then_inc(sem("mix_conv"), 1)
        dve.wait_ge(sem("mix_tanh"), 1)
        dve.scalar_tensor_tensor(mixr[:, :], trow[:, :], 1.0, mixr[:, :], ALU.add, ALU.mult).then_inc(sem("mix_silu"), 1)
        dve.wait_ge(sem("mix_tanh"), 2)
        dve.tensor_scalar(mixr[:, :], trow[:, :], 0.5, 0.5, ALU.mult, ALU.add).then_inc(sem("gates_ready"), 1)

        def dst(n):
            return feats[n // NC][:, n % NC, :]

        for n in range(NPROJ + 2):
            if n < NPROJ:
                x3 = bank[n % 4].rearrange("p (b s) -> p b s", b=B)
                y3 = dst(n).rearrange("p (b s) -> p b s", b=B)
                dve.wait_ge(sem("first_tap"), n + 1)
                for k in range(1, TAPS):
                    ins = dve.scalar_tensor_tensor(y3[:, :, k:S], x3[:, :, 0:S - k],
                                                   conv[:, n // NC, n % NC, TAPS - 1 - k:TAPS - k], y3[:, :, k:S],
                                                   ALU.mult, ALU.add)
                    if k < TAPS - 1:
                        link(ins)
                ins.then_inc(sem("conv_done"), 1)
            if 1 <= n <= NPROJ:
                m = n - 1
                dve.wait_ge(sem("tanh_first"), m + 1)
                ins = dve.scalar_tensor_tensor(dst(m), th[:, m, :], 1.0, dst(m), ALU.add, ALU.mult)
                ins.then_inc(sem("silu_first" if m < 2 * NC else "values_ready"), 1)
            if 2 <= n < 2 * NC + 2:
                m = n - 2
                dve.wait_ge(sem("tanh_second"), m + 1)
                dve.scalar_tensor_tensor(dst(m), th[:, m, :], 1.0, dst(m), ALU.add, ALU.mult)\
                   .then_inc(sem("feature_ready"), 1)
        def norms_out(i):
            dve.wait_ge(sem("norms_done"), i + 1)
            dve.tensor_scalar(norms[:, i, :], bank[6][:, i * NM:(i + 1) * NM], 16e-6, None, ALU.add)\
               .then_inc(sem("norms_summed"), 1)

        norms_out(0)
        for h in range(GH):
            dve.wait_ge(sem("gamma_spread"), h + 1)
            if h == 0:
                dve.wait_ge(sem("values_ready"), NC)
            dve.scalar_tensor_tensor(four(ybuf, h), bank[h], 1.0, vf[:, h, :], ALU.subtract, ALU.mult)\
               .then_inc(sem("gamma_used_v"), 1)
            dve.wait_ge(sem("gamma_used_a"), h + 1)
            link(dve.memset(tbuf[:, 4 * h:4 * h + 4, :].rearrange("p m w -> p (m w)")[:, 0:TOK:S], 0.0))
            dve.wait_ge(sem("gamma_used_v"), h + 1)
            dve.tensor_tensor_scan(ema[:, h, :], four(tbuf, h), four(ybuf, h), 0.0, ALU.mult, ALU.subtract)\
               .then_inc(sem("ema_ready"), 1)
        dve.wait_ge(sem("gates_turned"), 1)
        dve.tensor_copy(gtok[:, :, :, :].rearrange("p a t h -> p (a t h)"), bank[7][:, 0:2 * NM]).then_inc(sem("gtok_ready"), 1)
        dve.wait_ge(sem("gtok_ready"), 1)
        dve.wait_ge(sem("norms_ready"), 1)
        bt = gtok[:, 0, :, :].rearrange("p t h -> p (t h)")
        mt = gtok[:, 1, :, :].rearrange("p t h -> p (t h)")
        dve.tensor_tensor(scal[:, 0, :], scal[:, 0, :], bt, ALU.mult).then_inc(sem("factors_ready"), 1)
        dve.scalar_tensor_tensor(scal[:, 1, :], bt, 0.5, norms[:, 0, :], ALU.mult, ALU.mult).then_inc(sem("factors_ready"), 1)
        link(dve.tensor_scalar(scal[:, 2, :], mt, -1.0, 1.0, ALU.mult, ALU.add))
        link(dve.tensor_scalar(scal[:, 3, :], mt, 0.5, None, ALU.mult))
        dve.wait_ge(sem("factors_ready"), 2)

        def factor(i, t):
            return over_width(scal[:, i, 4 * t:4 * t + 4], P)

        for t in range(NT):
            dve.wait_ge(sem("v_turned"), t + 1)
            dve.tensor_tensor(four3(vtok, t), bank3(4 + t), factor(1, t), ALU.mult).then_inc(sem("vtok_ready"), 1)
        for t in range(NT):
            dve.wait_ge(sem("gram_done"), t + 1)
            dve.tensor_tensor(four3(nT_s, t), bank3(t), factor(0, t), ALU.mult).then_inc(sem("n_ready"), 1)
        dve.wait_ge(sem("n_ready"), NT)
        dve.wait_ge(sem("masks_ready"), 1)
        link(dve.tensor_tensor(tbuf[:, :, :], nT_s[:, :, :], over_tiles(mask1[:, :], NM), ALU.mult))
        link(dve.tensor_tensor(xm[:, :, :], over_tiles(ident[:, :], NM), tbuf[:, :, :], ALU.subtract))
        dve.wait_ge(sem("nT_ready"), NT)
        link(dve.tensor_tensor(tbuf[:, :, :], nT_all[:, :, :], over_tiles(masks[:, 0, :], NM), ALU.mult))
        dve.tensor_tensor(xmT[:, :, :], over_tiles(ident[:, :], NM), tbuf[:, :, :], ALU.subtract).then_inc(sem("xm_started"), 1)
        for t in range(NT):
            dve.wait_ge(sem("qk_done"), t + 1)
            dve.tensor_tensor(four3(qk, t), bank3(t), over_tiles(incl[:, :], 4), ALU.mult).then_inc(sem("qk_ready"), 1)
        norms_out(1)
        dve.wait_ge(sem("xm_started"), 1)
        for l in range(1, len(LEVELS) - 1):
            for t in range(NT):
                n = NT * (l - 1) + t
                if l < len(LEVELS) - 2:
                    dve.wait_ge(sem("w_done"), n + 1)
                    dve.tensor_tensor(four(xm, t), four(xm, t), bank[4 + t % 2], ALU.subtract).then_inc(sem("xm_ready"), 1)
                dve.wait_ge(sem("wT_done"), n + 1)
                dve.tensor_tensor(four(xmT, t), four(xmT, t), bank[6 + t % 2], ALU.subtract).then_inc(sem("xmT_ready"), 1)
            dve.wait_ge(sem("xm_ready"), NT * min(l, len(LEVELS) - 3))
            dve.wait_ge(sem("xmT_ready"), NT * l)
        for t in range(NT):
            dve.wait_ge(sem("r1_done"), t + 1)
            dve.tensor_copy(four(rbuf, t), bank[t]).then_inc(sem("r1_ready"), 1)
        dve.wait_ge(sem("r1_ready"), NT)
        for t in range(NT):
            dve.wait_ge(sem("r2_done"), t + 1)
            dve.tensor_tensor(four(rbuf, t), four(rbuf, t), bank[t], ALU.subtract).then_inc(sem("u_ready"), 1)
        dve.wait_ge(sem("norms_ready"), 2)
        link(dve.tensor_tensor(scal[:, 2, :], scal[:, 2, :], norms[:, 1, :], ALU.mult))
        for t in range(NT):
            dve.wait_ge(sem("o_done"), t + 1)
            link(dve.tensor_tensor(four3(ybuf, t), bank3(4 + t), factor(2, t), ALU.mult))
            dve.wait_ge(sem("ema_turned"), t + 1)
            link(dve.tensor_tensor(four3(tbuf, t), bank3(t), factor(3, t), ALU.mult))
            link(dve.tensor_tensor(four(ybuf, t), four(ybuf, t), four(tbuf, t), ALU.add))
        for t in range(NT + 1):
            if t < NT:
                of_tile = norms[:, 0, 4 * t:4 * t + 4]
                link(dve.tensor_tensor(four(tbuf, t), four(ybuf, t), four(ybuf, t), ALU.mult))
                link(dve.tensor_reduce(of_tile, four3(tbuf, t), AX.X, ALU.add))
                dve.tensor_scalar(of_tile, of_tile, 1.0 / P, EPS, ALU.mult, ALU.add).then_inc(sem("mean_square"), 1)
            if t >= 1:
                dve.wait_ge(sem("rms_ready"), t)
                dve.tensor_tensor(four3(ybuf, t - 1), four3(ybuf, t - 1), over_width(norms[:, 0, 4 * t - 4:4 * t], P), ALU.mult)\
                   .then_inc(sem("mixed_ready"), 1)
        for c in (0, 1):
            dve.wait_ge(sem("turned"), 5)
            dve.tensor_scalar(kf[:, c, :], bank[c], rmsw[:, 0:1], None, ALU.mult).then_inc(sem("turned_copied"), 1)
        for t in range(NT):
            dve.wait_ge(sem("wo_done"), t + 1)
            link(dve.tensor_tensor(xa[:, t, :], xa[:, t, :], bank[4 + t], ALU.add))
            norm_stats(dve, link, xa, t)
            norm_apply(dve, 5, n2, xa, t).then_inc(sem("n2_ready"), 1)

    def act_delta(act):
        copy_turned(act, act.copy, 3, (2, 3), xT)
        for i, g in enumerate((beta, gamma)):
            act.wait_ge(sem("gates_done"), i + 1)
            act.activation(g[:, :], bank[4 + i][0:GH, :], ACT.Tanh, scale=0.5).then_inc(sem("gate_tanh"), 1)
        act.wait_ge(sem("mix_conv"), 1)
        act.activation(trow[:, :], mixr[:, :], ACT.Tanh, scale=0.5).then_inc(sem("mix_tanh"), 1)
        act.wait_ge(sem("mix_silu"), 1)
        act.wait_ge(sem("hbias_ready"), 1)
        act.activation(trow[:, :], mixr[:, :], ACT.Tanh, scale=0.25, bias=hbias[:, :]).then_inc(sem("mix_tanh"), 1)

        def src(n):
            return feats[n // NC][:, n % NC, :]

        act.wait_ge(sem("delta_small_loaded"), 16 * 9)
        for n in range(NPROJ + 2):
            if n < NPROJ:
                act.wait_ge(sem("proj_done"), n + 1)
                act.activation(src(n), bank[n % 4], ACT.Copy, scale=conv[:, n // NC, n % NC, TAPS - 1:TAPS])\
                   .then_inc(sem("first_tap"), 1)
            if 1 <= n <= NPROJ:
                act.wait_ge(sem("conv_done"), n)
                act.activation(th[:, n - 1, :], src(n - 1), ACT.Tanh, scale=0.5).then_inc(sem("tanh_first"), 1)
            if 2 <= n < 2 * NC + 2:
                act.wait_ge(sem("silu_first"), n - 1)
                act.activation(th[:, n - 2, :], src(n - 2), ACT.Tanh, scale=0.25).then_inc(sem("tanh_second"), 1)
        for h in range(GH):
            act.wait_ge(sem("gamma_spread"), h + 1)
            act.wait_ge(sem("gamma_used_v"), h + 1)
            act.copy(four(tbuf, h), bank[h]).then_inc(sem("gamma_used_a"), 1)
        for t in range(NT):
            act.wait_ge(sem("transposed_n"), t + 1)
            act.copy(four(nT_all, t), bank[4 + t]).then_inc(sem("nT_ready"), 1)
        for l in range(1, len(LEVELS) - 1):
            for t in range(NT):
                act.wait_ge(sem("y_done"), NT * (l - 1) + t + 1)
                act.copy(four(ybuf, t), bank[t]).then_inc(sem("y_ready"), 1)
        for t in range(NT):
            act.wait_ge(sem("c_done"), t + 1)
            act.copy(four(ybuf, t), bank[4 + t]).then_inc(sem("c_ready"), 1)
        for c in (2, 3):
            act.wait_ge(sem("turned"), 5)
            act.activation(kf[:, c, :], bank[c], ACT.Copy, scale=rmsw[:, 0:1]).then_inc(sem("turned_copied"), 1)

    def pe_delta(pe):
        pe_turn(pe, tmp, "n1_ready")
        pe.wait_ge(sem("turned_copied"), 16)
        pe.wait_ge(sem("delta_small_loaded"), 16 * 9)
        for i in range(3):
            for c in range(NC):
                k = pe.matmul(bank[4 + i][0:GH, :], wgates[:, c, GH * i:GH * (i + 1)], xT[:, c, :], start=c == 0, stop=c == NC - 1)
            k.then_inc(sem("gates_done"), 1)
        pe.wait_ge(sem("dw_loaded"), 64)
        for n in range(NPROJ):
            if n >= 4:
                pe.wait_ge(sem("conv_done"), n - 3)
            for c in range(NC):
                k = pe.matmul(bank[n % 4], dw[n // NC][:, c, (n % NC) * P:(n % NC + 1) * P], xT[:, c, :],
                              start=c == 0, stop=c == NC - 1)
            k.then_inc(sem("proj_done"), 1)
        pe.wait_ge(sem("gates_ready"), 3)
        pe.wait_ge(sem("masks_ready"), 1)
        pe.wait_ge(sem("conv_done"), NPROJ)

        def sum_squares(i):
            pe.wait_ge(sem("squares_ready"), i + 1)
            for m in range(NM):
                k = pe.matmul(bank[6][:, i * NM + m:i * NM + m + 1],
                              squares[i][:, m % GH, (m // GH) * P:(m // GH + 1) * P], ones[:, 0:1], start=True, stop=True)
            k.then_inc(sem("norms_done"), 1)

        sum_squares(0)
        for h in range(GH):
            pe.matmul(bank[h], sel[:, h, :], gamma[:, :], start=True, stop=True).then_inc(sem("gamma_spread"), 1)
        for i, g in enumerate((beta, mixr)):
            for t in range(NT):
                k = pe.transpose(bank[7][:, (i * NT + t) * GH:(i * NT + t + 1) * GH], g[:, t * P:(t + 1) * P],
                                 ident[0:GH, 0:GH])
        k.then_inc(sem("gates_turned"), 1)

        def tile(f, m):
            return f[:, m % GH, (m // GH) * P:(m // GH + 1) * P]

        def each(b0, t, lhs, rhs, done):
            for m in range(4 * t, 4 * t + 4):
                k = pe.matmul(bank[b0][:, level_matrix(m)], lhs(m), rhs(m), start=True, stop=True)
            k.then_inc(sem(done), 1)

        def turn(b0, t, src, done):
            for m in range(4 * t, 4 * t + 4):
                k = pe.transpose(bank[b0][:, level_matrix(m)], src(m), ident[:, :])
            k.then_inc(sem(done), 1)

        pe.wait_ge(sem("feature_ready"), 2 * NC)
        pe.wait_ge(sem("values_ready"), NC)
        pe.wait_ge(sem("gtok_ready"), 1)
        pe.wait_ge(sem("norms_summed"), 1)
        for t in range(NT):
            turn(4 + t, t, lambda m: tile(vf, m), "v_turned")
        for t in range(NT):
            pe.wait_ge(sem("gamma_used_a"), NT)
            each(t, t, lambda m: tile(kf, m), lambda m: tile(kf, m), "gram_done")
        for t in range(NT):
            pe.wait_ge(sem("vtok_ready"), t + 1)
            pe.wait_ge(sem("n_ready"), t + 1)
            turn(4 + t, t, lambda m: nT_s[:, m, :], "transposed_n")
        for t in range(NT):
            each(t, t, lambda m: tile(kf, m), lambda m: tile(qf, m), "qk_done")
        for t in range(NT):
            pe.wait_ge(sem("nT_ready"), t + 1)
        sum_squares(1)
        pe.wait_ge(sem("xm_started"), 1)
        for l in range(1, len(LEVELS) - 1):
            for t in range(NT):
                if l == 1:
                    pe.wait_ge(sem("qk_ready"), t + 1)
                pe.wait_ge(sem("level_ready"), NT * (l - 1) + t + 1)
                if l > 1:
                    pe.wait_ge(sem("xm_ready"), NT * (l - 2) + t + 1)
                each(t, t, lambda m: nT_s[:, m, :], lambda m: xm[:, m, :], "y_done")
            for t in range(NT):
                pe.wait_ge(sem("y_ready"), NT * (l - 1) + t + 1)
                n = NT * (l - 1) + t
                if n >= 2:
                    pe.wait_ge(sem("xmT_ready"), n - 1)
                elif n == 0:
                    pe.wait_ge(sem("norms_summed"), 2)
                if l < len(LEVELS) - 2:
                    each(4 + t % 2, t, lambda m: xmT[:, m, :], lambda m: ybuf[:, m, :], "w_done")
                each(6 + t % 2, t, lambda m: ybuf[:, m, :], lambda m: xmT[:, m, :], "wT_done")
        for t in range(NT):
            pe.wait_ge(sem("xmT_ready"), NT * (len(LEVELS) - 3) + t + 1)
            each(t, t, lambda m: xmT[:, m, :], lambda m: vtok[:, m, :], "r1_done")
        for t in range(NT):
            pe.wait_ge(sem("r1_ready"), t + 1)
            pe.wait_ge(sem("level_ready"), NT * (len(LEVELS) - 2) + t + 1)
            if t == 0:
                pe.wait_ge(sem("xmT_ready"), NT * (len(LEVELS) - 2))
            each(4 + t, t, lambda m: nT_s[:, m, :], lambda m: rbuf[:, m, :], "c_done")
        for t in range(NT):
            pe.wait_ge(sem("c_ready"), t + 1)
            each(t, t, lambda m: xmT[:, m, :], lambda m: ybuf[:, m, :], "r2_done")
        for t in range(NT):
            pe.wait_ge(sem("u_ready"), t + 1)
            each(4 + t, t, lambda m: qk[:, m, :], lambda m: rbuf[:, m, :], "o_done")
        for t in range(NT):
            if t == 0:
                pe.wait_ge(sem("ema_ready"), GH)
            turn(t, t, lambda m: tile(ema, m), "ema_turned")
        for t in range(NT):
            pe.wait_ge(sem("mixed_ready"), t + 1)
            for c in range(NC):
                k = pe.transpose(bank[c][:, t * P:(t + 1) * P], ybuf[:, 4 * t + c, :], ident[:, :])
        k.then_inc(sem("turned"), 1)
        pe.wait_ge(sem("turned_copied"), 20)
        for t in range(NT):
            for c in range(NC):
                k = pe.matmul(bank[4 + t], kf[:, c, t * P:(t + 1) * P], dwo[:, c, :], start=c == 0, stop=c == NC - 1)
            k.then_inc(sem("wo_done"), 1)

    NS = 8
    NPIECE = 6
    HH = HID // 2
    NG2 = NH // 2
    PERIOD = 4
    place = [16384, 32768, 49152, 65536, 114688, 131072, 98304, 81920]
    w12 = [at(f"w12_{k}", R + place[k], [P, NC, HH]) for k in range(NS)]
    w3 = [at(f"w3_{k}", R + place[k], [P, NH // 2, D]) for k in range(NS)]
    n2T = at("n2T", R, [P, NC, TOK])
    wslots = at("wslots", R, [P, NT * NEXP, CAP])
    eout = at("eout", R + 10240, [P, D])
    yT = at("yT", R, [P, NC, TOK])
    n2 = at("n2", R + 147456, [P, NT, D])
    eth = at("eth", R + 147456, [P, 3, 2 * CAP])
    slots = at("slots", R + 155648, [P, NT * NEXP, CAP])
    scat = at("scat", R + 165888, [P, NEXP, TOK])
    disp = at("disp", R + 182272, [P, NC, NEXP * CAP])
    hT = at("hT", R + 192512, [P, NH, CAP])
    M0 = R + 197632
    upper = at("upper", M0, [P, P])
    iotac = at("iotac", M0 + 512, [P, CAP])
    iotae = at("iotae", M0 + 832, [P, NEXP])
    logit = at("logit", M0 + 864, [P, NT, NEXP])
    top = at("top", M0 + 992, [P, NT, 8])
    topi = at("topi", M0 + 1120, [P, NT, 8], U32)
    topf = at("topf", M0 + 1248, [P, NT, 8])
    first = at("first", M0 + 1376, [P, NT, NEXP])
    second = at("second", M0 + 1504, [P, NT, NEXP])
    chosen = at("chosen", M0 + 1632, [P, NT, NEXP])
    weight = at("weight", M0 + 1760, [P, NT, NEXP])
    pos = at("pos", M0 + 1888, [P, NT, NEXP])
    rw = at("rw", M0 + 2016, [P, 2, NT])
    wg = at("wg", 1728, [P, NC, NEXP])
    bg = at("bg", 1856, [P, NEXP])

    def sp_experts(sp):
        freed = {4: ("r1_done", NT), 5: ("o_done", NT), 6: ("ema_turned", NT), 7: ("wo_done", NT)}
        for n in range(NPIECE * NEXP):
            e, j, k = n // NPIECE, n % NPIECE, n % NS
            if n == 0:
                sp.wait_ge(sem("ffn_done"), NT)
            elif n in freed:
                sp.wait_ge(sem(freed[n][0]), freed[n][1])
            elif n >= NS:
                sp.wait_ge(sem("pieces_used"), n - NS + 1)
            if j < 4:
                src = a["ew1" if j % 2 == 0 else "ew2"][e, :, (j // 2) * HH:(j // 2 + 1) * HH]
                sp.dma_start(w12[k][:, :, :], src.rearrange("(c p) n -> p c n", p=P)).then_inc(sem(f"piece_loaded{k}"), 16)
            else:
                src = a["ew3"][e, (j - 4) * HH:(j - 3) * HH, :]
                sp.dma_start(w3[k][:, :, :], src.rearrange("(c p) n -> p c n", p=P)).then_inc(sem(f"piece_loaded{k}"), 16)

    def pool_experts(pool, link):
        pool.wait_ge(sem("turned"), 5)
        link(pool.memset(upper[:, :], 1.0))
        link(pool.affine_select(out=upper[:, :], in_=upper[:, :], compare_op=ALU.is_ge, fill=0.0, base=0,
                                pattern=[[1, P]], channel_multiplier=-1))
        link(pool.iota(topi[:, :, :].rearrange("p t k -> p (t k)")[:, 0:NEXP], pattern=[[1, NEXP]], base=0, channel_multiplier=0))
        link(pool.tensor_copy(iotae[:, :], topi[:, :, :].rearrange("p t k -> p (t k)")[:, 0:NEXP]))
        link(pool.iota(hT[:, 0, :].bitcast(U32), pattern=[[1, CAP]], base=0, channel_multiplier=0))
        pool.tensor_copy(iotac[:, :], hT[:, 0, :].bitcast(U32)).then_inc(sem("iotas_ready"), 1)
        for t in range(NT):
            norm_rstd(pool, link, 5, t)
        pool.memset(scat[:, :, :], 0.0).then_inc(sem("scat_zeroed"), 1)
        pool.wait_ge(sem("scat_turned"), NEXP)
        pool.memset(eout[:, :], 0.0).then_inc(sem("zeros_ready"), 1)

    def dve_experts(dve, link):
        copy_turned(dve, dve.tensor_copy, 5, (0, 1), n2T)
        dve.wait_ge(sem("delta_small_loaded"), 16 * 9)
        dve.wait_ge(sem("router_product"), 1)
        link(dve.tensor_tensor(logit[:, :, :], bank[4][:, 0:NT * NEXP].rearrange("p (t e) -> p t e", t=NT),
                               over_tiles(bg[:, :]), ALU.add))
        dve.wait_ge(sem("iotas_ready"), 1)
        for t in range(NT):
            link(dve.max(top[:, t, :], logit[:, t, :]))
            link(dve.max_index(topi[:, t, :], top[:, t, :], logit[:, t, :]))
        dve.tensor_tensor(rw[:, 1, :], top[:, :, 1], top[:, :, 0], ALU.subtract).then_inc(sem("margin_ready"), 1)
        link(dve.tensor_copy(topf[:, :, :], topi[:, :, :]))
        link(dve.tensor_tensor(first[:, :, :], over_tiles(iotae[:, :]), over_width(topf[:, :, 0], NEXP), ALU.is_equal))
        link(dve.tensor_tensor(second[:, :, :], over_tiles(iotae[:, :]), over_width(topf[:, :, 1], NEXP), ALU.is_equal))
        dve.tensor_tensor(chosen[:, :, :], first[:, :, :], second[:, :, :], ALU.add).then_inc(sem("chosen_ready"), 1)
        dve.wait_ge(sem("margin_exp"), 1)
        link(dve.tensor_scalar(rw[:, 0, :], rw[:, 1, :], 1.0, None, ALU.add))
        link(dve.reciprocal(rw[:, 0, :], rw[:, 0, :]))
        link(dve.tensor_tensor(rw[:, 1, :], rw[:, 1, :], rw[:, 0, :], ALU.mult))
        link(dve.tensor_tensor(first[:, :, :], first[:, :, :], over_width(rw[:, 0, :], NEXP), ALU.mult))
        link(dve.tensor_tensor(second[:, :, :], second[:, :, :], over_width(rw[:, 1, :], NEXP), ALU.mult))
        link(dve.tensor_tensor(weight[:, :, :], first[:, :, :], second[:, :, :], ALU.add))
        link(dve.tensor_scalar(weight[:, :, :], weight[:, :, :], 0.5, None, ALU.mult))
        dve.wait_ge(sem("router_product"), 2)
        link(dve.tensor_tensor(pos[:, :, :].rearrange("p t e -> p (t e)"), bank[5][:, 0:NT * NEXP],
                               chosen[:, :, :].rearrange("p t e -> p (t e)"), ALU.mult))
        link(dve.tensor_scalar(pos[:, :, :], pos[:, :, :], -1.0, None, ALU.add))
        dve.tensor_tensor(slots[:, :, :], over_tiles(iotac[:, :], NT * NEXP),
                          over_width(pos[:, :, :].rearrange("p t e -> p (t e)"), CAP), ALU.is_equal).then_inc(sem("slots_ready"), 1)
        dve.wait_ge(sem("slots_ready"), 1)
        dve.tensor_tensor(wslots[:, :, :], slots[:, :, :], over_width(weight[:, :, :].rearrange("p t e -> p (t e)"), CAP),
                          ALU.mult).then_inc(sem("wslots_ready"), 1)
        half = NEXP * CAP // 2
        for c in range(NC):
            dve.wait_ge(sem("gathered"), c + 1)
            dve.tensor_copy(disp[:, c, 0:half], bank[c][:, 0:half]).then_inc(sem("disp_ready_v"), 1)
        dve.wait_ge(sem("scat_zeroed"), 1)
        for e in range(0, NEXP, 2):
            dve.wait_ge(sem("scat_turned"), e + 1)
            dve.tensor_copy(scat[0:CAP, e, :], bank[e][0:CAP, :]).then_inc(sem("scat_ready_v"), 1)
        dve.wait_ge(sem("zeros_ready"), 1)
        dve.memset(stat[:, :, :], 0.0).then_inc(sem("hidden_ready"), NG2)

    def pe_experts(pe):
        pe_turn(pe, n2, "n2_ready")
        pe.wait_ge(sem("turned_copied"), 24)
        for t in range(NT):
            for c in range(NC):
                k = pe.matmul(bank[4][:, t * NEXP:(t + 1) * NEXP], n2T[:, c, t * P:(t + 1) * P], wg[:, c, :],
                              start=c == 0, stop=c == NC - 1)
        k.then_inc(sem("router_product"), 1)
        pe.wait_ge(sem("chosen_ready"), 1)
        for t in range(NT):
            for s in range(t + 1):
                k = pe.matmul(bank[5][:, t * NEXP:(t + 1) * NEXP], upper[:, :] if s == t else ones[:, :], chosen[:, s, :],
                              start=s == 0, stop=s == t)
        k.then_inc(sem("router_product"), 1)
        pe.wait_ge(sem("slots_ready"), 1)
        half = NEXP // 2
        for c in range(NC):
            for h in range(2):
                for t in range(NT):
                    k = pe.matmul(bank[c + 4 * h][:, 0:half * CAP], n2[:, t, c * P:(c + 1) * P],
                                  slots[:, t * NEXP + h * half:t * NEXP + (h + 1) * half, :].rearrange("p e s -> p (e s)"),
                                  start=t == 0, stop=t == NT - 1)
            k.then_inc(sem("gathered"), 1)
        pe.wait_ge(sem("wslots_ready"), 1)
        for e in range(NEXP):
            pe.wait_ge(sem("disp_ready_v" if e < 4 else "disp_ready_a"), e % 4 + 1)
            for t in range(NT):
                k = pe.transpose(bank[e][0:CAP, t * P:(t + 1) * P], wslots[:, t * NEXP + e, :], ident[:, :])
            k.then_inc(sem("scat_turned"), 1)
        pe.wait_ge(sem("scat_ready_v"), NEXP // 2)
        pe.wait_ge(sem("scat_ready_a"), NEXP // 2)
        pe.wait_ge(sem("disp_ready_v"), NC)
        pe.wait_ge(sem("disp_ready_a"), NC)
        for c in range(NC):
            for t in range(NT):
                pe.matmul(bank[c][:, t * P:(t + 1) * P], xa[:, t, c * P:(c + 1) * P], ident[:, :], start=t == 0, stop=False,
                          skip_group_check=True)

        def hidden(e0, i, g):
            e = e0 + PERIOD * i
            pe.wait_ge(sem("hidden_ready"), NG2 * e + g + (7 if g < 2 else 6))
            half = g // (NG2 // 2)
            places = [(NPIECE * e0 + 2 * half + w) % NS for w in (0, 1)]
            if g % (NG2 // 2) == 0:
                for w in (0, 1):
                    pe.wait_ge(sem(f"piece_loaded{places[w]}"), 16 * (3 * i + (NPIECE * e0 + 2 * half + w) // NS + 1))
            for w in (0, 1):
                for m in (0, 1):
                    f = ((2 * g + m) * P) % HH
                    for c in range(NC):
                        k = pe.matmul(bank[4 + g % 3][:, (2 * w + m) * CAP:(2 * w + m + 1) * CAP], w12[places[w]][:, c, f:f + P],
                                      disp[:, c, bass.ds(e * CAP, CAP)], start=c == 0, stop=c == NC - 1)
            k.then_inc(sem("hidden_done"), 1)

        def down(e0, i):
            e = e0 + PERIOD * i
            pe.wait_ge(sem("eout_ready"), e + 1)
            for f in range(NH):
                if f % 2 == 0:
                    pe.wait_ge(sem("hidden_ready"), NG2 * (e + 1) + f // 2 + 1)
                n = NPIECE * e0 + 4 + f // (NH // 2)
                if f % (NH // 2) == 0:
                    pe.wait_ge(sem(f"piece_loaded{n % NS}"), 16 * (3 * i + n // NS + 1))
                k = pe.matmul(bank[7][0:CAP, :], hT[:, f, :], w3[n % NS][:, f % (NH // 2), :], start=f == 0, stop=f == NH - 1)
                if f == NH // 2 - 1:
                    k.then_inc(sem("pieces_used"), 5)
                if f == NH - 1:
                    k.then_inc(sem("down_done"), 1)

        def scatter(e0, i):
            e = e0 + PERIOD * i
            pe.wait_ge(sem("eout_ready"), e + 2)
            for c in range(NC):
                k = pe.matmul(bank[c], eout[:, c * P:(c + 1) * P], scat[:, bass.ds(e, 1), :].rearrange("p e t -> p (e t)"),
                              start=False, stop=False, skip_group_check=True)
            k.then_inc(sem("pieces_used"), 1)

        with pe.Fori(0, NEXP // PERIOD) as i:
            for e0 in range(PERIOD):
                for g in range(NG2):
                    hidden(e0, i, g)
                    if g == 0 and e0 > 0:
                        scatter(e0 - 1, i)
                down(e0, i)
            scatter(PERIOD - 1, i)
        pe.wait_ge(sem("yT_ready"), 4)
        for t in range(NT):
            for c in range(NC):
                k = pe.transpose(bank[4 + t % 4][:, c * P:(c + 1) * P], yT[:, c, t * P:(t + 1) * P], ident[:, :])
            k.then_inc(sem("y_turned"), 1)

    def act_experts(act):
        copy_turned(act, act.copy, 5, (2, 3), n2T)
        act.wait_ge(sem("margin_ready"), 1)
        act.activation(rw[:, 1, :], rw[:, 1, :], ACT.Exp).then_inc(sem("margin_exp"), 1)
        half = NEXP * CAP // 2
        for c in range(NC):
            act.wait_ge(sem("gathered"), c + 1)
            act.copy(disp[:, c, half:2 * half], bank[4 + c][:, 0:half]).then_inc(sem("disp_ready_a"), 1)
        act.wait_ge(sem("scat_zeroed"), 1)
        for e in range(1, NEXP, 2):
            act.wait_ge(sem("scat_turned"), e + 1)
            act.copy(scat[0:CAP, e, :], bank[e][0:CAP, :]).then_inc(sem("scat_ready_a"), 1)
        act.wait_ge(sem("zeros_ready"), 1)
        act.copy(rstd[:, :], rstd[:, :]).then_inc(sem("eout_ready"), 1)
        with act.Fori(0, NEXP // PERIOD) as i:
            for e0 in range(PERIOD):
                e = e0 + PERIOD * i
                for g in range(NG2):
                    act.wait_ge(sem("hidden_done"), NG2 * e + g + 1)
                    act.activation(eth[:, g % 3, :], bank[4 + g % 3][:, 0:2 * CAP], ACT.Tanh, scale=0.5)\
                       .then_inc(sem("hidden_tanh"), 1)
                act.wait_ge(sem("down_done"), e + 1)
                act.copy(eout[0:CAP, :], bank[7][0:CAP, :]).then_inc(sem("eout_ready"), 1)
        act.wait_ge(sem("pieces_used"), NPIECE * NEXP)
        for c in (2, 3):
            act.copy(yT[:, c, :], bank[c]).then_inc(sem("yT_ready"), 1)

    def dve_experts_loop(dve):
        with dve.Fori(0, NEXP // PERIOD) as i:
            for e0 in range(PERIOD):
                e = e0 + PERIOD * i
                for g in range(NG2):
                    n = NG2 * e + g
                    dve.wait_ge(sem("hidden_tanh"), n + 1)
                    dve.scalar_tensor_tensor(eth[:, g % 3, :], eth[:, g % 3, :], 1.0, bank[4 + g % 3][:, 0:2 * CAP],
                                             ALU.add, ALU.mult).then_inc(sem("gate_ready"), 1)
                    dve.wait_ge(sem("gate_ready"), n + 1)
                    dve.tensor_tensor(hT[:, 2 * g:2 * g + 2, :].rearrange("p f s -> p (f s)"), eth[:, g % 3, :],
                                      bank[4 + g % 3][:, 2 * CAP:4 * CAP], ALU.mult).then_inc(sem("hidden_ready"), 1)
        dve.wait_ge(sem("pieces_used"), NPIECE * NEXP)
        for c in (0, 1):
            dve.tensor_copy(yT[:, c, :], bank[c]).then_inc(sem("yT_ready"), 1)
        for t in range(NT):
            dve.wait_ge(sem("y_turned"), t + 1)
            dve.tensor_copy(xa[:, t, :], bank[4 + t % 4]).then_inc(sem("result_ready"), 1)

    @block.sync
    def _(sp):
        sp_self(sp)
        batches(sp, sp_cross)
        sp_ffn(sp)
        sp_delta(sp)
        sp_experts(sp)
        for t in range(NT):
            sp.wait_ge(sem("result_ready"), t + 1)
            sp.dma_start(out_dram[:, t, :], xa[:, t, :]).then_inc(sem("out_written"), 16)
        sp.wait_ge(sem("out_written"), 16 * NT)

    @block.gpsimd
    def _(pool):
        link = Chain(pool, "pool_chain")
        pool_self(pool, link)
        pool.wait_ge(sem("o1_done"), B)
        pool.memset(qb_h[:, :, :].bitcast(U32), 0)
        pool.memset(qb_l[:, :, :].bitcast(U32), 0).then_inc(sem("queries_zeroed"), 1)
        for t in range(NT):
            norm_rstd(pool, link, 2, t)
        pool_masks(pool, link)
        pool_delta(pool, link)
        pool_experts(pool, link)

    @block.vector
    def _(dve):
        link = Chain(dve, "dve_chain")
        dve_self(dve, link)
        batches(dve, dve_cross, last=True, link=link)
        dve_ffn(dve, link)
        dve_delta(dve, link)
        dve_experts(dve, link)
        dve_experts_loop(dve)

    @block.scalar
    def _(act):
        act_self(act)
        batches(act, act_cross, last=True)
        act_ffn(act)
        act_delta(act)
        act_experts(act)

    @block.tensor
    def _(pe):
        pe_self(pe)
        batches(pe, pe_cross)
        pe_ffn(pe)
        pe_delta(pe)
        pe_experts(pe)


def kernel(**inputs):
    from concourse.bacc import Bacc
    from concourse.bass_utils import run_bass_kernel_spmd

    def get(name):
        return np.asarray(inputs[name])

    arrays = {"x": get("x"), "ctxT": get("ctx_1024").transpose(0, 2, 1)}
    for name in ("Wq1", "Wk1", "Wv1", "Wq2", "Wk2", "Wv2"):
        arrays[name.lower()] = get("L0_xattn_" + name).transpose(1, 0, 2).reshape(D, D)
    for name in ("bv1", "bv2", "g1", "be1", "g2", "be2", "g3", "be3", "bf2"):
        arrays[name] = get("L0_xattn_" + name).reshape(-1)
    for name in ("Wf1", "Wf2"):
        arrays[name.lower()] = get("L0_xattn_" + name)
    arrays["bf1"] = get("L0_xattn_bf1").reshape(NH, P).T
    for name in ("Wq", "Wk", "Wv", "Wo"):
        arrays["d" + name.lower()] = get("L0_attn_" + name)
    for name in ("conv_q", "conv_k", "conv_v"):
        arrays[name] = get("L0_attn_" + name).reshape(NC, P, TAPS).transpose(1, 0, 2)
    arrays["wgates"] = np.concatenate([get("L0_attn_" + n) for n in ("Wb", "Wdec", "Wmix")], axis=1)
    arrays["conv_mix"] = get("L0_attn_conv_mix")
    arrays["mix_bias"] = get("L0_attn_mix_bias").reshape(GH, 1)
    arrays["rms_w"] = get("L0_attn_rms_w").reshape(P, 1)
    arrays["wg"] = get("L0_ffn_Wg")
    arrays["bg"] = get("L0_ffn_bg")
    for name in ("W1", "W2", "W3"):
        arrays["e" + name.lower()] = get("L0_ffn_" + name)
    arrays = {f"in_{k}": np.ascontiguousarray(v) for k, v in arrays.items()}

    nc = Bacc("TRN2", target_bir_lowering=False, num_devices=1)
    a = {k[3:]: nc.dram_tensor(k, v.shape, F32, kind="ExternalInput").ap() for k, v in arrays.items()}
    out = nc.dram_tensor("out", (B, S, D), F32, kind="ExternalOutput").ap()
    build(nc, a, out)
    result = run_bass_kernel_spmd(nc, [arrays], core_ids=[0])
    return result.results[0]["out"]
```
